# Optimizing a Trainium2 kernel written in Bass

```python
import numpy as np
import jax
import jax.numpy as jnp

def _softmax(x, axis=-1):
    return jax.nn.softmax(x, axis=axis)

def _gelu(x):
    return jax.nn.gelu(x, approximate=True)

def _silu(x):
    return jax.nn.silu(x)

def _sigmoid(x):
    return jax.nn.sigmoid(x)

def _layernorm(x, axis=-1, eps=1e-05):
    m = jnp.mean(x, axis=axis, keepdims=True)
    v = jnp.var(x, axis=axis, keepdims=True)
    return (x - m) / jnp.sqrt(v + eps)

def _scatter_add(tgt, idx, src, axis=0):
    return tgt.at[idx].add(src)

def _segment_sum(src, seg, n):
    return jax.ops.segment_sum(src, seg, n)
kernel_name = 'mk_xattn_ffn_d2_seqx_r8_0e0805'

def setup_inputs(seed: int=0):
    np.random.seed(seed)
    _w = jnp.asarray

    def _rec_inputs():
        import jax
        import jax.numpy as jnp
        _rk = jax.random.key(seed)
        x = -0.0002928 + 1 * jax.random.normal(jax.random.fold_in(_rk, 1), (64, 64, 128), jnp.float32)
        _lenS = 64 - jax.random.randint(jax.random.fold_in(_rk, 7), (64,), 0, max(1, 64 // 4) + 1, jnp.int32)
        _lenS2 = 64 - jax.random.randint(jax.random.fold_in(_rk, 8), (64,), 0, max(1, 64 // 4) + 1, jnp.int32)
        _ctx_1024P = jax.random.normal(jax.random.fold_in(_rk, 11), (64, 16, 128), jnp.float32)
        _ctx_1024c = jax.random.dirichlet(jax.random.fold_in(_rk, 511), 0.3 * jnp.ones((16,), jnp.float32), (64, 64))
        _ctx_1024t = jnp.einsum('bsk,bkd->bsd', _ctx_1024c, _ctx_1024P)
        _ctx_1024t = _ctx_1024t * jax.lax.rsqrt(jnp.mean(jnp.square(_ctx_1024t)) + 1e-12) * 0.953939
        ctx_1024 = -1.39393e-06 + 0.999914 * (_ctx_1024t + 0.3 * jax.random.normal(jax.random.fold_in(_rk, 611), (64, 64, 128), jnp.float32))
        return (x, ctx_1024)
    x, ctx_1024 = _rec_inputs()

    def _L0_xattn_setup():
        import jax, jax.numpy as jnp
        import numpy as np
        import math
        CHANNELS = 64
        N_HEADS = 8
        K_CH = CHANNELS // N_HEADS
        ROPE_D = int(K_CH * 0.5)
        BASE = 1250

        def _rope(x):
            d = ROPE_D
            t = x.shape[2]
            theta = 1.0 / BASE ** (jnp.arange(0, d, 2, dtype=jnp.float32) / d)
            ang = jnp.arange(t, dtype=jnp.float32)[:, None] * theta[None, :]
            ang = jnp.concatenate([ang, ang], axis=-1)
            cos = jnp.cos(ang)[None, None, :, :].astype(x.dtype)
            sin = jnp.sin(ang)[None, None, :, :].astype(x.dtype)
            x_rope, x_pass = (x[..., :d], x[..., d:])
            neg_half = jnp.concatenate([-x_rope[..., d // 2:], x_rope[..., :d // 2]], axis=-1)
            return jnp.concatenate([x_rope * cos + neg_half * sin, x_pass], axis=-1)

        def _split_heads(y):
            b, _, t = y.shape
            return y.reshape(b, N_HEADS, K_CH, t).transpose(0, 1, 3, 2)
        key = jax.random.key(seed)
        ks = jax.random.split(key, 10)
        B, T = (8, 128)
        w_scale = 1.0 / math.sqrt(CHANNELS)
        return {'x': jax.random.normal(ks[0], (B, CHANNELS, T), jnp.float32), 'c': jax.random.normal(ks[1], (B, CHANNELS, T), jnp.float32), 'Wq': jax.random.normal(ks[2], (CHANNELS, CHANNELS), jnp.float32) * w_scale, 'bq': jax.random.normal(ks[3], (CHANNELS,), jnp.float32) * 0.02, 'Wk': jax.random.normal(ks[4], (CHANNELS, CHANNELS), jnp.float32) * w_scale, 'bk': jax.random.normal(ks[5], (CHANNELS,), jnp.float32) * 0.02, 'Wv': jax.random.normal(ks[6], (CHANNELS, CHANNELS), jnp.float32) * w_scale, 'bv': jax.random.normal(ks[7], (CHANNELS,), jnp.float32) * 0.02, 'Wo': jax.random.normal(ks[8], (CHANNELS, CHANNELS), jnp.float32) * w_scale, 'bo': jax.random.normal(ks[9], (CHANNELS,), jnp.float32) * 0.02}
    _L0_xattn_all = _L0_xattn_setup()
    _L0_xattn_in = {k: v for k, v in _L0_xattn_all.items() if k in ('Wq', 'bq', 'Wk', 'bk', 'Wv', 'bv', 'Wo', 'bo')}
    del _L0_xattn_all

    def _L0_ffn_setup():
        import jax, jax.numpy as jnp
        import numpy as np
        E, K = (8, 2)
        key = jax.random.key(seed)
        ks = jax.random.split(key, 5)
        B, S, H, I = (2, 128, 128, 512)
        scale_h = 1.0 / np.sqrt(H)
        scale_i = 1.0 / np.sqrt(I)
        return {'hidden_states': jax.random.normal(ks[0], (B, S, H), jnp.float32), 'conf_w': jax.random.normal(ks[1], (E, H), jnp.float32) * 0.1 * scale_h, 'conf_b': jnp.zeros((E,), jnp.float32), 'gate_w': jax.random.normal(ks[2], (E, I, H), jnp.float32) * scale_h, 'up_w': jax.random.normal(ks[3], (E, I, H), jnp.float32) * scale_h, 'down_w': jax.random.normal(ks[4], (E, H, I), jnp.float32) * scale_i, 'wealth': jnp.ones((E,), jnp.float32)}
    _L0_ffn_all = _L0_ffn_setup()
    _L0_ffn_in = {k: v for k, v in _L0_ffn_all.items() if k in ('conf_w', 'conf_b', 'gate_w', 'up_w', 'down_w', 'wealth')}
    del _L0_ffn_all

    def _L1_xattn_setup():
        import jax, jax.numpy as jnp
        import numpy as np
        B, S, D, H = (4, 256, 128, 16)
        DK = D // H
        key = jax.random.key(seed)
        ks = jax.random.split(key, 11)
        s = 1.0 / np.sqrt(D)
        return {'query': jax.random.normal(ks[0], (B, S, D), jnp.float32), 'key': jax.random.normal(ks[1], (B, S, D), jnp.float32), 'value': jax.random.normal(ks[2], (B, S, D), jnp.float32), 'Wq_w': jax.random.normal(ks[3], (D, D), jnp.float32) * s, 'Wq_b': jnp.zeros((D,), jnp.float32), 'Wk_w': jax.random.normal(ks[4], (D, D), jnp.float32) * s, 'Wk_b': jnp.zeros((D,), jnp.float32), 'Wv_w': jax.random.normal(ks[5], (D, D), jnp.float32) * s, 'Wv_b': jnp.zeros((D,), jnp.float32), 'Wo_w': jax.random.normal(ks[6], (D, D), jnp.float32) * s, 'Wo_b': jnp.zeros((D,), jnp.float32)}
    _L1_xattn_all = _L1_xattn_setup()
    _L1_xattn_in = {k: v for k, v in _L1_xattn_all.items() if k in ('Wq_w', 'Wq_b', 'Wk_w', 'Wk_b', 'Wv_w', 'Wv_b', 'Wo_w', 'Wo_b')}
    del _L1_xattn_all

    def _L1_ffn_setup():
        import jax, jax.numpy as jnp
        import numpy as np
        D = 128
        N_EXP = 8
        TOP_K = 1
        key = jax.random.key(seed)
        ks = jax.random.split(key, 7)
        s = 0.02
        return {'x': jax.random.normal(ks[0], (4, 256, D), jnp.float32), 'gate_w': jax.random.normal(ks[1], (D, N_EXP), jnp.float32) * s, 'gate_b': jnp.zeros((N_EXP,), jnp.float32), 'w1': jax.random.normal(ks[2], (N_EXP, D, 4 * D), jnp.float32) * s, 'b1': jnp.zeros((N_EXP, 4 * D), jnp.float32), 'w2': jax.random.normal(ks[3], (N_EXP, 4 * D, D), jnp.float32) * s, 'b2': jnp.zeros((N_EXP, D), jnp.float32)}
    _L1_ffn_all = _L1_ffn_setup()
    _L1_ffn_in = {k: v for k, v in _L1_ffn_all.items() if k in ('gate_w', 'gate_b', 'w1', 'b1', 'w2', 'b2')}
    del _L1_ffn_all
    return {'x': x, 'ctx_1024': ctx_1024, 'L0_xattn_Wq': _L0_xattn_in['Wq'], 'L0_xattn_bq': _L0_xattn_in['bq'], 'L0_xattn_Wk': _L0_xattn_in['Wk'], 'L0_xattn_bk': _L0_xattn_in['bk'], 'L0_xattn_Wv': _L0_xattn_in['Wv'], 'L0_xattn_bv': _L0_xattn_in['bv'], 'L0_xattn_Wo': _L0_xattn_in['Wo'], 'L0_xattn_bo': _L0_xattn_in['bo'], 'L0_ffn_conf_w': _L0_ffn_in['conf_w'], 'L0_ffn_conf_b': _L0_ffn_in['conf_b'], 'L0_ffn_gate_w': _L0_ffn_in['gate_w'], 'L0_ffn_up_w': _L0_ffn_in['up_w'], 'L0_ffn_down_w': _L0_ffn_in['down_w'], 'L0_ffn_wealth': _L0_ffn_in['wealth'], 'L1_xattn_Wq_w': _L1_xattn_in['Wq_w'], 'L1_xattn_Wq_b': _L1_xattn_in['Wq_b'], 'L1_xattn_Wk_w': _L1_xattn_in['Wk_w'], 'L1_xattn_Wk_b': _L1_xattn_in['Wk_b'], 'L1_xattn_Wv_w': _L1_xattn_in['Wv_w'], 'L1_xattn_Wv_b': _L1_xattn_in['Wv_b'], 'L1_xattn_Wo_w': _L1_xattn_in['Wo_w'], 'L1_xattn_Wo_b': _L1_xattn_in['Wo_b'], 'L1_ffn_gate_w': _L1_ffn_in['gate_w'], 'L1_ffn_gate_b': _L1_ffn_in['gate_b'], 'L1_ffn_w1': _L1_ffn_in['w1'], 'L1_ffn_b1': _L1_ffn_in['b1'], 'L1_ffn_w2': _L1_ffn_in['w2'], 'L1_ffn_b2': _L1_ffn_in['b2']}

def reference(x, ctx_1024, L0_xattn_Wq, L0_xattn_bq, L0_xattn_Wk, L0_xattn_bk, L0_xattn_Wv, L0_xattn_bv, L0_xattn_Wo, L0_xattn_bo, L0_ffn_conf_w, L0_ffn_conf_b, L0_ffn_gate_w, L0_ffn_up_w, L0_ffn_down_w, L0_ffn_wealth, L1_xattn_Wq_w, L1_xattn_Wq_b, L1_xattn_Wk_w, L1_xattn_Wk_b, L1_xattn_Wv_w, L1_xattn_Wv_b, L1_xattn_Wo_w, L1_xattn_Wo_b, L1_ffn_gate_w, L1_ffn_gate_b, L1_ffn_w1, L1_ffn_b1, L1_ffn_w2, L1_ffn_b2):
    import jax
    import jax.numpy as jnp

    def _L0_xattn_ref(x, c, Wq, bq, Wk, bk, Wv, bv, Wo, bo):
        import jax, jax.numpy as jnp
        import numpy as np
        import math
        CHANNELS = 64
        N_HEADS = 8
        K_CH = CHANNELS // N_HEADS
        ROPE_D = int(K_CH * 0.5)
        BASE = 1250

        def _rope(x):
            d = ROPE_D
            t = x.shape[2]
            theta = 1.0 / BASE ** (jnp.arange(0, d, 2, dtype=jnp.float32) / d)
            ang = jnp.arange(t, dtype=jnp.float32)[:, None] * theta[None, :]
            ang = jnp.concatenate([ang, ang], axis=-1)
            cos = jnp.cos(ang)[None, None, :, :].astype(x.dtype)
            sin = jnp.sin(ang)[None, None, :, :].astype(x.dtype)
            x_rope, x_pass = (x[..., :d], x[..., d:])
            neg_half = jnp.concatenate([-x_rope[..., d // 2:], x_rope[..., :d // 2]], axis=-1)
            return jnp.concatenate([x_rope * cos + neg_half * sin, x_pass], axis=-1)

        def _split_heads(y):
            b, _, t = y.shape
            return y.reshape(b, N_HEADS, K_CH, t).transpose(0, 1, 3, 2)
        q = jnp.einsum('oc,bct->bot', Wq, x) + bq[None, :, None]
        k = jnp.einsum('oc,bct->bot', Wk, c) + bk[None, :, None]
        v = jnp.einsum('oc,bct->bot', Wv, c) + bv[None, :, None]
        q = _rope(_split_heads(q))
        k = _rope(_split_heads(k))
        v = _split_heads(v)
        scale = 1.0 / math.sqrt(K_CH)
        scores = jnp.einsum('bhtc,bhsc->bhts', q, k) * scale
        p_attn = jax.nn.softmax(scores, axis=-1)
        out = jnp.einsum('bhts,bhsc->bhtc', p_attn, v)
        b, _, t, _ = out.shape
        out = out.transpose(0, 1, 3, 2).reshape(b, CHANNELS, t)
        return jnp.einsum('oc,bct->bot', Wo, out) + bo[None, :, None]

    def _L0_ffn_ref(hidden_states, conf_w, conf_b, gate_w, up_w, down_w, wealth):
        import jax, jax.numpy as jnp
        import numpy as np
        E, K = (8, 2)
        x = hidden_states
        confidences = jax.nn.sigmoid(jnp.einsum('bsh,eh->bse', x, conf_w) + conf_b)
        bids = confidences * wealth
        top_bids, selected_experts = jax.lax.top_k(bids, K)
        sorted_bids = -jnp.sort(-bids, axis=-1)
        payments = jnp.broadcast_to(sorted_bids[..., K:K + 1], top_bids.shape)
        routing_weights = jax.nn.softmax(top_bids, axis=-1)
        combine = jnp.sum(jax.nn.one_hot(selected_experts, E, dtype=x.dtype) * routing_weights[..., None], axis=2)

        def ffn(gw, uw, dw):
            g = jnp.einsum('bsh,ih->bsi', x, gw)
            u = jnp.einsum('bsh,ih->bsi', x, uw)
            return jnp.einsum('bsi,hi->bsh', jax.nn.silu(g) * u, dw)
        expert_out = jax.vmap(ffn)(gate_w, up_w, down_w)
        output = jnp.einsum('ebsh,bse->bsh', expert_out, combine)
        return output

    def _L1_xattn_ref(query, key, value, Wq_w, Wq_b, Wk_w, Wk_b, Wv_w, Wv_b, Wo_w, Wo_b):
        import jax, jax.numpy as jnp
        import numpy as np
        B, S, D, H = (4, 256, 128, 16)
        DK = D // H
        b, s, d = query.shape
        q = query @ Wq_w.T + Wq_b
        k = key @ Wk_w.T + Wk_b
        v = value @ Wv_w.T + Wv_b
        q = q.reshape(b, s, H, DK).transpose(0, 2, 1, 3)
        k = k.reshape(b, s, H, DK).transpose(0, 2, 1, 3)
        v = v.reshape(b, s, H, DK).transpose(0, 2, 1, 3)
        scores = jnp.einsum('bhqd,bhkd->bhqk', q, k) / jnp.sqrt(jnp.asarray(DK, q.dtype))
        attn = jax.nn.softmax(scores, axis=-1)
        z = jnp.einsum('bhqk,bhkd->bhqd', attn, v)
        z = z.transpose(0, 2, 1, 3).reshape(b, s, H * DK)
        return z @ Wo_w.T + Wo_b

    def _L1_ffn_ref(x, gate_w, gate_b, w1, b1, w2, b2):
        import jax, jax.numpy as jnp
        import numpy as np
        D = 128
        N_EXP = 8
        TOP_K = 1
        b, s, d = x.shape
        xf = x.reshape(-1, d)
        logits = xf @ gate_w + gate_b
        pb = jax.nn.softmax(logits, axis=-1)
        _, idx = jax.lax.top_k(pb, TOP_K)
        sel = jnp.any(idx[:, :, None] == jnp.arange(N_EXP)[None, None, :], axis=1)
        weights = pb * sel

        def expert_step(acc, params):
            w1e, b1e, w2e, b2e, wgt = params
            h = jax.nn.gelu(xf @ w1e + b1e, approximate=False)
            y = h @ w2e + b2e
            return (acc + wgt[:, None] * y, None)
        out0 = jnp.zeros_like(xf)
        out, _ = jax.lax.scan(expert_step, out0, (w1, b1, w2, b2, weights.T))
        return out.reshape(b, s, d)
    x = x + _L0_xattn_ref(_layernorm(x, axis=-1), ctx_1024, L0_xattn_Wq, L0_xattn_bq, L0_xattn_Wk, L0_xattn_bk, L0_xattn_Wv, L0_xattn_bv, L0_xattn_Wo, L0_xattn_bo)
    x = x + _L0_ffn_ref(_layernorm(x, axis=-1), L0_ffn_conf_w, L0_ffn_conf_b, L0_ffn_gate_w, L0_ffn_up_w, L0_ffn_down_w, L0_ffn_wealth)
    x = x + _L1_xattn_ref(_layernorm(x, axis=-1), ctx_1024, ctx_1024, L1_xattn_Wq_w, L1_xattn_Wq_b, L1_xattn_Wk_w, L1_xattn_Wk_b, L1_xattn_Wv_w, L1_xattn_Wv_b, L1_xattn_Wo_w, L1_xattn_Wo_b)
    x = x + _L1_ffn_ref(_layernorm(x, axis=-1), L1_ffn_gate_w, L1_ffn_gate_b, L1_ffn_w1, L1_ffn_b1, L1_ffn_w2, L1_ffn_b2)
    return x

_drawn_inputs = setup_inputs


def setup_inputs(seed=0):
    import zlib

    import numpy as np

    out = dict(_drawn_inputs(seed))
    spreads = {'L0_ffn_conf_b': (0.0, 0.1),
     'L0_ffn_wealth': (1.0, 0.2),
     'L1_xattn_Wq_b': (0.0, 0.406),
     'L1_xattn_Wk_b': (0.0, 0.8),
     'L1_xattn_Wv_b': (0.0, 0.1),
     'L1_xattn_Wo_b': (0.0, 0.1),
     'L1_ffn_gate_b': (0.0, 0.8),
     'L1_ffn_b1': (0.0, 0.8),
     'L1_ffn_b2': (0.0, 0.572)}
    factors = {'L0_xattn_bq': 7.829,
     'L0_xattn_bk': 8.0,
     'L0_xattn_bv': 3.372,
     'L0_xattn_bo': 3.307,
     'L1_ffn_gate_w': 3.733,
     'L1_ffn_w1': 7.776,
     'L1_ffn_w2': 6.989}
    for name, (base, spread) in spreads.items():
        noise = np.random.default_rng([zlib.crc32(name.encode()), seed]).standard_normal(out[name].shape)
        drawn = base * np.exp(spread * noise) if base else spread * noise
        out[name] = jnp.asarray(drawn.astype(out[name].dtype))
    for name, factor in factors.items():
        out[name] = (out[name] * factor).astype(out[name].dtype)
    return out
```

```python
from contextlib import ExitStack

import concourse.bass as bass
import numpy as np
from concourse import mybir

F32 = mybir.dt.float32
F16 = mybir.dt.float16
BF16 = mybir.dt.bfloat16
I32 = mybir.dt.int32
U32 = mybir.dt.uint32
ALU = mybir.AluOpType
ACT = mybir.ActivationFunctionType
AX_X = mybir.AxisListType.X
ds = bass.ds

P = 128
B, CH, D = 64, 64, 128
TILES = B * CH // P
EPS = 1e-5
E = 8
F = 512
FC = F // P
H0, KC = 8, 8
H1 = 16
GROUPS0 = H0 // 4
GROUPS1 = H1 // 4
ROW_MAX = 3 * KC
REGION = B * CH + P
SPARE = E * REGION
BLOCKS0 = 2 * TILES + E
BLOCKS1 = TILES + E
BUFS = 4
GAP_STEP = 3
PADS_STEP = 2
G0, U0, D0, G1, D1 = 0, E, 2 * E, 3 * E, 4 * E
W_COLUMNS = 5 * E
W_SCALE = 64.0
X_SCALE = 64.0


def counted(n):
    return not isinstance(n, int) or n > 0


def alone(engine):
    engine.nop(nofuse=True)


def steady_loop(engine, step, first, end, last):
    for i in range(first):
        step(i, i % 2)
    with engine.Fori(first // 2, end // 2) as turn:
        step(2 * turn, 0)
        step(2 * turn + 1, 1)
    for i in range(end, last):
        step(i, i % 2)


def between(i, lo, hi):
    return not isinstance(i, int) or lo <= i < hi


class Names:
    pass


def semaphore(nc, env, name):
    sem = nc.alloc_semaphore(name)
    env.phase_semaphores.append(sem)
    return sem


def tile_of(t, i):
    return t[:, ds(i, 1), :].rearrange("p a n -> p (a n)")


def attention0(nc, env, stack):
    s = Names()
    (s.norm_stat, s.norm_aggr, s.norm_eps, s.norm_rstd, s.norm_done, s.proj_done, s.rope_mul, s.rope_sum,
     s.rope_done, s.rope_hi, s.rope_lo, s.v_mm, s.v_ready, s.v_hi_done, s.v_lo_done, s.low_dve, s.low_pool, s.k_mm,
     s.qa_mm, s.k_ready, s.qa_ready, s.s_mm, s.max_done, s.m_mm, s.qb_ready, s.st_mm, s.exp_done, s.pv_mm,
     s.sums_inv, s.heads_ready, s.ht_mm, s.ht_ready, s.out_mm, s.x_ready, s.n2_stat, s.n2_aggr, s.n2_eps, s.n2_rstd,
     s.n2_done, s.xt_mm, s.xt_ready, s.logit_mm, s.logit_b, s.gate_exp, s.gate_1p, s.gate_inv, s.bids_ready,
     s.top_val, s.top_idx, s.idx_f, s.sel_ready, s.selsum_ready, s.rank_mm, s.rank_read, s.pos_mul, s.pos_ready,
     s.idx_ready, s.prev_ready, s.x_in_first, s.x_in, s.w_in, s.tabs_t, s.tabs_done, s.ones_set, s.consts_set) = \
        (semaphore(nc, env, "a0_" + n) for n in """norm_stat norm_aggr norm_eps norm_rstd norm_done proj_done rope_mul rope_sum rope_done rope_hi
        rope_lo v_mm v_ready v_hi_done v_lo_done low_dve low_pool k_mm qa_mm k_ready qa_ready s_mm max_done
        m_mm qb_ready st_mm exp_done pv_mm sums_inv heads_ready ht_mm ht_ready out_mm x_ready n2_stat
        n2_aggr n2_eps n2_rstd n2_done xt_mm xt_ready logit_mm logit_b gate_exp gate_1p gate_inv bids_ready
        top_val top_idx idx_f sel_ready selsum_ready rank_mm rank_read pos_mul pos_ready idx_ready
        prev_ready x_in_first x_in w_in tabs_t tabs_done ones_set consts_set""".split())
    s.ctx_in = [semaphore(nc, env, f"a0_ctx_in{p}") for p in range(2)]
    s.scattered = [semaphore(nc, env, f"a0_scattered{p}") for p in range(2)]

    def sb(name, shape, dt=F32):
        return stack.enter_context(nc.sbuf_tensor("t0_" + name, shape, dt))

    X = env.X
    w_qk = sb("w_qk", [P, 4, P])
    w_v = sb("w_v", [P, P])
    w_o = sb("w_o", [P, P])
    rot = sb("rot", [P, 2, 2, P])
    b_qk = sb("b_qk", [P, 4])
    rot_b = sb("rot_b", [P, 2, P])
    b_tmp = sb("b_tmp", [P, 2, P])
    b_v = sb("b_v", [P, P])
    b_o = sb("b_o", [P, 1])
    sel, k_bias = env.sel, env.k_bias_sb
    w_c = sb("w_c", [P, E])
    b_c = sb("b_c", [P, E])
    wealth = sb("wealth", [P, E])
    ctx = sb("ctx", [P, 2, P])
    stat = sb("stat", [P, 6])
    aggr = sb("aggr", [P, 2])
    rstd = sb("rstd", [P, 1])
    var_eps = sb("var_eps", [P, 1])
    var_eps2 = sb("var_eps2", [P, 1])
    xn = sb("xn", [P, 2, P])
    rm = sb("rm", [P, 2, 2, P])
    rs = sb("rs", [P, 2, P])
    rf = sb("rf", [P, 2, P])
    r_hi = sb("r_hi", [P, 2, 2, P], F16)
    r_lo = sb("r_lo", [P, 2, 2, P], F16)
    Qa = sb("Qa", [P, 2, 4, P], F16)
    Qb = sb("Qb", [P, 2, 4, P], F16)
    Kt = sb("Kt", [P, 2, 4, P], F16)
    v_f = sb("v_f", [P, P])
    V_hi = sb("V_hi", [P, 2, 2, H0, KC + 1], F16)
    V_lo = sb("V_lo", [P, 2, 2, H0, KC + 1], F16)
    M = sb("M", [P, 4, P], F16)
    PT = sb("PT", [P, 4, 4, P])
    PT_hi = PT[:].bitcast(BF16).rearrange("p j n (t two) -> p j n t two", two=2)[:, :, :, :, 1]
    PT_lo = sb("PT_lo", [P, 4, 4, P], F16)
    inv = sb("inv", [P, 2 * H0])
    heads = sb("heads", [P, P])
    hT = sb("hT", [P, P])
    stat2 = sb("stat2", [P, 6])
    aggr2 = sb("aggr2", [P, 2])
    rstd2 = sb("rstd2", [P, 1])
    xr = sb("xr", [P, 2, P])
    xT = sb("xT", [P, P])
    lb = sb("lb", [P, E])
    le = sb("le", [P, E])
    l1 = sb("l1", [P, E])
    li = sb("li", [P, E])
    bids = sb("bids", [P, E])
    top = sb("top", [P, E])
    topi = sb("topi", [P, E], U32)
    topf = sb("topf", [P, 2])
    selsum = sb("selsum", [P, E], F16)
    base = sb("base", [P, E])
    pm = sb("pm", [P, 2, E])
    idx = sb("idx", [P, 2, 2], I32)

    work, q_bank, kv_bank = env.bank[0], env.bank[1], env.bank[2]
    s_bank, route_bank, st_bank, pv_bank = env.bank[3], env.bank[4], env.bank[5:7], env.bank[7]
    pv4 = pv_bank[:, 0:2 * H0 * (KC + 1)].rearrange("p (h c) -> p h c", c=KC + 1)

    def stages(i):
        return [between(i, lag, TILES + lag) for lag in range(5)]

    def least(count):
        return min(count, TILES) if isinstance(count, int) else count

    def loads(t, p):
        return 8 * (t - p) + 16

    def scatters(t, p):
        return 16 * (t - p)

    with nc.Block() as block:
        @block.sync
        def _(sp):
            x_dram = env.io["x"].rearrange("(i p) d -> p i d", p=P)
            c_dram = env.io["ctx"].rearrange("(i p) d -> p i d", p=P)
            sp.dma_start(X[:, 0:2, :], x_dram[:, 0:2, :]).then_inc(s.x_in_first, 16)
            sp.dma_start(ctx[:, 0, :], c_dram[:, 0, :]).then_inc(s.ctx_in[0], 16)
            loads = [(w_qk, env.io["a0_w_qk"]), (rot, env.io["a0_rot"]), (b_qk, env.io["a0_b_qk"]), (w_v, env.io["a0_w_v"]), (b_v, env.io["a0_b_v"]),
                     (sel, env.io["c_sel"]), (k_bias, env.io["c_k_bias"]), (w_o, env.io["a0_w_o"]), (b_o, env.io["a0_b_o"]), (w_c, env.io["f0_w_c"]),
                     (b_c, env.io["f0_b_c"]), (wealth, env.io["f0_wealth"]), (env.ident, env.io["c_ident"]), (env.ident16, env.io["c_ident16"]),
                     (env.tri16, env.io["c_tri16"]), (env.region, env.io["c_region"]), (env.iota2, env.io["c_iota2"])]
            for dst, src in loads:
                sp.dma_start(dst[:], src).then_inc(s.w_in, 16)
            sp.dma_start(ctx[:, 1, :], c_dram[:, 1, :]).then_inc(s.ctx_in[1], 16)
            sp.dma_start(X[:, 2:TILES, :], x_dram[:, 2:TILES, :]).then_inc(s.x_in, 16)
            env.n_w_in = 16 * len(loads)
            with sp.Fori(1, TILES // 2) as turn:
                for p in range(2):
                    i = 2 * turn
                    sp.wait_ge(s.v_mm, i + p - 1)
                    sp.dma_start(ctx[:, p, :], tile_of(c_dram, i + p)).then_inc(s.ctx_in[p], 16)

        @block.tensor
        def _(pe):
            def project(t, p):
                pe.wait_ge(s.norm_done, t + 1)
                pe.wait_ge(s.ctx_in[p], loads(t, p))
                if counted(t - 3):
                    pe.wait_ge(s.x_ready, t - 3)
                for n in range(4):
                    rhs = xn[:, p, :] if n < 2 else ctx[:, p, :]
                    mm = nc.tensor.matmul(work[:, n * P:(n + 1) * P], w_qk[:, n, :], rhs, start=True, stop=True)
                mm.then_inc(s.proj_done, 1)

            def project_v(t, p):
                pe.wait_ge(s.k_ready, t + 1)
                if counted(t):
                    pe.wait_ge(s.qb_ready, t)
                nc.tensor.matmul(kv_bank[:, 0:P], ctx[:, p, :], w_v[:], start=True, stop=True).then_inc(s.v_mm, 1)

            def replicate_q(bank, p, start, stop):
                for n in range(4):
                    for part, r in enumerate((r_hi, r_lo)):
                        mm = nc.tensor.matmul(bank[:, n * P:(n + 1) * P], sel[:, 2 * n + part, :], r[:, p, 0, :],
                                              start=(n == 0 and part == 0), stop=stop and part == 1, skip_group_check=True)
                return mm

            def queries(t, p):
                pe.wait_ge(s.rope_hi, t + 1)
                pe.wait_ge(s.rope_lo, t + 1)
                if counted(t):
                    pe.wait_ge(s.qa_ready, t)
                replicate_q(q_bank, p, True, True).then_inc(s.qa_mm, 1)

            def keys(t, p):
                pe.wait_ge(s.rope_hi, t + 1)
                pe.wait_ge(s.rope_lo, t + 1)
                if counted(t):
                    pe.wait_ge(s.v_ready, t)
                if counted(t - 1):
                    pe.wait_ge(s.qb_ready, t - 1)
                for n in range(4):
                    for part, r in enumerate((r_hi, r_lo)):
                        mm = nc.tensor.matmul(kv_bank[:, n * P:(n + 1) * P], sel[:, 8 + 2 * n + part, :], r[:, p, 1, :],
                                              start=(n == 0 and part == 0), stop=(part == 1), skip_group_check=True)
                mm.then_inc(s.k_mm, 1)

            def scores(t, p, j):
                if j == 0:
                    pe.wait_ge(s.k_ready, t + 1)
                    pe.wait_ge(s.qa_ready, t + 1)
                if counted(4 * t + j):
                    pe.wait_ge(s.max_done, 4 * t + j)
                r = slice(32 * j, 32 * j + 32)
                for n in range(4):
                    mm = nc.tensor.matmul(s_bank[:, n * P:(n + 1) * P], Qa[r, p, n, :], Kt[r, p, n, :],
                                          start=True, stop=True)
                mm.then_inc(s.s_mm, 1)

            def queries_less_max(t, p):
                pe.wait_ge(s.max_done, 4 * t + 4)
                pe.wait_ge(s.k_ready, least(t + 2))
                pe.wait_ge(s.v_ready, t + 1)
                replicate_q(kv_bank, p, True, False)
                for n in range(4):
                    mm = nc.tensor.matmul(kv_bank[:, n * P:(n + 1) * P], M[:, n, :], env.ident16[:], start=False, stop=True,
                                          skip_group_check=True)
                mm.then_inc(s.m_mm, 1)

            def scores_t(t, p, j):
                if j == 0:
                    pe.wait_ge(s.qb_ready, t + 1)
                if counted(4 * t + j - 1):
                    pe.wait_ge(s.exp_done, 4 * t + j - 1)
                r = slice(32 * j, 32 * j + 32)
                for n in range(4):
                    mm = nc.tensor.matmul(st_bank[j % 2][:, n * P:(n + 1) * P], Kt[r, p, n, :], Qb[r, p, n, :],
                                          start=True, stop=True)
                mm.then_inc(s.st_mm, 1)

            def values(t, p, j):
                if j % 2 == 0:
                    pe.wait_ge(s.low_dve, 2 * t + j // 2 + 1)
                else:
                    pe.wait_ge(s.low_pool, 2 * t + j // 2 + 1)
                if j == 0:
                    if counted(t):
                        pe.wait_ge(s.heads_ready, t)
                    pe.wait_ge(s.v_lo_done, t + 1)
                for n in range(4):
                    b, h = n // 2, 4 * (n % 2) + j
                    for part, (w, v) in enumerate((w, v) for w in (PT_hi, PT_lo) for v in (V_hi, V_lo)):
                        mm = nc.tensor.matmul(pv4[:, b * H0 + h, :], w[:, j, n, :], v[:, p, b, h, :],
                                              start=(part == 0), stop=(part == 3))
                mm.then_inc(s.pv_mm, 1)

            def step(i, p):
                A1, A2, Bs, O, R = stages(i)
                q = 1 - p
                if A1:
                    project(i, p)
                if A2:
                    scores(i - 1, q, 0)
                if Bs:
                    scores_t(i - 2, p, 0)
                if R:
                    pe.wait_ge(s.n2_done, i - 3)
                    if counted(i - 4):
                        pe.wait_ge(s.rank_read, i - 4)
                    nc.tensor.transpose(route_bank[:, 0:P], xr[:, p, :], env.ident[:]).then_inc(s.xt_mm, 1)
                if A2:
                    project_v(i - 1, q)
                if Bs:
                    scores_t(i - 2, p, 1)
                if R:
                    pe.wait_ge(s.xt_ready, i - 3)
                    nc.tensor.matmul(route_bank[:, 0:E], xT[:], w_c[:], start=True, stop=True).then_inc(s.logit_mm, 1)
                if O:
                    pe.wait_ge(s.heads_ready, i - 2)
                    pe.wait_ge(s.rope_mul, least(i + 1))
                    nc.tensor.transpose(work[:, 0:P], heads[:], env.ident[:]).then_inc(s.ht_mm, 1)
                if A2:
                    scores(i - 1, q, 1)
                if Bs:
                    values(i - 2, p, 0)
                if O:
                    pe.wait_ge(s.ht_ready, i - 2)
                    nc.tensor.matmul(work[:, 0:P], w_o[:], hT[:], start=True, stop=True).then_inc(s.out_mm, 1)
                if Bs:
                    scores_t(i - 2, p, 2)
                    values(i - 2, p, 1)
                if A2:
                    scores(i - 1, q, 2)
                if Bs:
                    scores_t(i - 2, p, 3)
                    values(i - 2, p, 2)
                if A1:
                    keys(i, p)
                if A2:
                    scores(i - 1, q, 3)
                if Bs:
                    values(i - 2, p, 3)
                if A1:
                    queries(i, p)
                if R:
                    pe.wait_ge(s.selsum_ready, i - 3)
                    if counted(i - 4):
                        pe.wait_ge(s.prev_ready, i - 4)
                    nc.tensor.matmul(route_bank[:, 0:E], env.tri16[:], selsum[:], start=True, stop=False)
                    nc.tensor.matmul(route_bank[:, 0:E], env.ones16[:], env.prev[:], start=False, stop=True) \
                        .then_inc(s.rank_mm, 1)
                if A2:
                    queries_less_max(i - 1, q)

            pe.wait_ge(s.w_in, env.n_w_in)
            pe.wait_ge(s.ones_set, 5)
            steady_loop(pe, step, 6, TILES - 2, TILES + 4)

        @block.scalar
        def _(act):
            def exps(t, j):
                act.wait_ge(s.st_mm, 4 * t + j + 1)
                if counted(4 * t + j - 3):
                    act.wait_ge(s.pv_mm, 4 * t + j - 3)
                nc.scalar.activation(PT[:, j, :, :].rearrange("p n t -> p (n t)"), st_bank[j % 2][:], ACT.Exp) \
                    .then_inc(s.exp_done, 1)

            def step(i, p):
                A1, A2, Bs, O, R = stages(i)
                q = 1 - p
                if Bs:
                    exps(i - 2, 0)
                if R:
                    act.wait_ge(s.xt_mm, i - 3)
                    if counted(i - 4):
                        act.wait_ge(s.logit_mm, i - 4)
                    nc.scalar.copy(xT[:], route_bank[:, 0:P]).then_inc(s.xt_ready, 1)
                if Bs:
                    exps(i - 2, 1)
                if O:
                    act.wait_ge(s.ht_mm, i - 2)
                    if counted(i - 3):
                        act.wait_ge(s.out_mm, i - 3)
                    nc.scalar.copy(hT[:], work[:, 0:P]).then_inc(s.ht_ready, 1)
                if A2:
                    act.wait_ge(s.v_ready, i)
                    nc.scalar.copy(V_hi[:, q, :, :, 0:KC], v_f[:].rearrange("p (b h c) -> p b h c", b=2, h=H0)) \
                        .then_inc(s.v_hi_done, 1)
                if R:
                    act.wait_ge(s.logit_b, i - 3)
                    nc.scalar.activation(le[:], lb[:], ACT.Exp, scale=-1.0).then_inc(s.gate_exp, 1)
                if Bs:
                    exps(i - 2, 2)
                if A1:
                    act.wait_ge(s.rope_done, i + 1)
                    if counted(i - 1):
                        act.wait_ge(s.m_mm, i - 1)
                    nc.scalar.copy(r_hi[:, p, :, :], rf[:]).then_inc(s.rope_hi, 1)
                if Bs:
                    exps(i - 2, 3)
                if A1:
                    act.wait_ge(s.k_mm, i + 1)
                    if counted(4 * i - 4):
                        act.wait_ge(s.st_mm, 4 * i - 4)
                    nc.scalar.activation(Kt[:, p, :, :].rearrange("p n t -> p (n t)"), kv_bank[:], ACT.Identity,
                                         bias=k_bias[:, 0:1]).then_inc(s.k_ready, 1)
                    act.wait_ge(s.qa_mm, i + 1)
                    if counted(4 * i - 4):
                        act.wait_ge(s.s_mm, 4 * i - 4)
                    nc.scalar.copy(Qa[:, p, :, :].rearrange("p n t -> p (n t)"), q_bank[:]).then_inc(s.qa_ready, 1)
                if A2:
                    act.wait_ge(s.m_mm, i)
                    if counted(4 * i - 8):
                        act.wait_ge(s.st_mm, 4 * i - 8)
                    nc.scalar.copy(Qb[:, q, :, :].rearrange("p n t -> p (n t)"), kv_bank[:]).then_inc(s.qb_ready, 1)

            act.wait_ge(s.w_in, env.n_w_in)
            act.wait_ge(s.ones_set, 5)
            steady_loop(act, step, 6, TILES - 2, TILES + 4)

        @block.vector
        def _(dve):
            def norm_stats(t):
                nc.vector.bn_stats(stat[:], tile_of(X, t)).then_inc(s.norm_stat, 1)
                dve.wait_ge(s.norm_stat, t + 1)
                alone(dve)
                nc.vector.bn_aggr(aggr[:], stat[:]).then_inc(s.norm_aggr, 1)

            def norm(t, p):
                dve.wait_ge(s.norm_rstd, t + 1)
                if counted(t - 1):
                    dve.wait_ge(s.proj_done, t - 1)
                nc.vector.tensor_scalar(xn[:, p, :], tile_of(X, t), aggr[:, 0:1], rstd[:, 0:1], ALU.subtract, ALU.mult) \
                    .then_inc(s.norm_done, 1)

            def rotate(t):
                dve.wait_ge(s.proj_done, t + 1)
                if counted(t):
                    dve.wait_ge(s.rope_sum, t)
                nc.vector.tensor_tensor(rm[:].rearrange("p a b t -> p (a b t)"), work[:],
                                        rot[:].rearrange("p a b t -> p (a b t)"), ALU.mult).then_inc(s.rope_mul, 1)

            def value_rows(t, p):
                dve.wait_ge(s.v_mm, t + 1)
                if counted(4 * t - 4):
                    dve.wait_ge(s.pv_mm, 4 * t - 4)
                if counted(t):
                    dve.wait_ge(s.v_lo_done, t)
                nc.vector.tensor_tensor(v_f[:], kv_bank[:, 0:P], b_v[:], ALU.add).then_inc(s.v_ready, 1)

            def value_lows(t, p):
                dve.wait_ge(s.v_hi_done, t + 1)
                nc.vector.tensor_tensor(V_lo[:, p, :, :, 0:KC], v_f[:].rearrange("p (b h c) -> p b h c", b=2, h=H0),
                                        V_hi[:, p, :, :, 0:KC], ALU.subtract).then_inc(s.v_lo_done, 1)

            def weight_lows(t, j):
                dve.wait_ge(s.exp_done, 4 * t + j + 1)
                if counted(4 * t + j - 3):
                    dve.wait_ge(s.pv_mm, 4 * t + j - 3)
                nc.vector.tensor_tensor(PT_lo[:, j, :, :], PT[:, j, :, :], PT_hi[:, j, :, :], ALU.subtract) \
                    .then_inc(s.low_dve, 1)

            def maxima(t, j):
                dve.wait_ge(s.s_mm, 4 * t + j + 1)
                if j == 0:
                    if counted(t):
                        dve.wait_ge(s.m_mm, t)
                nc.vector.tensor_reduce(M[:, :, 32 * j + ROW_MAX:32 * j + ROW_MAX + 1],
                                        s_bank[:].rearrange("p (n t) -> p n t", n=4), AX_X, ALU.max) \
                    .then_inc(s.max_done, 1)

            def step(i, p):
                A1, A2, Bs, O, R = stages(i)
                q = 1 - p
                t = i - 4
                u = i - 3
                if R:
                    sel_t = tile_of(env.SEL, t).rearrange("p (k e) -> p k e", k=2)
                if A1:
                    rotate(i)
                if A2:
                    maxima(i - 1, 0)
                if Bs:
                    weight_lows(i - 2, 0)
                if R:
                    dve.wait_ge(s.logit_mm, t + 1)
                    nc.vector.tensor_tensor(lb[:], route_bank[:, 0:E], b_c[:], ALU.add).then_inc(s.logit_b, 1)
                if A2:
                    value_rows(i - 1, q)
                    maxima(i - 1, 1)
                if R:
                    dve.wait_ge(s.gate_exp, t + 1)
                    nc.vector.tensor_scalar(l1[:], le[:], 1.0, None, ALU.add).then_inc(s.gate_1p, 1)
                if A2:
                    value_lows(i - 1, q)
                if O:
                    dve.wait_ge(s.out_mm, u + 1)
                    nc.vector.scalar_tensor_tensor(tile_of(X, u), work[:, 0:P], b_o[:, 0:1], tile_of(X, u),
                                                   ALU.add, ALU.add).then_inc(s.x_ready, 1)
                if R:
                    dve.wait_ge(s.gate_1p, t + 1)
                    nc.vector.reciprocal(li[:], l1[:]).then_inc(s.gate_inv, 1)
                if between(i, -1, TILES - 1):
                    dve.wait_ge(s.norm_done, i + 1)
                    if isinstance(i, int) and i == 1:
                        dve.wait_ge(s.x_in, 16)
                    alone(dve)
                    nc.vector.bn_stats(stat[:], tile_of(X, i + 1)).then_inc(s.norm_stat, 1)
                if R:
                    dve.wait_ge(s.gate_inv, t + 1)
                    nc.vector.tensor_tensor(bids[:], li[:], wealth[:], ALU.mult).then_inc(s.bids_ready, 1)
                if O:
                    dve.wait_ge(s.x_ready, u + 1)
                    alone(dve)
                    nc.vector.bn_stats(stat2[:], tile_of(X, u)).then_inc(s.n2_stat, 1)
                if between(i, -1, TILES - 1):
                    dve.wait_ge(s.norm_stat, i + 2)
                    alone(dve)
                    nc.vector.bn_aggr(aggr[:], stat[:]).then_inc(s.norm_aggr, 1)
                if R:
                    dve.wait_ge(s.bids_ready, t + 1)
                    alone(dve)
                    nc.vector.max(top[:], bids[:]).then_inc(s.top_val, 1)
                if O:
                    dve.wait_ge(s.n2_stat, u + 1)
                    alone(dve)
                    nc.vector.bn_aggr(aggr2[:], stat2[:]).then_inc(s.n2_aggr, 1)
                if A2:
                    maxima(i - 1, 2)
                if R:
                    dve.wait_ge(s.top_val, t + 1)
                    alone(dve)
                    nc.vector.max_index(topi[:], top[:], bids[:]).then_inc(s.top_idx, 1)
                    nc.vector.tensor_scalar(tile_of(env.TOP, t), top[:, 0:2], 1.0, None, ALU.mult)
                if Bs:
                    weight_lows(i - 2, 2)
                if R:
                    dve.wait_ge(s.top_idx, t + 1)
                    nc.vector.tensor_copy(topf[:], topi[:, 0:2]).then_inc(s.idx_f, 1)
                if between(i, -1, TILES - 1):
                    norm(i + 1, q)
                if R:
                    dve.wait_ge(s.idx_f, t + 1)
                    nc.vector.tensor_tensor(sel_t, env.iota2[:], topf[:].unsqueeze(2).to_broadcast([P, 2, E]), ALU.is_equal) \
                        .then_inc(s.sel_ready, 1)
                if O:
                    dve.wait_ge(s.n2_rstd, u + 1)
                    if counted(scatters(u, q)):
                        dve.wait_ge(s.scattered[q], scatters(u, q))
                    if counted(u - 1):
                        dve.wait_ge(s.xt_mm, u - 1)
                    nc.vector.tensor_scalar(xr[:, q, :], tile_of(X, u), aggr2[:, 0:1], rstd2[:, 0:1],
                                            ALU.subtract, ALU.mult).then_inc(s.n2_done, 1)
                if R:
                    dve.wait_ge(s.sel_ready, t + 1)
                    if counted(t):
                        dve.wait_ge(s.prev_ready, t)
                    nc.vector.tensor_tensor(selsum[:], sel_t[:, 0, :], sel_t[:, 1, :], ALU.add).then_inc(s.selsum_ready, 1)
                if A2:
                    maxima(i - 1, 3)
                if R:
                    dve.wait_ge(s.rank_mm, t + 1)
                    nc.vector.tensor_tensor(base[:], route_bank[:, 0:E], env.region[:], ALU.add).then_inc(s.rank_read, 1)
                    nc.vector.tensor_tensor(env.prev[:], env.prev[:], selsum[:], ALU.add).then_inc(s.prev_ready, 1)
                if Bs:
                    dve.wait_ge(s.pv_mm, 4 * i - 4)
                    nc.vector.reciprocal(inv[:], pv4[:, :, KC]).then_inc(s.sums_inv, 1)
                if R:
                    dve.wait_ge(s.rank_read, t + 1)
                    nc.vector.tensor_tensor(pm[:], sel_t, base[:].unsqueeze(1).to_broadcast([P, 2, E]), ALU.mult) \
                        .then_inc(s.pos_mul, 1)
                if Bs:
                    dve.wait_ge(s.sums_inv, i - 1)
                    if counted(i - 2):
                        dve.wait_ge(s.ht_mm, i - 2)
                    nc.vector.tensor_tensor(heads[:].rearrange("p (h c) -> p h c", c=KC), pv4[:, :, 0:KC],
                                            inv[:].unsqueeze(2).to_broadcast([P, 2 * H0, KC]), ALU.mult) \
                        .then_inc(s.heads_ready, 1)
                if R:
                    dve.wait_ge(s.pos_mul, t + 1)
                    nc.vector.tensor_reduce(tile_of(env.POS, t), pm[:], AX_X, ALU.add).then_inc(s.pos_ready, 1)
                    dve.wait_ge(s.pos_ready, t + 1)
                    if counted(scatters(t, p)):
                        dve.wait_ge(s.scattered[p], scatters(t, p))
                    nc.vector.tensor_scalar(idx[:, p, :], tile_of(env.POS, t), 1.0, None, ALU.mult).then_inc(s.idx_ready, 1)

            nc.vector.memset(V_hi[:], 1.0).then_inc(s.ones_set, 1)
            nc.vector.memset(V_lo[:], 0.0).then_inc(s.ones_set, 1)
            nc.vector.memset(M[:], 0.0).then_inc(s.ones_set, 1)
            nc.vector.memset(env.zeros[:], 0.0)
            nc.vector.memset(env.ones16[:], 1.0).then_inc(s.ones_set, 1)
            nc.vector.memset(env.prev[:], 0.0).then_inc(s.ones_set, 1)
            dve.wait_ge(s.x_in_first, 16)
            norm_stats(0)
            dve.wait_ge(s.w_in, env.n_w_in)
            for n in range(2):
                nc.vector.tensor_scalar(b_tmp[:, n, :], rot[:, n, 1, :], b_qk[:, 2 * n + 1:2 * n + 2], None, ALU.mult) \
                    .then_inc(s.tabs_t, 1)
            for n in range(2):
                dve.wait_ge(s.tabs_t, n + 1)
                nc.vector.scalar_tensor_tensor(rot_b[:, n, :], rot[:, n, 0, :], b_qk[:, 2 * n:2 * n + 1], b_tmp[:, n, :],
                                               ALU.mult, ALU.add).then_inc(s.tabs_done, 1)
            dve.wait_ge(s.ones_set, 5)
            norm(0, 0)
            steady_loop(dve, step, 6, TILES - 2, TILES + 4)

        @block.gpsimd
        def _(pool):
            nc.gpsimd.memset(env.eps[:], EPS).then_inc(s.consts_set, 1)
            nc.gpsimd.memset(env.minus_half[:], -0.5).then_inc(s.consts_set, 1)
            pool.wait_ge(s.consts_set, 2)

            def norm_scale(t):
                pool.wait_ge(s.norm_aggr, t + 1)
                nc.gpsimd.tensor_tensor(var_eps[:], aggr[:, 1:2], env.eps[:], ALU.add).then_inc(s.norm_eps, 1)
                pool.wait_ge(s.norm_eps, t + 1)
                nc.gpsimd.tensor_tensor(rstd[:], var_eps[:], env.minus_half[:], ALU.pow).then_inc(s.norm_rstd, 1)

            def step(i, p):
                A1, A2, Bs, O, R = stages(i)

                def weight_lows(t, j):
                    pool.wait_ge(s.exp_done, 4 * t + j + 1)
                    if counted(4 * t + j - 3):
                        pool.wait_ge(s.pv_mm, 4 * t + j - 3)
                    nc.gpsimd.tensor_tensor(PT_lo[:, j, :, :], PT[:, j, :, :], PT_hi[:, j, :, :], ALU.subtract) \
                        .then_inc(s.low_pool, 1)

                if between(i, 5, TILES + 5):
                    pool.wait_ge(s.idx_ready, i - 4)
                    alone(pool)
                    for k in range(2):
                        nc.gpsimd.indirect_dma_start(env.sorted_x, bass.IndirectOffsetOnAxis(idx[:, 1 - p, k:k + 1], 0),
                                                     xr[:, 1 - p, :], None).then_inc(s.scattered[1 - p], 16)
                if Bs:
                    weight_lows(i - 2, 1)
                if A1:
                    pool.wait_ge(s.rope_mul, i + 1)
                    nc.gpsimd.tensor_tensor(rs[:], rm[:, :, 0, :], rm[:, :, 1, :], ALU.add).then_inc(s.rope_sum, 1)
                    pool.wait_ge(s.rope_sum, i + 1)
                    if counted(i):
                        pool.wait_ge(s.rope_hi, i)
                    nc.gpsimd.tensor_tensor(rf[:], rs[:], rot_b[:], ALU.add).then_inc(s.rope_done, 1)
                    pool.wait_ge(s.rope_hi, i + 1)
                    if counted(i - 1):
                        pool.wait_ge(s.m_mm, i - 1)
                    nc.gpsimd.tensor_tensor(r_lo[:, p, :, :], rf[:], r_hi[:, p, :, :], ALU.subtract).then_inc(s.rope_lo, 1)
                if Bs:
                    weight_lows(i - 2, 3)
                if between(i, -1, TILES - 1):
                    norm_scale(i + 1)
                if O:
                    pool.wait_ge(s.n2_aggr, i - 2)
                    nc.gpsimd.tensor_tensor(var_eps2[:], aggr2[:, 1:2], env.eps[:], ALU.add).then_inc(s.n2_eps, 1)
                    pool.wait_ge(s.n2_eps, i - 2)
                    nc.gpsimd.tensor_tensor(rstd2[:], var_eps2[:], env.minus_half[:], ALU.pow).then_inc(s.n2_rstd, 1)

            norm_scale(0)
            pool.wait_ge(s.tabs_done, 2)
            steady_loop(pool, step, 6, TILES - 2, TILES + 5)
            for p in range(2):
                pool.wait_ge(s.scattered[p], 16 * TILES)


def split_weights(nc, env, stack):
    s = Names()
    (s.hi_done, s.lo_done) = \
        (semaphore(nc, env, "w_" + n) for n in "hi_done lo_done".split())
    s.w_in = [semaphore(nc, env, f"w_in{p}") for p in range(2)]
    w = stack.enter_context(nc.sbuf_tensor("w_full", [P, 2, 2, F], F32))
    turns = W_COLUMNS // 2

    def loads(t, p):
        return 8 * (t - p) + 16

    with nc.Block() as block:
        @block.sync
        def _(sp):
            for p in range(2):
                sp.dma_start(w[:, p, :, :], env.io["w_experts"][:, 2 * p:2 * p + 2, :]).then_inc(s.w_in[p], 16)
            with sp.Fori(1, turns // 2) as turn:
                for p in range(2):
                    i = 2 * turn + p
                    sp.wait_ge(s.lo_done, i - 1)
                    sp.dma_start(w[:, p, :, :], env.io["w_experts"][:, ds(2 * i, 2), :]).then_inc(s.w_in[p], 16)

        @block.scalar
        def _(act):
            with act.Fori(0, turns // 2) as turn:
                for p in range(2):
                    i = 2 * turn + p
                    act.wait_ge(s.w_in[p], loads(i, p))
                    nc.scalar.activation(env.w_hi[:, ds(2 * i, 2), :], w[:, p, :, :], ACT.Copy, scale=W_SCALE) \
                        .then_inc(s.hi_done, 1)

        @block.vector
        def _(dve):
            with dve.Fori(0, turns // 2) as turn:
                for p in range(2):
                    i = 2 * turn + p
                    dve.wait_ge(s.hi_done, i + 1)
                    nc.vector.scalar_tensor_tensor(env.w_lo[:, ds(2 * i, 2), :], w[:, p, :, :], W_SCALE,
                                                   env.w_hi[:, ds(2 * i, 2), :], ALU.mult, ALU.subtract) \
                        .then_inc(s.lo_done, 1)


def plan(nc, env, stack, name, slots, blocks, block_iota):
    s = Names()
    (s.iota_in, s.counted, s.step, s.pads_written, s.gap_exp) = \
        (semaphore(nc, env, f"{name}_{n}") for n in "iota_in counted step pads_written gap_exp".split())

    def sb(n, shape, dt=F32):
        return stack.enter_context(nc.sbuf_tensor(f"{name}_{n}", shape, dt))

    iota = sb("iota", [P, blocks, E])
    steps = sb("steps", [P, E, TILES])
    before = sb("before", [P, E, E])
    more = sb("more", [P, E, TILES])
    need = sb("need", [P, E])
    part = sb("part", [P, E, E])
    first = sb("first", [P, E])
    end = sb("end", [P, E])
    shift = sb("shift", [P, E])
    src_e = sb("src_e", [P, E])
    pad_f = sb("pad_f", [P, E])
    inside = sb("inside", [P, blocks, E])
    past = sb("past", [P, blocks, E])
    used = sb("used", [P, blocks])
    src = sb("src", [P, blocks])
    own = sb("own", [P, blocks])
    pads = sb("pads", [P, E], I32)
    gap = sb("gap", [P, TILES])
    total = sb("total", [P, TILES])
    shifts = sb("shifts", [P, TILES * slots, E])
    y_shift = sb("y_shift", [P, TILES * slots])
    counts = env.bank[0]

    with nc.Block() as block:
        @block.sync
        def _(sp):
            sp.dma_start(iota[:], block_iota).then_inc(s.iota_in, 16)
            sp.dma_start(steps[:], env.io["c_steps"]).then_inc(s.iota_in, 16)
            sp.dma_start(before[:], env.io["c_before"]).then_inc(s.iota_in, 16)
            sp.dma_start(env.sorted_x[SPARE:SPARE + P, :], env.zeros[:]).then_inc(s.pads_written, 16)
            sp.wait_ge(s.step, PADS_STEP)
            for e in range(E):
                row = sp.value_load(pads[0:1, e:e + 1], min_val=0, max_val=E * REGION - P)
                sp.dma_start(env.sorted_x[ds(row, P), :], env.zeros[:]).then_inc(s.pads_written, 16)
            sp.wait_ge(s.pads_written, 16 * (E + 1))

        if slots == 2:
            @block.scalar
            def _(act):
                act.wait_ge(s.step, GAP_STEP)
                nc.scalar.activation(gap[:], gap[:], ACT.Exp).then_inc(s.gap_exp, 1)

        @block.tensor
        def _(pe):
            nc.tensor.matmul(counts[:, 0:E], env.ones16[:], env.prev[:], start=True, stop=True).then_inc(s.counted, 1)

        @block.vector
        def _(dve):
            done = [0]

            def after(op):
                op.then_inc(s.step, 1)
                done[0] += 1
                dve.wait_ge(s.step, done[0])

            dve.wait_ge(s.counted, 1)
            dve.wait_ge(s.iota_in, 48)
            after(nc.vector.tensor_tensor(pad_f[:], counts[:, 0:E], env.region[:], ALU.add))
            after(nc.vector.tensor_scalar(pads[:], pad_f[:], 1.0, None, ALU.mult))
            assert done[0] == PADS_STEP
            if slots == 2:
                after(nc.vector.tensor_tensor(gap[:], env.TOP[:, :, 1], env.TOP[:, :, 0], ALU.subtract))
                assert done[0] == GAP_STEP
                dve.wait_ge(s.gap_exp, 1)
                after(nc.vector.tensor_scalar(total[:], gap[:], 1.0, None, ALU.add))
                after(nc.vector.reciprocal(env.W[:, :, 0], total[:]))
                after(nc.vector.tensor_tensor(env.W[:, :, 1], env.W[:, :, 0], gap[:], ALU.mult))
            after(nc.vector.tensor_tensor(more[:], counts[:, 0:E].unsqueeze(2).to_broadcast([P, E, TILES]), steps[:],
                                          ALU.is_gt))
            after(nc.vector.tensor_reduce(need[:], more[:], AX_X, ALU.add))
            after(nc.vector.tensor_tensor(part[:], before[:], need[:].unsqueeze(1).to_broadcast([P, E, E]), ALU.mult))
            after(nc.vector.tensor_reduce(first[:], part[:], AX_X, ALU.add))
            after(nc.vector.tensor_tensor(end[:], first[:], need[:], ALU.add))
            after(nc.vector.scalar_tensor_tensor(shift[:], first[:], -float(P), env.region[:], ALU.mult, ALU.add))
            after(nc.vector.tensor_scalar(src_e[:], shift[:], float(SPARE), None, ALU.subtract))
            after(nc.vector.tensor_tensor(inside[:], iota[:], first[:].unsqueeze(1).to_broadcast([P, blocks, E]), ALU.is_ge))
            after(nc.vector.tensor_tensor(past[:], iota[:], end[:].unsqueeze(1).to_broadcast([P, blocks, E]), ALU.is_ge))
            after(nc.vector.tensor_tensor(inside[:], inside[:], past[:], ALU.subtract))
            after(nc.vector.tensor_reduce(used[:], inside[:], AX_X, ALU.add))
            after(nc.vector.tensor_tensor(used[:], used[:], iota[:, :, 0], ALU.mult))
            after(nc.vector.tensor_tensor(past[:], inside[:], src_e[:].unsqueeze(1).to_broadcast([P, blocks, E]), ALU.mult))
            after(nc.vector.tensor_reduce(src[:], past[:], AX_X, ALU.add))
            after(nc.vector.scalar_tensor_tensor(src[:], used[:], float(P), src[:], ALU.mult, ALU.add))
            after(nc.vector.tensor_scalar(env.block_row[:, 0:blocks], src[:], float(SPARE), None, ALU.add))
            after(nc.vector.tensor_tensor(past[:], inside[:], env.iota2[:, 0:1, :].to_broadcast([P, blocks, E]), ALU.mult))
            after(nc.vector.tensor_reduce(own[:], past[:], AX_X, ALU.add))
            after(nc.vector.tensor_scalar(env.block_expert[:, 0:blocks], own[:], 1.0, None, ALU.mult))
            after(nc.vector.tensor_tensor(shifts[:], env.SEL[:, :, 0:slots * E].rearrange("p t (k e) -> p (t k) e", k=slots),
                                          shift[:].unsqueeze(1).to_broadcast([P, TILES * slots, E]), ALU.mult))
            after(nc.vector.tensor_reduce(y_shift[:], shifts[:], AX_X, ALU.add))
            after(nc.vector.tensor_tensor(env.Y_AT[:, :, 0:slots], env.POS[:, :, 0:slots], y_shift[:].rearrange("p (t k) -> p t k", k=slots),
                                          ALU.subtract))


def experts(nc, env, stack, name, blocks, gated, w_in, w_out, sorted_y):
    s = Names()
    (s.turned, s.x_hi_done, s.x_lo_done, s.hidden_mm, s.act_done, s.h_done, s.h_hi_done, s.h_lo_done, s.y_mm,
     s.y_ready) = \
        (semaphore(nc, env, f"{name}_{n}") for n in "turned x_hi_done x_lo_done hidden_mm act_done h_done h_hi_done h_lo_done y_mm y_ready".split())
    s.x_in = [semaphore(nc, env, f"{name}_x_in{p}") for p in range(BUFS)]
    s.y_out = [semaphore(nc, env, f"{name}_y_out{p}") for p in range(BUFS)]

    def sb(n, shape, dt=F32):
        return stack.enter_context(nc.sbuf_tensor(f"{name}_{n}", shape, dt))

    x = sb("x", [P, BUFS, P])
    x_hi = sb("x_hi", [P, 2, P], F16)
    x_lo = sb("x_lo", [P, 2, P], F16)
    g = sb("g", [P, 2, F])
    h = sb("h", [P, 2, F])
    h_hi = sb("h_hi", [P, 2, FC, P], F16)
    h_lo = sb("h_lo", [P, 2, FC, P], F16)
    y = sb("y", [P, BUFS, P])
    if not gated:
        b_hidden = sb("b_hidden", [P, E, FC])
        b_out = sb("b_out", [P, E, P])
        s.b_in = semaphore(nc, env, f"{name}_b_in")
    x_bank, gate_bank, up_bank, y_bank = env.bank[0:2], env.bank[2:4], env.bank[4:6], env.bank[6:8]

    def turn_count(t, p):
        if isinstance(t, int):
            return 16 * (t // BUFS + 1) if t >= 0 else 0
        return (16 // BUFS) * (t - p) + 16

    def steps(engine, step, lag_first, lag_last):
        first = -(-lag_first // BUFS) * BUFS
        last = blocks + lag_last
        for i in range(first):
            step(i, i % BUFS)
        with engine.Fori(first // BUFS, blocks // BUFS) as turn:
            for p in range(BUFS):
                step(BUFS * turn + p, p)
        for i in range(blocks, last):
            step(i, i % BUFS)

    with nc.Block() as block:
        @block.sync
        def _(sp):
            def step(i, p):
                if between(i, 0, blocks):
                    row = sp.value_load(env.block_row[0:1, ds(i, 1)], min_val=0, max_val=SPARE)
                    if counted(i - BUFS + 1):
                        sp.wait_ge(s.turned, i - BUFS + 1)
                    sp.dma_start(x[:, p, :], env.sorted_x[ds(row, P), :]).then_inc(s.x_in[p], 16)
                if between(i, 6, blocks + 6):
                    sp.wait_ge(s.y_ready, i - 5)
                    sp.dma_start(sorted_y.rearrange("(b p) d -> p b d", p=P)[:, ds(i - 6, 1), :].rearrange("p a d -> p (a d)"),
                                 y[:, (p - 6) % BUFS, :]).then_inc(s.y_out[(p - 6) % BUFS], 16)

            if not gated:
                sp.dma_start(b_hidden[:], env.io["f1_b_hidden"]).then_inc(s.b_in, 16)
                sp.dma_start(b_out[:], env.io["f1_b_out"]).then_inc(s.b_in, 16)
            steps(sp, step, 6, 6)
            for p in range(BUFS):
                sp.wait_ge(s.y_out[p], 16 * blocks // BUFS)

        @block.tensor
        def _(pe):
            def split_product(out, w, n, xs, turned=False):
                for k in range(3):
                    wk, xk = (env.w_hi, env.w_lo, env.w_hi)[k], (xs[0], xs[0], xs[1])[k]
                    mm = nc.tensor.matmul(out, wk[:, ds(w, 1), n * P:(n + 1) * P].rearrange("p a f -> p (a f)"), xk,
                                          start=(k == 0), stop=(k == 2))
                return mm

            def step(i, p):
                if between(i, 0, blocks):
                    pe.wait_ge(s.x_in[p], turn_count(i, p))
                    if counted(i - 1):
                        pe.wait_ge(s.x_lo_done, i - 1)
                    nc.tensor.transpose(x_bank[p % 2][:, 0:P], x[:, p, :], env.ident[:]).then_inc(s.turned, 1)
                if between(i, 1, blocks + 1):
                    q = (p + 1) % 2
                    e = pe.value_load(env.block_expert[0:1, ds(i - 1, 1)], min_val=0, max_val=E - 1)
                    pe.wait_ge(s.x_hi_done, i)
                    pe.wait_ge(s.x_lo_done, i)
                    if counted(i - 2):
                        pe.wait_ge(s.h_done, i - 2)
                    xs = (x_hi[:, q, :], x_lo[:, q, :])
                    for w0, bank in zip(w_in, (gate_bank, up_bank)):
                        for n in range(FC):
                            mm = split_product(bank[q][:, n * P:(n + 1) * P], e + w0, n, xs)
                        mm.then_inc(s.hidden_mm, 1)
                if between(i, 2, blocks + 2):
                    e = pe.value_load(env.block_expert[0:1, ds(i - 2, 1)], min_val=0, max_val=E - 1)
                    pe.wait_ge(s.h_hi_done, i - 1)
                    pe.wait_ge(s.h_lo_done, i - 1)
                    if counted(i - 3):
                        pe.wait_ge(s.y_ready, i - 3)
                    for n in range(FC):
                        for k in range(3):
                            hk, wk = (h_hi, h_hi, h_lo)[k], (env.w_hi, env.w_lo, env.w_hi)[k]
                            mm = nc.tensor.matmul(y_bank[p % 2][:, 0:P], hk[:, p % 2, n, :],
                                                  wk[:, ds(e + w_out, 1), n * P:(n + 1) * P].rearrange("p a f -> p (a f)"),
                                                  start=(n == 0 and k == 0), stop=(n == FC - 1 and k == 2))
                    mm.then_inc(s.y_mm, 1)

            steps(pe, step, 2, 2)

        @block.scalar
        def _(act):
            def step(i, p):
                if between(i, 0, blocks):
                    act.wait_ge(s.turned, i + 1)
                    if counted((i - 1) * len(w_in)):
                        act.wait_ge(s.hidden_mm, (i - 1) * len(w_in))
                    nc.scalar.activation(x_hi[:, p % 2, :], x_bank[p % 2][:, 0:P], ACT.Copy, scale=X_SCALE).then_inc(s.x_hi_done, 1)
                if between(i, 1, blocks + 1):
                    q = (p + 1) % 2
                    if gated:
                        act.wait_ge(s.hidden_mm, 2 * i - 1)
                        if counted(i - 2):
                            act.wait_ge(s.h_done, i - 2)
                        nc.scalar.activation(g[:, q, :], gate_bank[q][:], ACT.Silu, scale=1 / (X_SCALE * W_SCALE)) \
                            .then_inc(s.act_done, 1)
                        act.wait_ge(s.h_done, i)
                    else:
                        act.wait_ge(s.h_done, i)
                        if counted(i - 2):
                            act.wait_ge(s.h_lo_done, i - 2)
                        nc.scalar.activation(h[:, q, :], g[:, q, :], ACT.Gelu).then_inc(s.act_done, 1)
                        act.wait_ge(s.act_done, i)
                    if counted(i - 2):
                        act.wait_ge(s.y_mm, i - 2)
                    nc.scalar.activation(h_hi[:, q, :, :].rearrange("p n t -> p (n t)"), h[:, q, :], ACT.Copy,
                                         scale=1.0 if gated else W_SCALE).then_inc(s.h_hi_done, 1)

            steps(act, step, 1, 1)

        @block.vector
        def _(dve):
            def step(i, p):
                if between(i, 0, blocks):
                    dve.wait_ge(s.x_hi_done, i + 1)
                    nc.vector.scalar_tensor_tensor(x_lo[:, p % 2, :], x_bank[p % 2][:, 0:P], X_SCALE, x_hi[:, p % 2, :],
                                                   ALU.mult, ALU.subtract).then_inc(s.x_lo_done, 1)
                if between(i, 2, blocks + 2):
                    dve.wait_ge(s.y_mm, i - 1)
                    if counted(turn_count(i - 2 - BUFS, (p - 2) % BUFS)):
                        dve.wait_ge(s.y_out[(p - 2) % BUFS], turn_count(i - 2 - BUFS, (p - 2) % BUFS))
                    if gated:
                        nc.vector.tensor_scalar(y[:, (p - 2) % BUFS, :], y_bank[p % 2][:, 0:P], 1 / (W_SCALE * W_SCALE), None,
                                                ALU.mult).then_inc(s.y_ready, 1)
                    else:
                        alone(dve)
                        e = dve.value_load(env.block_expert[0:1, ds(i - 2, 1)], min_val=0, max_val=E - 1)
                        nc.vector.scalar_tensor_tensor(y[:, (p - 2) % BUFS, :], y_bank[p % 2][:, 0:P], 1 / (W_SCALE * W_SCALE),
                                                       b_out[:, ds(e, 1), :].rearrange("p a d -> p (a d)"), ALU.mult, ALU.add) \
                            .then_inc(s.y_ready, 1)
                if between(i, 1, blocks + 1):
                    q = (p + 1) % 2
                    if gated:
                        dve.wait_ge(s.hidden_mm, 2 * i)
                        dve.wait_ge(s.act_done, i)
                        if counted(i - 2):
                            dve.wait_ge(s.h_lo_done, i - 2)
                        nc.vector.scalar_tensor_tensor(h[:, q, :], up_bank[q][:], 1 / X_SCALE, g[:, q, :], ALU.mult, ALU.mult) \
                            .then_inc(s.h_done, 1)
                    else:
                        dve.wait_ge(s.hidden_mm, i)
                        alone(dve)
                        e = dve.value_load(env.block_expert[0:1, ds(i - 1, 1)], min_val=0, max_val=E - 1)
                        if counted(i - 2):
                            dve.wait_ge(s.act_done, i - 2)
                        nc.vector.scalar_tensor_tensor(g[:, q, :].rearrange("p (n t) -> p n t", n=FC),
                                                       gate_bank[q][:].rearrange("p (n t) -> p n t", n=FC),
                                                       1 / (X_SCALE * W_SCALE),
                                                       b_hidden[:, ds(e, 1), :].rearrange("p a n -> p (a n)").unsqueeze(2)
                                                       .to_broadcast([P, FC, P]), ALU.mult, ALU.add).then_inc(s.h_done, 1)
                    dve.wait_ge(s.h_hi_done, i)
                    nc.vector.scalar_tensor_tensor(h_lo[:, q, :, :].rearrange("p n t -> p (n t)"), h[:, q, :],
                                                   1.0 if gated else W_SCALE, h_hi[:, q, :, :].rearrange("p n t -> p (n t)"),
                                                   ALU.mult, ALU.subtract).then_inc(s.h_lo_done, 1)

            if not gated:
                dve.wait_ge(s.b_in, 32)
            steps(dve, step, 6, 2)


def attention1(nc, env, stack):
    s = Names()
    (s.at_ready, s.w_ready, s.added_1, s.added_2, s.norm_stat, s.norm_aggr, s.norm_eps, s.norm_rstd, s.norm_done,
     s.turned, s.turned_copied, s.proj_done, s.q_hi, s.k_hi, s.q_lo, s.k_lo, s.v_ready, s.v_hi_done, s.v_lo_done,
     s.k_mm, s.q_mm, s.k_ready, s.qa_ready, s.s_mm, s.max_done, s.m_mm, s.qb_ready, s.st_mm, s.exp_done, s.low_dve,
     s.low_pool, s.pv_mm, s.sums_inv, s.sums_done, s.heads_ready, s.x_bias, s.ht_mm, s.ht_ready, s.out_mm, s.x_ready,
     s.n2_stat, s.n2_aggr, s.n2_eps, s.n2_rstd, s.n2_done, s.xt_mm, s.xt_ready, s.logit_mm, s.logit_b, s.top_val,
     s.top_neg, s.top_idx, s.gate_exp, s.gate_sum, s.idx_f, s.sel_ready, s.sel_half, s.rank_mm, s.rank_read,
     s.prev_ready, s.pos_mul, s.pos_ready, s.idx_ready, s.w_in, s.scale_done, s.ones_set) = \
        (semaphore(nc, env, "a1_" + n) for n in """at_ready w_ready added_1 added_2 norm_stat norm_aggr norm_eps norm_rstd norm_done turned
        turned_copied proj_done q_hi k_hi q_lo k_lo v_ready v_hi_done v_lo_done k_mm q_mm k_ready qa_ready
        s_mm max_done m_mm qb_ready st_mm exp_done low_dve low_pool pv_mm sums_inv sums_done heads_ready
        x_bias ht_mm ht_ready out_mm x_ready n2_stat n2_aggr n2_eps n2_rstd n2_done xt_mm xt_ready logit_mm
        logit_b top_val top_neg top_idx gate_exp gate_sum idx_f sel_ready sel_half rank_mm rank_read
        prev_ready pos_mul pos_ready idx_ready w_in scale_done ones_set""".split())
    s.ctx_in = [semaphore(nc, env, f"a1_ctx_in{p}") for p in range(2)]
    s.gathered = [semaphore(nc, env, f"a1_gathered{p}") for p in range(2)]
    s.scattered = [semaphore(nc, env, f"a1_scattered{p}") for p in range(2)]

    def sb(name, shape, dt=F32):
        return stack.enter_context(nc.sbuf_tensor("t1_" + name, shape, dt))

    X, sel, k_bias = env.X, env.sel, env.k_bias_sb
    w_q, w_k, w_v, w_o = (sb("w_" + n, [P, P]) for n in "qkvo")
    b_qk = sb("b_qk", [P, 2])
    b_v, b_o = sb("b_v", [P, P]), sb("b_o", [P, P])
    w_g, b_g = sb("w_g", [P, E]), sb("b_g", [P, E])
    ctx = sb("ctx", [P, 2, P])
    y_at = sb("y_at", [P, 2, 2], I32)
    y_w = sb("y_w", [P, 2, 2])
    y = sb("y", [P, 2, 2, P])
    stat, aggr, rstd, var_eps = sb("stat", [P, 6]), sb("aggr", [P, 2]), sb("rstd", [P, 1]), sb("var_eps", [P, 1])
    stat2, aggr2, rstd2, var_eps2 = sb("stat2", [P, 6]), sb("aggr2", [P, 2]), sb("rstd2", [P, 1]), sb("var_eps2", [P, 1])
    xn = sb("xn", [P, 2, P])
    T = sb("T", [P, 2, P])
    r_hi = sb("r_hi", [P, 2, 2, P], F16)
    r_lo = sb("r_lo", [P, 2, 2, P], F16)
    Qa = sb("Qa", [P, 2, GROUPS1, P], F16)
    Qb = sb("Qb", [P, 2, GROUPS1, P], F16)
    Kt = sb("Kt", [P, 2, GROUPS1, P], F16)
    v_f = sb("v_f", [P, 2, P])
    V = sb("V", [P, 2, H1, 2 * KC + 1], F16)
    M = sb("M", [P, GROUPS1, P], F16)
    PT = sb("PT", [P, 2, 8, CH])
    PT_hi = PT[:].bitcast(BF16).rearrange("p r n (t two) -> p r n t two", two=2)[:, :, :, :, 1]
    PT_lo = sb("PT_lo", [P, 2, 8, CH], F16)
    inv = sb("inv", [P, H1])
    sums = sb("sums", [P, H1, KC])
    heads = sb("heads", [P, P])
    x_b = sb("x_b", [P, 2, P])
    hT = sb("hT", [P, P])
    xr = sb("xr", [P, 2, P])
    xT = sb("xT", [P, P])
    lb, le = sb("lb", [P, E]), sb("le", [P, E])
    top, topi, topf, topn = sb("top", [P, E]), sb("topi", [P, E], U32), sb("topf", [P, 1]), sb("topn", [P, 1])
    gate_sum = sb("gate_sum", [P, 1])
    sel16 = sb("sel16", [P, E], F16)
    base, pm = sb("base", [P, E]), sb("pm", [P, E])
    idx = sb("idx", [P, 2, 1], I32)

    work, q_bank, kv_bank = env.bank[0], env.bank[1], env.bank[2]
    s_bank, route_bank, st_bank, pv_bank = env.bank[3], env.bank[4], env.bank[5:7], env.bank[7]
    pv = pv_bank[:, 0:H1 * (2 * KC + 1)].rearrange("p (h c) -> p h c", c=2 * KC + 1)

    def stages(i):
        return [between(i, lag, TILES + lag) for lag in range(8)]

    def loads(t, p):
        return 8 * (t - p) + 16

    with nc.Block() as block:
        @block.sync
        def _(sp):
            c_dram = env.io["ctx"].rearrange("(i p) d -> p i d", p=P)
            weights = [(w_q, env.io["a1_w_q"]), (w_k, env.io["a1_w_k"]), (w_v, env.io["a1_w_v"]), (w_o, env.io["a1_w_o"]), (b_qk, env.io["a1_b_qk"]),
                       (b_v, env.io["a1_b_v"]), (b_o, env.io["a1_b_o"]), (w_g, env.io["f1_w_g"]), (b_g, env.io["f1_b_g"])]
            env.n_w_in = 16 * len(weights)
            for dst, src in weights:
                sp.dma_start(dst[:], src).then_inc(s.w_in, 16)
            for p in range(2):
                sp.dma_start(ctx[:, p, :], c_dram[:, p, :]).then_inc(s.ctx_in[p], 16)
            with sp.Fori(1, TILES // 2) as turn:
                for p in range(2):
                    i = 2 * turn
                    sp.wait_ge(s.turned, i + p - 1)
                    sp.dma_start(ctx[:, p, :], tile_of(c_dram, i + p)).then_inc(s.ctx_in[p], 16)

        @block.tensor
        def _(pe):
            def turn_rows(t, p):
                pe.wait_ge(s.norm_done, t + 1)
                pe.wait_ge(s.ctx_in[p], loads(t, p))
                if counted(t):
                    pe.wait_ge(s.q_lo, t)
                if counted(t):
                    pe.wait_ge(s.k_lo, t)
                if counted(t):
                    pe.wait_ge(s.v_ready, t)
                nc.tensor.transpose(work[:, 0:P], xn[:, p, :], env.ident[:])
                nc.tensor.transpose(work[:, P:2 * P], ctx[:, p, :], env.ident[:]).then_inc(s.turned, 1)

            def project(t, p):
                pe.wait_ge(s.turned_copied, t + 1)
                nc.tensor.matmul(work[:, 2 * P:3 * P], w_q[:], T[:, 0, :], start=True, stop=True)
                nc.tensor.matmul(work[:, 3 * P:4 * P], w_k[:], T[:, 1, :], start=True, stop=True)
                nc.tensor.matmul(work[:, 0:P], T[:, 1, :], w_v[:], start=True, stop=True).then_inc(s.proj_done, 1)

            def replicate(bank, p, kind, stop):
                for n in range(GROUPS1):
                    for part, r in enumerate((r_hi, r_lo)):
                        mm = nc.tensor.matmul(bank[:, n * P:(n + 1) * P], sel[:, 8 * kind + 2 * n + part, :], r[:, p, kind, :],
                                              start=(n == 0 and part == 0), stop=stop and part == 1, skip_group_check=True)
                return mm

            def keys_and_queries(t, p):
                pe.wait_ge(s.k_hi, t + 1)
                pe.wait_ge(s.k_lo, t + 1)
                if counted(t - 1):
                    pe.wait_ge(s.qb_ready, t - 1)
                replicate(kv_bank, p, 1, True).then_inc(s.k_mm, 1)
                pe.wait_ge(s.q_hi, t + 1)
                pe.wait_ge(s.q_lo, t + 1)
                if counted(t):
                    pe.wait_ge(s.qa_ready, t)
                replicate(q_bank, p, 0, True).then_inc(s.q_mm, 1)

            def head_products(bank, at, left, right, p, j):
                rows = slice(32 * j, 32 * j + 32)
                for n in range(GROUPS1):
                    for b in range(2):
                        c = slice(b * CH, b * CH + CH)
                        mm = nc.tensor.matmul(bank[c, at + n * CH:at + (n + 1) * CH], left[rows, p, n, c], right[rows, p, n, c],
                                              start=True, stop=True)
                return mm

            def scores(t, p, j):
                if j == 0:
                    pe.wait_ge(s.k_ready, t + 1)
                    pe.wait_ge(s.qa_ready, t + 1)
                if j % 2 == 0:
                    if counted(2 * t + j // 2):
                        pe.wait_ge(s.max_done, 2 * t + j // 2)
                else:
                    pe.wait_ge(s.s_mm, 4 * t + j)
                alone(pe)
                head_products(s_bank, 4 * CH * (j % 2), Qa, Kt, p, j).then_inc(s.s_mm, 1)

            def queries_less_max(t, p):
                pe.wait_ge(s.max_done, 2 * t + 2)
                pe.wait_ge(s.k_ready, min(t + 2, TILES) if isinstance(t, int) else t + 2)
                replicate(kv_bank, p, 0, False)
                for n in range(GROUPS1):
                    mm = nc.tensor.matmul(kv_bank[:, n * P:(n + 1) * P], M[:, n, :], env.ident16[:], start=False, stop=True,
                                          skip_group_check=True)
                mm.then_inc(s.m_mm, 1)

            def scores_t(t, p, j):
                if j == 0:
                    pe.wait_ge(s.qb_ready, t + 1)
                if j % 2 == 0:
                    if counted(2 * t + j // 2 - 1):
                        pe.wait_ge(s.exp_done, 2 * t + j // 2 - 1)
                else:
                    pe.wait_ge(s.st_mm, 4 * t + j)
                alone(pe)
                head_products(st_bank[j // 2], 4 * CH * (j % 2), Kt, Qb, p, j).then_inc(s.st_mm, 1)

            def values(t, p, r):
                if r == 0:
                    pe.wait_ge(s.low_dve, t + 1)
                    if counted(t):
                        pe.wait_ge(s.heads_ready, t)
                    pe.wait_ge(s.v_lo_done, t + 1)
                else:
                    pe.wait_ge(s.low_pool, t + 1)
                alone(pe)
                for jj in range(2):
                    for n in range(GROUPS1):
                        h = 4 * n + 2 * r + jj
                        for b in range(2):
                            c = slice(b * CH, b * CH + CH)
                            for part, w in enumerate((PT_hi, PT_lo)):
                                mm = nc.tensor.matmul(pv[c, h, :], w[c, r, 4 * jj + n, :], V[c, p, h, :],
                                                      start=(part == 0), stop=(part == 1))
                mm.then_inc(s.pv_mm, 1)

            def step(i, p):
                G, C, A1, A2, Bs, O, R, S = stages(i)
                q = 1 - p
                if A1:
                    turn_rows(i - 2, p)
                if A2:
                    scores(i - 3, q, 0)
                if Bs:
                    scores_t(i - 4, p, 0)
                if R:
                    pe.wait_ge(s.n2_done, i - 5)
                    if counted(i - 6):
                        pe.wait_ge(s.rank_read, i - 6)
                    nc.tensor.transpose(route_bank[:, 0:P], xr[:, p, :], env.ident[:]).then_inc(s.xt_mm, 1)
                if A2:
                    scores(i - 3, q, 1)
                if Bs:
                    scores_t(i - 4, p, 1)
                if A1:
                    project(i - 2, p)
                if Bs:
                    scores_t(i - 4, p, 2)
                if A2:
                    scores(i - 3, q, 2)
                if R:
                    pe.wait_ge(s.xt_ready, i - 5)
                    nc.tensor.matmul(route_bank[:, 0:E], xT[:], w_g[:], start=True, stop=True).then_inc(s.logit_mm, 1)
                if Bs:
                    scores_t(i - 4, p, 3)
                if A2:
                    scores(i - 3, q, 3)
                if Bs:
                    values(i - 4, p, 0)
                if O:
                    pe.wait_ge(s.heads_ready, i - 4)
                    pe.wait_ge(s.qa_ready, min(i - 2, TILES) if isinstance(i, int) else i - 2)
                    nc.tensor.transpose(q_bank[:, 0:P], heads[:], env.ident[:]).then_inc(s.ht_mm, 1)
                if Bs:
                    values(i - 4, p, 1)
                if O:
                    pe.wait_ge(s.ht_ready, i - 4)
                    nc.tensor.matmul(q_bank[:, 0:P], hT[:], w_o[:], start=True, stop=True).then_inc(s.out_mm, 1)
                if A1:
                    if counted(i - 4):
                        pe.wait_ge(s.x_ready, i - 4)
                    keys_and_queries(i - 2, p)
                if R:
                    pe.wait_ge(s.sel_half, i - 5)
                    if counted(i - 6):
                        pe.wait_ge(s.prev_ready, i - 6)
                    nc.tensor.matmul(route_bank[:, 0:E], env.tri16[:], sel16[:], start=True, stop=False)
                    nc.tensor.matmul(route_bank[:, 0:E], env.ones16[:], env.prev[:], start=False, stop=True) \
                        .then_inc(s.rank_mm, 1)
                if A2:
                    queries_less_max(i - 3, q)

            pe.wait_ge(s.w_in, env.n_w_in)
            pe.wait_ge(s.scale_done, 1)
            pe.wait_ge(s.ones_set, 3)
            steady_loop(pe, step, 8, TILES, TILES + 7)

        @block.scalar
        def _(act):
            def exps(t, r):
                act.wait_ge(s.st_mm, 4 * t + 2 * r + 2)
                if counted(2 * t + r - 1):
                    act.wait_ge(s.pv_mm, 2 * t + r - 1)
                nc.scalar.activation(PT[:, r, :, :].rearrange("p n t -> p (n t)"), st_bank[r][:], ACT.Exp) \
                    .then_inc(s.exp_done, 1)

            def step(i, p):
                G, C, A1, A2, Bs, O, R, S = stages(i)
                q = 1 - p
                if A1:
                    act.wait_ge(s.turned, i - 1)
                    if counted(i - 2):
                        act.wait_ge(s.proj_done, i - 2)
                    nc.scalar.copy(T[:].rearrange("p a t -> p (a t)"), work[:, 0:2 * P]).then_inc(s.turned_copied, 1)
                if Bs:
                    exps(i - 4, 0)
                if R:
                    act.wait_ge(s.xt_mm, i - 5)
                    if counted(i - 6):
                        act.wait_ge(s.logit_mm, i - 6)
                    nc.scalar.copy(xT[:], route_bank[:, 0:P]).then_inc(s.xt_ready, 1)
                if Bs:
                    exps(i - 4, 1)
                if A1:
                    act.wait_ge(s.proj_done, i - 1)
                    if counted(i - 3):
                        act.wait_ge(s.m_mm, i - 3)
                    for n, done in enumerate((s.q_hi, s.k_hi)):
                        nc.scalar.activation(r_hi[:, p, n, :], work[:, (2 + n) * P:(3 + n) * P], ACT.Identity,
                                             bias=b_qk[:, n:n + 1]).then_inc(done, 1)
                if A2:
                    act.wait_ge(s.v_ready, i - 2)
                    if counted(2 * (i - 4)):
                        act.wait_ge(s.pv_mm, 2 * (i - 4))
                    nc.scalar.copy(V[:, q, :, 0:KC], v_f[:, q, :].rearrange("p (h c) -> p h c", h=H1)).then_inc(s.v_hi_done, 1)
                if O:
                    act.wait_ge(s.ht_mm, i - 4)
                    if counted(i - 5):
                        act.wait_ge(s.out_mm, i - 5)
                    nc.scalar.copy(hT[:], q_bank[:, 0:P]).then_inc(s.ht_ready, 1)
                if R:
                    act.wait_ge(s.top_neg, i - 5)
                    if counted(i - 6):
                        act.wait_ge(s.gate_sum, i - 6)
                    nc.scalar.activation(le[:], lb[:], ACT.Exp, bias=topn[:, 0:1]).then_inc(s.gate_exp, 1)
                if A1:
                    act.wait_ge(s.k_mm, i - 1)
                    if counted(4 * (i - 3)):
                        act.wait_ge(s.st_mm, 4 * (i - 3))
                    nc.scalar.activation(Kt[:, p, :, :].rearrange("p n t -> p (n t)"), kv_bank[:], ACT.Identity,
                                         bias=k_bias[:, 0:1]).then_inc(s.k_ready, 1)
                    act.wait_ge(s.q_mm, i - 1)
                    if counted(4 * (i - 3)):
                        act.wait_ge(s.s_mm, 4 * (i - 3))
                    nc.scalar.copy(Qa[:, p, :, :].rearrange("p n t -> p (n t)"), q_bank[:]).then_inc(s.qa_ready, 1)
                if A2:
                    act.wait_ge(s.m_mm, i - 2)
                    if counted(4 * (i - 4)):
                        act.wait_ge(s.st_mm, 4 * (i - 4))
                    nc.scalar.copy(Qb[:, q, :, :].rearrange("p n t -> p (n t)"), kv_bank[:]).then_inc(s.qb_ready, 1)

            act.wait_ge(s.w_in, env.n_w_in)
            act.wait_ge(s.scale_done, 2)
            act.wait_ge(s.ones_set, 3)
            steady_loop(act, step, 8, TILES, TILES + 7)

        @block.vector
        def _(dve):
            def maxima(t, r):
                dve.wait_ge(s.s_mm, 4 * t + 2 * r + 2)
                if r == 0:
                    if counted(t):
                        dve.wait_ge(s.m_mm, t)
                rows = M[:].rearrange("p n (j r) -> p j n r", r=32)[:, 2 * r:2 * r + 2, :, ROW_MAX:ROW_MAX + 1]
                nc.vector.tensor_reduce(rows, s_bank[:].rearrange("p (j n t) -> p j n t", j=2, n=GROUPS1), AX_X, ALU.max) \
                    .then_inc(s.max_done, 1)

            def step(i, p):
                G, C, A1, A2, Bs, O, R, S = stages(i)
                q = 1 - p
                t = i - 6
                u = i - 5
                if G:
                    if counted(loads(i - 2, p)):
                        dve.wait_ge(s.gathered[p], loads(i - 2, p))
                    nc.vector.tensor_scalar(y_at[:, p, :], tile_of(env.Y_AT, i), 1.0, None, ALU.mult).then_inc(s.at_ready, 1)
                if A2:
                    maxima(i - 3, 0)
                if C:
                    if counted(i - 1):
                        dve.wait_ge(s.added_2, i - 1)
                    nc.vector.tensor_scalar(y_w[:, q, :], tile_of(env.W, i - 1), 1.0, None, ALU.mult).then_inc(s.w_ready, 1)
                if R:
                    dve.wait_ge(s.logit_mm, t + 1)
                    nc.vector.tensor_tensor(lb[:], route_bank[:, 0:E], b_g[:], ALU.add).then_inc(s.logit_b, 1)
                if C:
                    dve.wait_ge(s.w_ready, i)
                    dve.wait_ge(s.gathered[q], 2 * loads(i - 1, q))
                    nc.vector.scalar_tensor_tensor(tile_of(X, i - 1), y[:, q, 0, :], y_w[:, q, 0:1], tile_of(X, i - 1),
                                                   ALU.mult, ALU.add).then_inc(s.added_1, 1)
                if R:
                    dve.wait_ge(s.logit_b, t + 1)
                    alone(dve)
                    nc.vector.max(top[:], lb[:]).then_inc(s.top_val, 1)
                if C:
                    dve.wait_ge(s.added_1, i)
                    nc.vector.scalar_tensor_tensor(tile_of(X, i - 1), y[:, q, 1, :], y_w[:, q, 1:2], tile_of(X, i - 1),
                                                   ALU.mult, ALU.add).then_inc(s.added_2, 1)
                if R:
                    dve.wait_ge(s.top_val, t + 1)
                    nc.vector.tensor_scalar(topn[:], top[:, 0:1], -1.0, None, ALU.mult).then_inc(s.top_neg, 1)
                    alone(dve)
                    nc.vector.max_index(topi[:], top[:], lb[:]).then_inc(s.top_idx, 1)
                if Bs:
                    dve.wait_ge(s.exp_done, 2 * (i - 4) + 1)
                    if counted(2 * (i - 4) - 1):
                        dve.wait_ge(s.pv_mm, 2 * (i - 4) - 1)
                    nc.vector.tensor_tensor(PT_lo[:, 0, :, :], PT[:, 0, :, :], PT_hi[:, 0, :, :], ALU.subtract) \
                        .then_inc(s.low_dve, 1)
                if C:
                    dve.wait_ge(s.added_2, i)
                    if counted(i - 1):
                        dve.wait_ge(s.norm_aggr, i - 1)
                    alone(dve)
                    nc.vector.bn_stats(stat[:], tile_of(X, i - 1)).then_inc(s.norm_stat, 1)
                if R:
                    dve.wait_ge(s.top_idx, t + 1)
                    nc.vector.tensor_copy(topf[:], topi[:, 0:1]).then_inc(s.idx_f, 1)
                if C:
                    dve.wait_ge(s.norm_stat, i)
                    if counted(i - 1):
                        dve.wait_ge(s.norm_done, i - 1)
                    alone(dve)
                    nc.vector.bn_aggr(aggr[:], stat[:]).then_inc(s.norm_aggr, 1)
                if R:
                    dve.wait_ge(s.idx_f, t + 1)
                    nc.vector.tensor_scalar(tile_of(env.SEL, t)[:, 0:E], env.iota2[:, 0, :], topf[:, 0:1], None, ALU.is_equal) \
                        .then_inc(s.sel_ready, 1)
                if A1:
                    dve.wait_ge(s.k_hi, i - 1)
                    if counted(i - 3):
                        dve.wait_ge(s.v_lo_done, i - 3)
                    nc.vector.tensor_tensor(v_f[:, p, :], work[:, 0:P], b_v[:], ALU.add).then_inc(s.v_ready, 1)
                if R:
                    dve.wait_ge(s.sel_ready, t + 1)
                    if counted(t):
                        dve.wait_ge(s.prev_ready, t)
                    nc.vector.tensor_scalar(sel16[:], tile_of(env.SEL, t)[:, 0:E], 1.0, None, ALU.mult).then_inc(s.sel_half, 1)
                if A1:
                    for n, lo in enumerate((s.q_lo, s.k_lo)):
                        nc.vector.scalar_tensor_tensor(r_lo[:, p, n, :], work[:, (2 + n) * P:(3 + n) * P], b_qk[:, n:n + 1],
                                                       r_hi[:, p, n, :], ALU.add, ALU.subtract).then_inc(lo, 1)
                if A2:
                    maxima(i - 3, 1)
                if R:
                    dve.wait_ge(s.gate_exp, t + 1)
                    nc.vector.tensor_reduce(gate_sum[:], le[:], AX_X, ALU.add).then_inc(s.gate_sum, 1)
                if C:
                    dve.wait_ge(s.norm_rstd, i)
                    if counted(i - 3):
                        dve.wait_ge(s.turned, i - 3)
                    nc.vector.tensor_scalar(xn[:, q, :], tile_of(X, i - 1), aggr[:, 0:1], rstd[:, 0:1], ALU.subtract, ALU.mult) \
                        .then_inc(s.norm_done, 1)
                if R:
                    dve.wait_ge(s.gate_sum, t + 1)
                    nc.vector.reciprocal(tile_of(env.W1, t), gate_sum[:])
                if O:
                    dve.wait_ge(s.out_mm, u + 1)
                    dve.wait_ge(s.x_bias, u + 1)
                    nc.vector.tensor_tensor(tile_of(X, u), q_bank[:, 0:P], x_b[:, q, :], ALU.add).then_inc(s.x_ready, 1)
                    dve.wait_ge(s.x_ready, u + 1)
                    if counted(u):
                        dve.wait_ge(s.n2_aggr, u)
                    alone(dve)
                    nc.vector.bn_stats(stat2[:], tile_of(X, u)).then_inc(s.n2_stat, 1)
                if R:
                    dve.wait_ge(s.rank_mm, t + 1)
                    nc.vector.tensor_tensor(base[:], route_bank[:, 0:E], env.region[:], ALU.add).then_inc(s.rank_read, 1)
                    nc.vector.tensor_tensor(env.prev[:], env.prev[:], sel16[:], ALU.add).then_inc(s.prev_ready, 1)
                if O:
                    dve.wait_ge(s.n2_stat, u + 1)
                    if counted(u):
                        dve.wait_ge(s.n2_done, u)
                    alone(dve)
                    nc.vector.bn_aggr(aggr2[:], stat2[:]).then_inc(s.n2_aggr, 1)
                if R:
                    dve.wait_ge(s.rank_read, t + 1)
                    nc.vector.tensor_tensor(pm[:], sel16[:], base[:], ALU.mult).then_inc(s.pos_mul, 1)
                if Bs:
                    dve.wait_ge(s.pv_mm, 2 * (i - 3))
                    nc.vector.reciprocal(inv[:], pv[:, :, KC]).then_inc(s.sums_inv, 1)
                    nc.vector.tensor_scalar(sums[:], pv[:, :, 0:KC], 1.0, None, ALU.mult).then_inc(s.sums_inv, 1)
                if R:
                    dve.wait_ge(s.pos_mul, t + 1)
                    nc.vector.tensor_reduce(tile_of(env.POS, t)[:, 0:1], pm[:], AX_X, ALU.add).then_inc(s.pos_ready, 1)
                if Bs:
                    dve.wait_ge(s.sums_inv, 2 * (i - 3))
                    nc.vector.tensor_tensor(sums[:], sums[:], pv[:, :, KC + 1:2 * KC + 1], ALU.add).then_inc(s.sums_done, 1)
                if O:
                    dve.wait_ge(s.n2_rstd, u + 1)
                    if counted(loads(u - 2, q)):
                        dve.wait_ge(s.scattered[q], loads(u - 2, q))
                    if counted(u - 1):
                        dve.wait_ge(s.xt_mm, u - 1)
                    nc.vector.tensor_scalar(xr[:, q, :], tile_of(X, u), aggr2[:, 0:1], rstd2[:, 0:1],
                                            ALU.subtract, ALU.mult).then_inc(s.n2_done, 1)
                if R:
                    dve.wait_ge(s.pos_ready, t + 1)
                    if counted(loads(t - 2, p)):
                        dve.wait_ge(s.scattered[p], loads(t - 2, p))
                    nc.vector.tensor_scalar(idx[:, p, :], tile_of(env.POS, t)[:, 0:1], 1.0, None, ALU.mult).then_inc(s.idx_ready, 1)
                if Bs:
                    dve.wait_ge(s.sums_done, i - 3)
                    if counted(i - 4):
                        dve.wait_ge(s.ht_mm, i - 4)
                    nc.vector.tensor_tensor(heads[:].rearrange("p (h c) -> p h c", c=KC), sums[:],
                                            inv[:].unsqueeze(2).to_broadcast([P, H1, KC]), ALU.mult).then_inc(s.heads_ready, 1)

            nc.vector.memset(V[:], 1.0).then_inc(s.ones_set, 1)
            nc.vector.memset(M[:], 0.0).then_inc(s.ones_set, 1)
            nc.vector.memset(env.prev[:], 0.0).then_inc(s.ones_set, 1)
            dve.wait_ge(s.w_in, env.n_w_in)
            nc.vector.tensor_scalar(w_q[:], w_q[:], KC ** -0.5, None, ALU.mult).then_inc(s.scale_done, 1)
            nc.vector.tensor_scalar(b_qk[:, 0:1], b_qk[:, 0:1], KC ** -0.5, None, ALU.mult).then_inc(s.scale_done, 1)
            dve.wait_ge(s.scale_done, 2)
            dve.wait_ge(s.ones_set, 3)
            steady_loop(dve, step, 8, TILES, TILES + 7)

        @block.gpsimd
        def _(pool):
            def step(i, p):
                G, C, A1, A2, Bs, O, R, S = stages(i)
                q = 1 - p
                if S:
                    pool.wait_ge(s.idx_ready, i - 6)
                    alone(pool)
                    nc.gpsimd.indirect_dma_start(env.sorted_x, bass.IndirectOffsetOnAxis(idx[:, q, 0:1], 0),
                                                 xr[:, q, :], None).then_inc(s.scattered[q], 16)
                if G:
                    pool.wait_ge(s.at_ready, i + 1)
                    if counted(i - 1):
                        pool.wait_ge(s.added_2, i - 1)
                    alone(pool)
                    for k in range(2):
                        nc.gpsimd.indirect_dma_start(y[:, p, k, :], None, env.sorted_y0,
                                                     bass.IndirectOffsetOnAxis(y_at[:, p, k:k + 1], 0)).then_inc(s.gathered[p], 16)
                if A2:
                    pool.wait_ge(s.v_hi_done, i - 2)
                    nc.gpsimd.tensor_tensor(V[:, q, :, KC + 1:2 * KC + 1], v_f[:, q, :].rearrange("p (h c) -> p h c", h=H1),
                                            V[:, q, :, 0:KC], ALU.subtract).then_inc(s.v_lo_done, 1)
                if C:
                    pool.wait_ge(s.norm_aggr, i)
                    nc.gpsimd.tensor_tensor(var_eps[:], aggr[:, 1:2], env.eps[:], ALU.add).then_inc(s.norm_eps, 1)
                    pool.wait_ge(s.norm_eps, i)
                    nc.gpsimd.tensor_tensor(rstd[:], var_eps[:], env.minus_half[:], ALU.pow).then_inc(s.norm_rstd, 1)
                if Bs:
                    pool.wait_ge(s.exp_done, 2 * (i - 3))
                    nc.gpsimd.tensor_tensor(PT_lo[:, 1, :, :], PT[:, 1, :, :], PT_hi[:, 1, :, :], ALU.subtract) \
                        .then_inc(s.low_pool, 1)
                    if counted(i - 5):
                        pool.wait_ge(s.x_ready, i - 5)
                    nc.gpsimd.tensor_tensor(x_b[:, p, :], tile_of(X, i - 4), b_o[:], ALU.add).then_inc(s.x_bias, 1)
                if O:
                    pool.wait_ge(s.n2_aggr, i - 4)
                    nc.gpsimd.tensor_tensor(var_eps2[:], aggr2[:, 1:2], env.eps[:], ALU.add).then_inc(s.n2_eps, 1)
                    pool.wait_ge(s.n2_eps, i - 4)
                    nc.gpsimd.tensor_tensor(rstd2[:], var_eps2[:], env.minus_half[:], ALU.pow).then_inc(s.n2_rstd, 1)

            pool.wait_ge(s.w_in, env.n_w_in)
            pool.wait_ge(s.ones_set, 1)
            steady_loop(pool, step, 8, TILES, TILES + 7)
            for p in range(2):
                pool.wait_ge(s.scattered[p], 8 * TILES)


def finish(nc, env, stack):
    s = Names()
    (s.ready, s.added) = \
        (semaphore(nc, env, "f_" + n) for n in "ready added".split())
    s.gathered = [semaphore(nc, env, f"f_gathered{p}") for p in range(4)]
    s.stored = [semaphore(nc, env, f"f_stored{p}") for p in range(4)]
    y_at = stack.enter_context(nc.sbuf_tensor("f_y_at", [P, 4, 1], I32))
    y_w = stack.enter_context(nc.sbuf_tensor("f_y_w", [P, 4, 1], F32))
    y = stack.enter_context(nc.sbuf_tensor("f_y", [P, 4, P], F32))
    o = stack.enter_context(nc.sbuf_tensor("f_o", [P, 4, P], F32))
    out = env.io["out"].rearrange("(i p) d -> p i d", p=P)

    def steps(engine, step, lag):
        for i in range(8):
            step(i, i % 4)
        with engine.Fori(2, TILES // 4) as turn:
            for p in range(4):
                step(4 * turn + p, p)
        for i in range(TILES, TILES + lag):
            step(i, i % 4)

    with nc.Block() as block:
        @block.vector
        def _(dve):
            def step(i, p):
                if between(i, 0, TILES):
                    if counted(4 * (i - 4 - p) + 16):
                        dve.wait_ge(s.gathered[p], 4 * (i - 4 - p) + 16)
                    if not isinstance(i, int) or i >= 4:
                        dve.wait_ge(s.added, i - 3)
                    nc.vector.tensor_scalar(y_at[:, p, :], tile_of(env.Y_AT, i)[:, 0:1], 1.0, None, ALU.mult).then_inc(s.ready, 1)
                    nc.vector.tensor_scalar(y_w[:, p, :], tile_of(env.W1, i), 1.0, None, ALU.mult).then_inc(s.ready, 1)
                if between(i, 2, TILES + 2):
                    r = (p + 2) % 4
                    j = i - 2
                    dve.wait_ge(s.ready, 2 * (i - 1))
                    dve.wait_ge(s.gathered[r], 4 * (j - r) + 16)
                    if counted(4 * (j - 4 - r) + 16):
                        dve.wait_ge(s.stored[r], 4 * (j - 4 - r) + 16)
                    nc.vector.scalar_tensor_tensor(o[:, r, :], y[:, r, :], y_w[:, r, 0:1], tile_of(env.X, j), ALU.mult, ALU.add) \
                        .then_inc(s.added, 1)

            steps(dve, step, 2)

        @block.gpsimd
        def _(pool):
            def step(i, p):
                pool.wait_ge(s.ready, 2 * i + 2)
                if not isinstance(i, int) or i >= 4:
                    pool.wait_ge(s.added, i - 3)
                alone(pool)
                nc.gpsimd.indirect_dma_start(y[:, p, :], None, env.sorted_y1,
                                             bass.IndirectOffsetOnAxis(y_at[:, p, 0:1], 0)).then_inc(s.gathered[p], 16)

            steps(pool, step, 0)

        @block.sync
        def _(sp):
            def step(i, p):
                sp.wait_ge(s.added, i + 1)
                sp.dma_start(tile_of(out, i), o[:, p, :]).then_inc(s.stored[p], 16)

            steps(sp, step, 0)
            for p in range(4):
                sp.wait_ge(s.stored[p], 4 * TILES)


def build(nc, io, stop=None):
    env = Names()
    env.io = io
    env.X = nc.alloc_sbuf_tensor("X", [P, TILES, P], F32)
    env.bank = [nc.alloc_psum_tensor(f"bank{n}", [P, 512], F32) for n in range(8)]
    env.ident = nc.alloc_sbuf_tensor("ident", [P, P], F32)
    env.ident16 = nc.alloc_sbuf_tensor("ident16", [P, P], F16)
    env.tri16 = nc.alloc_sbuf_tensor("tri16", [P, P], F16)
    env.ones16 = nc.alloc_sbuf_tensor("ones16", [P, P], F16)
    env.region = nc.alloc_sbuf_tensor("region", [P, E], F32)
    env.iota2 = nc.alloc_sbuf_tensor("iota2", [P, 2, E], F32)
    env.prev = nc.alloc_sbuf_tensor("prev", [P, E], F16)
    env.eps = nc.alloc_sbuf_tensor("eps", [P, 1], F32)
    env.minus_half = nc.alloc_sbuf_tensor("minus_half", [P, 1], F32)
    env.TOP = nc.alloc_sbuf_tensor("TOP", [P, TILES, 2], F32)
    env.SEL = nc.alloc_sbuf_tensor("SEL", [P, TILES, 2 * E], F32)
    env.POS = nc.alloc_sbuf_tensor("POS", [P, TILES, 2], F32)
    env.sorted_x = nc.dram_tensor("sorted_x", (SPARE + P, P), F32, kind="Internal").ap()
    env.w_hi = nc.alloc_sbuf_tensor("w_hi", [P, W_COLUMNS, F], F16)
    env.w_lo = nc.alloc_sbuf_tensor("w_lo", [P, W_COLUMNS, F], F16)
    env.zeros = nc.alloc_sbuf_tensor("zeros", [P, P], F32)
    env.sorted_y0 = nc.dram_tensor("sorted_y0", (BLOCKS0 * P, P), F32, kind="Internal").ap()
    env.sorted_y1 = nc.dram_tensor("sorted_y1", (BLOCKS1 * P, P), F32, kind="Internal").ap()
    env.sel = nc.alloc_sbuf_tensor("sel", [P, 16, P], F16)
    env.k_bias_sb = nc.alloc_sbuf_tensor("k_bias", [P, 1], F32)
    env.block_row = nc.alloc_sbuf_tensor("block_row", [P, BLOCKS0], I32)
    env.block_expert = nc.alloc_sbuf_tensor("block_expert", [P, BLOCKS0], I32)
    env.Y_AT = nc.alloc_sbuf_tensor("Y_AT", [P, TILES, 2], F32)
    env.W = nc.alloc_sbuf_tensor("W", [P, TILES, 2], F32)
    env.W1 = nc.alloc_sbuf_tensor("W1", [P, TILES, 1], F32)
    phases = [lambda st: split_weights(nc, env, st),
              lambda st: attention0(nc, env, st),
              lambda st: plan(nc, env, st, "p0", 2, BLOCKS0, env.io["c_blocks0"]),
              lambda st: experts(nc, env, st, "e0", BLOCKS0, True, (G0, U0), D0, env.sorted_y0),
              lambda st: attention1(nc, env, st),
              lambda st: plan(nc, env, st, "p1", 1, BLOCKS1, env.io["c_blocks1"]),
              lambda st: experts(nc, env, st, "e1", BLOCKS1, False, (G1,), D1, env.sorted_y1),
              lambda st: finish(nc, env, st)]
    for phase in phases[:stop]:
        env.phase_semaphores = []
        with ExitStack() as stack:
            phase(stack)
        nc.all_engine_barrier()
        nc.clear_and_free_semaphores(env.phase_semaphores)
        nc.all_engine_barrier()
    return env


def block_diagonal(w):
    out = np.zeros((P, P), np.float32)
    out[:CH, :CH] = w
    out[CH:, CH:] = w
    return out


def head_rows(kind, batch, group, heads_per_group=4):
    hi, lo = np.zeros((P, P), np.float16), np.zeros((P, P), np.float16)
    for j in range(4):
        for r in range(ROW_MAX):
            third = r // KC
            is_lo = third == (2 if kind == "q" else 1)
            (lo if is_lo else hi)[64 * batch + (4 * group + j) * KC + r % KC, 32 * j + r] = 1
    return hi, lo


def constants():
    c = {}
    half = KC // 2
    theta = (1.0 / np.float32(1250) ** (np.arange(0, half, 2, dtype=np.float32) / np.float32(half))).astype(np.float32)
    ang = np.arange(D, dtype=np.float32)[None, :] * np.concatenate([theta, theta])[:, None]
    cos, sin = np.ones((KC, D), np.float32), np.zeros((KC, D), np.float32)
    cos[:half] = np.cos(ang)
    sin[:half] = np.sin(ang) * np.array([-1, -1, 1, 1], np.float32)[:, None]
    cos, sin = np.tile(cos, (P // KC, 1)), np.tile(sin, (P // KC, 1))
    scale = np.float32(KC ** -0.5)
    c["a0_rot"] = np.stack([np.stack([cos * scale, sin * scale], 1), np.stack([cos, sin], 1)], 1)
    c["c_sel"] = np.stack([m for kind in "qk" for b in range(2) for g in range(GROUPS0) for m in head_rows(kind, b, g)], 1)
    kb = np.zeros((P, 1), np.float32)
    kb[ROW_MAX::32] = -1
    c["c_k_bias"] = kb
    c["c_ident"] = np.eye(P, dtype=np.float32)
    c["c_ident16"] = np.eye(P, dtype=np.float16)
    c["c_tri16"] = np.triu(np.ones((P, P), np.float16), 1)
    c["c_region"] = np.tile(np.arange(E, dtype=np.float32) * REGION, (P, 1))
    for name, blocks in (("c_blocks0", BLOCKS0), ("c_blocks1", BLOCKS1)):
        c[name] = np.tile(np.arange(blocks, dtype=np.float32)[:, None], (P, 1, E))
    c["c_steps"] = np.tile(np.arange(TILES, dtype=np.float32) * P, (P, E, 1))
    c["c_before"] = np.tile(np.tril(np.ones((E, E), np.float32), -1), (P, 1, 1))
    c["c_iota2"] = np.tile(np.arange(E, dtype=np.float32), (P, 2, 1))
    return c


def layout(a):
    v = {"x": a["x"].reshape(-1, D), "ctx": a["ctx_1024"].reshape(-1, D)}
    partner = np.array([8 * h + c for h in range(H0) for c in (2, 3, 0, 1, 4, 5, 6, 7)])
    wq, wk = a["L0_xattn_Wq"], a["L0_xattn_Wk"]
    bq, bk = a["L0_xattn_bq"], a["L0_xattn_bk"]
    v["a0_w_qk"] = np.stack([block_diagonal(w.T) for w in (wq, wq[partner], wk, wk[partner])], 1)
    v["a0_b_qk"] = np.stack([np.tile(b, 2) for b in (bq, bq[partner], bk, bk[partner])], 1)
    v["a0_w_v"] = block_diagonal(a["L0_xattn_Wv"].T)
    v["a0_w_o"] = block_diagonal(a["L0_xattn_Wo"].T)
    v["a0_b_v"] = np.tile(a["L0_xattn_bv"], (P, 2))
    v["a0_b_o"] = np.tile(a["L0_xattn_bo"], 2)[:, None]
    v["f0_w_c"] = a["L0_ffn_conf_w"].T
    v["f0_b_c"] = np.tile(a["L0_ffn_conf_b"], (P, 1))
    v["f0_wealth"] = np.tile(a["L0_ffn_wealth"], (P, 1))
    by_feature = lambda w: w.reshape(E, F, D).transpose(2, 0, 1)
    by_hidden = lambda w: w.reshape(E, D, FC, P).transpose(3, 0, 2, 1).reshape(P, E, F)
    v["w_experts"] = np.concatenate([by_feature(a["L0_ffn_gate_w"]), by_feature(a["L0_ffn_up_w"]), by_hidden(a["L0_ffn_down_w"]),
                                     a["L1_ffn_w1"].transpose(1, 0, 2), by_hidden(a["L1_ffn_w2"].transpose(0, 2, 1))], 1)
    for n in "qkvo":
        v["a1_w_" + n] = a[f"L1_xattn_W{n}_w"].T
    v["a1_b_qk"] = np.stack([a["L1_xattn_Wq_b"], a["L1_xattn_Wk_b"]], 1)
    v["a1_b_v"] = np.tile(a["L1_xattn_Wv_b"], (P, 1))
    v["a1_b_o"] = np.tile(a["L1_xattn_Wo_b"], (P, 1))
    v["f1_w_g"] = a["L1_ffn_gate_w"]
    v["f1_b_g"] = np.tile(a["L1_ffn_gate_b"], (P, 1))
    v["f1_b_hidden"] = a["L1_ffn_b1"].reshape(E, FC, P).transpose(2, 0, 1)
    v["f1_b_out"] = np.tile(a["L1_ffn_b2"], (P, 1, 1))
    v.update(constants())
    return {k: np.ascontiguousarray(x) for k, x in v.items()}


def kernel(**inputs):
    import concourse.bacc as bacc
    from concourse.bass_utils import run_bass_kernel_spmd

    nc = bacc.Bacc("TRN2", target_bir_lowering=False, num_devices=1)
    arrays = layout({name: np.asarray(a) for name, a in inputs.items()})
    io = {name: nc.dram_tensor(name, a.shape, mybir.dt.from_np(a.dtype), kind="ExternalInput").ap() for name, a in arrays.items()}
    io["out"] = nc.dram_tensor("out", (B * CH, D), F32, kind="ExternalOutput").ap()
    build(nc, io)
    result = run_bass_kernel_spmd(nc, [arrays], core_ids=[0])
    return result.results[0]["out"].reshape(B, CH, D)
```

```python
from contextlib import ExitStack

import concourse.bass as bass
import numpy as np
from concourse import mybir

F32 = mybir.dt.float32
F16 = mybir.dt.float16
BF16 = mybir.dt.bfloat16
I32 = mybir.dt.int32
U32 = mybir.dt.uint32
ALU = mybir.AluOpType
ACT = mybir.ActivationFunctionType
AX_X = mybir.AxisListType.X
ds = bass.ds

P = 128
B, CH, D = 64, 64, 128
TILES = B * CH // P
EPS = 1e-5
E = 8
F = 512
FC = F // P
H0, KC = 8, 8
H1 = 16
GROUPS0 = H0 // 4
GROUPS1 = H1 // 4
PAIRS = [(8 * m + j, 8 * m + 4 + j) for j in range(4) for m in range(2)]
ROW_MAX = 3 * KC
UNROLL = 4
BLOCK = 2 * P
R = BLOCK // P
REGION = B * CH + BLOCK
SPARE = E * REGION
MOST = B * CH // BLOCK
BLOCKS0 = 2 * MOST + E
BLOCKS1 = MOST + E
GAP_STEP = 3
PADS_STEP = 2
G0, U0, D0, G1, D1 = 0, E, 2 * E, 3 * E, 4 * E
W_COLUMNS = 5 * E
SHARE = W_COLUMNS * F // TILES
W_SCALE = 64.0
X_SCALE = 64.0


def counted(n):
    return not isinstance(n, int) or n > 0


def alone(engine):
    engine.nop(nofuse=True)


def steady_loop(engine, step, first, end, last):
    for i in range(first):
        step(i, i % 2)
    with engine.Fori(first // UNROLL, end // UNROLL) as turn:
        for k in range(UNROLL):
            step(UNROLL * turn + k, k % 2)
    for i in range(end, last):
        step(i, i % 2)


def between(i, lo, hi):
    return not isinstance(i, int) or lo <= i < hi


class Names:
    pass


def semaphore(nc, env, name):
    sem = nc.alloc_semaphore(name)
    env.phase_semaphores.append(sem)
    return sem


def tile_of(t, i):
    return t[:, ds(i, 1), :].rearrange("p a n -> p (a n)")


def attention0(nc, env, stack):
    s = Names()
    (s.norm_stat, s.norm_aggr, s.norm_eps, s.norm_rstd, s.norm_done, s.proj_done, s.rope_mul, s.rope_sum,
     s.rope_done, s.rope_hi, s.rope_lo, s.v_mm, s.v_ready, s.v_hi_done, s.v_lo_done, s.low_dve, s.low_pool, s.k_mm,
     s.qa_mm, s.k_ready, s.qa_ready, s.s_mm, s.max_done, s.m_mm, s.qb_ready, s.st_mm, s.exp_done, s.pv_mm,
     s.sums_inv, s.heads_ready, s.ht_mm, s.ht_ready, s.out_mm, s.x_ready, s.n2_stat, s.n2_aggr, s.n2_eps, s.n2_rstd,
     s.n2_done, s.xt_mm, s.xt_ready, s.logit_mm, s.logit_b, s.gate_exp, s.gate_1p, s.gate_inv, s.bids_ready,
     s.top_val, s.top_idx, s.idx_f, s.sel_ready, s.selsum_ready, s.rank_mm, s.rank_read, s.pos_mul, s.pos_ready,
     s.idx_ready, s.prev_ready, s.x_in_first, s.x_in, s.w_in, s.tabs_t, s.tabs_done, s.ones_set, s.consts_set, s.w_hi_done, s.w_lo_done, s.pv_copied) = \
        (semaphore(nc, env, "a0_" + n) for n in """norm_stat norm_aggr norm_eps norm_rstd norm_done proj_done rope_mul rope_sum rope_done rope_hi
        rope_lo v_mm v_ready v_hi_done v_lo_done low_dve low_pool k_mm qa_mm k_ready qa_ready s_mm max_done
        m_mm qb_ready st_mm exp_done pv_mm sums_inv heads_ready ht_mm ht_ready out_mm x_ready n2_stat
        n2_aggr n2_eps n2_rstd n2_done xt_mm xt_ready logit_mm logit_b gate_exp gate_1p gate_inv bids_ready
        top_val top_idx idx_f sel_ready selsum_ready rank_mm rank_read pos_mul pos_ready idx_ready
        prev_ready x_in_first x_in w_in tabs_t tabs_done ones_set consts_set w_hi_done w_lo_done pv_copied""".split())
    s.ctx_in = [semaphore(nc, env, f"a0_ctx_in{p}") for p in range(2)]
    s.weights_in = [semaphore(nc, env, f"a0_weights_in{p}") for p in range(2)]
    s.scattered = [semaphore(nc, env, f"a0_scattered{p}") for p in range(2)]

    def sb(name, shape, dt=F32):
        return stack.enter_context(nc.sbuf_tensor("t0_" + name, shape, dt))

    X = env.X
    w_qk = sb("w_qk", [P, 4, P])
    w_v = sb("w_v", [P, P])
    w_o = sb("w_o", [P, P])
    rot = sb("rot", [P, 2, 2, P])
    b_qk = sb("b_qk", [P, 4])
    rot_b = sb("rot_b", [P, 2, P])
    b_tmp = sb("b_tmp", [P, 2, P])
    b_v = sb("b_v", [P, P])
    b_o = sb("b_o", [P, 1])
    sel, k_bias = env.sel, env.k_bias_sb
    w_c = sb("w_c", [P, E])
    b_c = sb("b_c", [P, E])
    wealth = sb("wealth", [P, E])
    ctx = sb("ctx", [P, 2, P])
    stat = sb("stat", [P, 6])
    aggr = sb("aggr", [P, 2])
    rstd = sb("rstd", [P, 1])
    var_eps = sb("var_eps", [P, 1])
    var_eps2 = sb("var_eps2", [P, 1])
    xn = sb("xn", [P, 2, P])
    rm = sb("rm", [P, 2, 2, P])
    rs = sb("rs", [P, 2, P])
    rf = sb("rf", [P, 2, P])
    r_hi = sb("r_hi", [P, 2, 2, P], F16)
    r_lo = sb("r_lo", [P, 2, 2, P], F16)
    Qa = sb("Qa", [P, 2, 4, P], F16)
    Qb = sb("Qb", [P, 2, 4, P], F16)
    Kt = sb("Kt", [P, 2, 4, P], F16)
    v_f = sb("v_f", [P, P])
    V = sb("V", [P, 2, 2, H0, 2 * KC + 1], F16)
    M = sb("M", [P, 4, P], F16)
    PT = sb("PT", [P, 4, 4, P])
    PT_hi = PT[:].bitcast(BF16).rearrange("p j n (t two) -> p j n t two", two=2)[:, :, :, :, 1]
    PT_lo = sb("PT_lo", [P, 4, 4, P], F16)
    inv = sb("inv", [P, 2 * H0])
    pv_s = sb("pv_s", [P, 2 * H0, 2 * KC + 1])
    sums = sb("sums", [P, 2 * H0, KC])
    heads = sb("heads", [P, P])
    hT = sb("hT", [P, P])
    stat2 = sb("stat2", [P, 6])
    aggr2 = sb("aggr2", [P, 2])
    rstd2 = sb("rstd2", [P, 1])
    xr = sb("xr", [P, 2, P])
    xT = sb("xT", [P, P])
    lb = sb("lb", [P, E])
    le = sb("le", [P, E])
    l1 = sb("l1", [P, E])
    li = sb("li", [P, E])
    bids = sb("bids", [P, E])
    top = sb("top", [P, E])
    topi = sb("topi", [P, E], U32)
    topf = sb("topf", [P, 2])
    selsum = sb("selsum", [P, E], F16)
    base = sb("base", [P, E])
    pm = sb("pm", [P, 2, E])
    idx = sb("idx", [P, 2, 2], I32)
    w_full = sb("w_full", [P, 2, SHARE])
    w_hi, w_lo = (w[:].rearrange("p c f -> p (c f)") for w in (env.w_hi, env.w_lo))

    work, q_bank, kv_bank = env.bank[0], env.bank[1], env.bank[2]
    s_bank, route_bank, st_bank, pv_bank = env.bank[3], env.bank[4], env.bank[5:7], env.bank[7]
    pv4 = pv_bank[:, 0:2 * H0 * (2 * KC + 1)].rearrange("p (h c) -> p h c", c=2 * KC + 1)

    def stages(i):
        return [between(i, lag, TILES + lag) for lag in range(5)]

    def least(count):
        return min(count, TILES) if isinstance(count, int) else count

    def loads(t, p):
        return 8 * (t - p) + 16

    def scatters(t, p):
        return 16 * (t - p)

    with nc.Block() as block:
        @block.sync
        def _(sp):
            x_dram = env.io["x"].rearrange("(i p) d -> p i d", p=P)
            c_dram = env.io["ctx"].rearrange("(i p) d -> p i d", p=P)
            sp.dma_start(X[:, 0:2, :], x_dram[:, 0:2, :]).then_inc(s.x_in_first, 16)
            sp.dma_start(ctx[:, 0, :], c_dram[:, 0, :]).then_inc(s.ctx_in[0], 16)
            loads = [(w_qk, env.io["a0_w_qk"]), (rot, env.io["a0_rot"]), (b_qk, env.io["a0_b_qk"]), (w_v, env.io["a0_w_v"]), (b_v, env.io["a0_b_v"]),
                     (sel, env.io["c_sel"]), (k_bias, env.io["c_k_bias"]), (w_o, env.io["a0_w_o"]), (b_o, env.io["a0_b_o"]), (w_c, env.io["f0_w_c"]),
                     (b_c, env.io["f0_b_c"]), (wealth, env.io["f0_wealth"]), (env.ident, env.io["c_ident"]), (env.ident16, env.io["c_ident16"]),
                     (env.tri16, env.io["c_tri16"]), (env.region, env.io["c_region"]), (env.iota2, env.io["c_iota2"])]
            for dst, src in loads:
                sp.dma_start(dst[:], src).then_inc(s.w_in, 16)
            sp.dma_start(ctx[:, 1, :], c_dram[:, 1, :]).then_inc(s.ctx_in[1], 16)
            sp.dma_start(X[:, 2:TILES, :], x_dram[:, 2:TILES, :]).then_inc(s.x_in, 16)
            env.n_w_in = 16 * len(loads)
            w_dram = env.io["w_experts"].rearrange("p c f -> p (c f)")
            for p in range(2):
                sp.dma_start(w_full[:, p, :], w_dram[:, p * SHARE:(p + 1) * SHARE]).then_inc(s.weights_in[p], 16)
            with sp.Fori(1, TILES // 2) as turn:
                for p in range(2):
                    i = 2 * turn
                    sp.wait_ge(s.v_mm, i + p - 1)
                    sp.dma_start(ctx[:, p, :], tile_of(c_dram, i + p)).then_inc(s.ctx_in[p], 16)
                    sp.wait_ge(s.w_lo_done, i + p - 1)
                    sp.dma_start(w_full[:, p, :], w_dram[:, ds(SHARE * (i + p), SHARE)]).then_inc(s.weights_in[p], 16)

        @block.tensor
        def _(pe):
            def project(t, p):
                pe.wait_ge(s.norm_done, t + 1)
                pe.wait_ge(s.ctx_in[p], loads(t, p))
                if counted(t - 3):
                    pe.wait_ge(s.x_ready, t - 3)
                for n in range(4):
                    rhs = xn[:, p, :] if n < 2 else ctx[:, p, :]
                    mm = nc.tensor.matmul(work[:, n * P:(n + 1) * P], w_qk[:, n, :], rhs, start=True, stop=True)
                mm.then_inc(s.proj_done, 1)

            def project_v(t, p):
                pe.wait_ge(s.k_ready, t + 1)
                if counted(t):
                    pe.wait_ge(s.qb_ready, t)
                nc.tensor.matmul(kv_bank[:, 0:P], ctx[:, p, :], w_v[:], start=True, stop=True).then_inc(s.v_mm, 1)

            def replicate_q(bank, p, start, stop):
                for n in range(4):
                    for part, r in enumerate((r_hi, r_lo)):
                        mm = nc.tensor.matmul(bank[:, n * P:(n + 1) * P], sel[:, 2 * n + part, :], r[:, p, 0, :],
                                              start=(n == 0 and part == 0), stop=stop and part == 1, skip_group_check=True)
                return mm

            def queries(t, p):
                pe.wait_ge(s.rope_hi, t + 1)
                pe.wait_ge(s.rope_lo, t + 1)
                if counted(t):
                    pe.wait_ge(s.qa_ready, t)
                replicate_q(q_bank, p, True, True).then_inc(s.qa_mm, 1)

            def keys(t, p):
                pe.wait_ge(s.rope_hi, t + 1)
                pe.wait_ge(s.rope_lo, t + 1)
                if counted(t):
                    pe.wait_ge(s.v_ready, t)
                if counted(t - 1):
                    pe.wait_ge(s.qb_ready, t - 1)
                for n in range(4):
                    for part, r in enumerate((r_hi, r_lo)):
                        mm = nc.tensor.matmul(kv_bank[:, n * P:(n + 1) * P], sel[:, 8 + 2 * n + part, :], r[:, p, 1, :],
                                              start=(n == 0 and part == 0), stop=(part == 1), skip_group_check=True)
                mm.then_inc(s.k_mm, 1)

            def scores(t, p, j):
                if j == 0:
                    pe.wait_ge(s.k_ready, t + 1)
                    pe.wait_ge(s.qa_ready, t + 1)
                if counted(4 * t + j):
                    pe.wait_ge(s.max_done, 4 * t + j)
                r = slice(32 * j, 32 * j + 32)
                for n in range(4):
                    mm = nc.tensor.matmul(s_bank[:, n * P:(n + 1) * P], Qa[r, p, n, :], Kt[r, p, n, :],
                                          start=True, stop=True)
                mm.then_inc(s.s_mm, 1)

            def queries_less_max(t, p):
                pe.wait_ge(s.max_done, 4 * t + 4)
                pe.wait_ge(s.k_ready, least(t + 2))
                pe.wait_ge(s.v_ready, t + 1)
                for n in range(4):
                    mm = nc.tensor.matmul(kv_bank[:, n * P:(n + 1) * P], M[:, n, :], env.ident16[:], start=True, stop=True)
                mm.then_inc(s.m_mm, 1)

            def scores_t(t, p, j):
                if j == 0:
                    pe.wait_ge(s.qb_ready, t + 1)
                if counted(4 * t + j - 1):
                    pe.wait_ge(s.exp_done, 4 * t + j - 1)
                r = slice(32 * j, 32 * j + 32)
                for n in range(4):
                    mm = nc.tensor.matmul(st_bank[j % 2][:, n * P:(n + 1) * P], Kt[r, p, n, :], Qb[r, p, n, :],
                                          start=True, stop=True)
                mm.then_inc(s.st_mm, 1)

            def values(t, p, j):
                if j % 2 == 0:
                    pe.wait_ge(s.low_dve, 2 * t + j // 2 + 1)
                else:
                    pe.wait_ge(s.low_pool, 2 * t + j // 2 + 1)
                if j == 0:
                    if counted(t):
                        pe.wait_ge(s.pv_copied, t)
                    pe.wait_ge(s.v_lo_done, t + 1)
                for n in range(4):
                    b, h = n // 2, 4 * (n % 2) + j
                    for part, w in enumerate((PT_hi, PT_lo)):
                        mm = nc.tensor.matmul(pv4[:, b * H0 + h, :], w[:, j, n, :], V[:, p, b, h, :],
                                              start=(part == 0), stop=(part == 1))
                mm.then_inc(s.pv_mm, 1)

            def step(i, p):
                A1, A2, Bs, O, R = stages(i)
                q = 1 - p
                if A1:
                    project(i, p)
                if A2:
                    scores(i - 1, q, 0)
                if Bs:
                    scores_t(i - 2, p, 0)
                if R:
                    pe.wait_ge(s.n2_done, i - 3)
                    if counted(i - 4):
                        pe.wait_ge(s.rank_read, i - 4)
                    nc.tensor.transpose(route_bank[:, 0:P], xr[:, p, :], env.ident[:]).then_inc(s.xt_mm, 1)
                if A2:
                    project_v(i - 1, q)
                if Bs:
                    scores_t(i - 2, p, 1)
                if R:
                    pe.wait_ge(s.xt_ready, i - 3)
                    nc.tensor.matmul(route_bank[:, 0:E], xT[:], w_c[:], start=True, stop=True).then_inc(s.logit_mm, 1)
                if O:
                    pe.wait_ge(s.heads_ready, i - 2)
                    pe.wait_ge(s.rope_mul, least(i + 1))
                    nc.tensor.transpose(work[:, 0:P], heads[:], env.ident[:]).then_inc(s.ht_mm, 1)
                if A2:
                    scores(i - 1, q, 1)
                if Bs:
                    values(i - 2, p, 0)
                if O:
                    pe.wait_ge(s.ht_ready, i - 2)
                    nc.tensor.matmul(work[:, 0:P], w_o[:], hT[:], start=True, stop=True).then_inc(s.out_mm, 1)
                if Bs:
                    scores_t(i - 2, p, 2)
                    values(i - 2, p, 1)
                if A2:
                    scores(i - 1, q, 2)
                if Bs:
                    scores_t(i - 2, p, 3)
                if A1:
                    keys(i, p)
                if Bs:
                    values(i - 2, p, 2)
                if A2:
                    scores(i - 1, q, 3)
                if A1:
                    queries(i, p)
                if Bs:
                    values(i - 2, p, 3)
                if A2:
                    queries_less_max(i - 1, q)
                if R:
                    pe.wait_ge(s.selsum_ready, i - 3)
                    if counted(i - 4):
                        pe.wait_ge(s.prev_ready, i - 4)
                    nc.tensor.matmul(route_bank[:, 0:E], env.tri16[:], selsum[:], start=True, stop=False)
                    nc.tensor.matmul(route_bank[:, 0:E], env.ones16[:], env.prev[:], start=False, stop=True) \
                        .then_inc(s.rank_mm, 1)

            pe.wait_ge(s.w_in, env.n_w_in)
            pe.wait_ge(s.ones_set, 4)
            steady_loop(pe, step, 8, TILES - 4, TILES + 4)

        @block.scalar
        def _(act):
            def exps(t, j):
                act.wait_ge(s.st_mm, 4 * t + j + 1)
                if counted(4 * t + j - 3):
                    act.wait_ge(s.pv_mm, 4 * t + j - 3)
                nc.scalar.activation(PT[:, j, :, :].rearrange("p n t -> p (n t)"), st_bank[j % 2][:], ACT.Exp) \
                    .then_inc(s.exp_done, 1)

            def step(i, p):
                A1, A2, Bs, O, R = stages(i)
                q = 1 - p
                if Bs:
                    exps(i - 2, 0)
                if R:
                    act.wait_ge(s.xt_mm, i - 3)
                    if counted(i - 4):
                        act.wait_ge(s.logit_mm, i - 4)
                    nc.scalar.copy(xT[:], route_bank[:, 0:P]).then_inc(s.xt_ready, 1)
                if Bs:
                    exps(i - 2, 1)
                if A1:
                    act.wait_ge(s.rope_done, i + 1)
                    if counted(i - 1):
                        act.wait_ge(s.qa_mm, i - 1)
                    nc.scalar.copy(r_hi[:, p, :, :], rf[:]).then_inc(s.rope_hi, 1)
                if O:
                    act.wait_ge(s.ht_mm, i - 2)
                    if counted(i - 3):
                        act.wait_ge(s.out_mm, i - 3)
                    nc.scalar.copy(hT[:], work[:, 0:P]).then_inc(s.ht_ready, 1)
                if A2:
                    act.wait_ge(s.v_ready, i)
                    nc.scalar.copy(V[:, q, :, :, 0:KC], v_f[:].rearrange("p (b h c) -> p b h c", b=2, h=H0)) \
                        .then_inc(s.v_hi_done, 1)
                if R:
                    act.wait_ge(s.logit_b, i - 3)
                    nc.scalar.activation(le[:], lb[:], ACT.Exp, scale=-1.0).then_inc(s.gate_exp, 1)
                if A1:
                    act.wait_ge(s.weights_in[p], loads(i, p))
                    nc.scalar.activation(w_hi[:, ds(SHARE * i, SHARE)], w_full[:, p, :], ACT.Copy, scale=W_SCALE) \
                        .then_inc(s.w_hi_done, 1)
                if Bs:
                    exps(i - 2, 2)
                if Bs:
                    exps(i - 2, 3)
                if A1:
                    act.wait_ge(s.k_mm, i + 1)
                    if counted(4 * i - 4):
                        act.wait_ge(s.st_mm, 4 * i - 4)
                    nc.scalar.activation(Kt[:, p, :, :].rearrange("p n t -> p (n t)"), kv_bank[:], ACT.Identity,
                                         bias=k_bias[:, 0:1]).then_inc(s.k_ready, 1)
                    act.wait_ge(s.qa_mm, i + 1)
                    if counted(4 * i - 4):
                        act.wait_ge(s.s_mm, 4 * i - 4)
                    if counted(i - 1):
                        act.wait_ge(s.qb_ready, i - 1)
                    nc.scalar.copy(Qa[:, p, :, :].rearrange("p n t -> p (n t)"), q_bank[:]).then_inc(s.qa_ready, 1)
                if Bs:
                    act.wait_ge(s.pv_mm, 4 * i - 4)
                    if counted(2 * i - 4):
                        act.wait_ge(s.sums_inv, 2 * i - 4)
                    nc.scalar.copy(pv_s[:].rearrange("p h c -> p (h c)"), pv_bank[:, 0:2 * H0 * (2 * KC + 1)]).then_inc(s.pv_copied, 1)

            act.wait_ge(s.w_in, env.n_w_in)
            act.wait_ge(s.ones_set, 4)
            steady_loop(act, step, 8, TILES - 4, TILES + 4)

        @block.vector
        def _(dve):
            def norm_stats(t):
                nc.vector.bn_stats(stat[:], tile_of(X, t)).then_inc(s.norm_stat, 1)
                dve.wait_ge(s.norm_stat, t + 1)
                alone(dve)
                nc.vector.bn_aggr(aggr[:], stat[:]).then_inc(s.norm_aggr, 1)

            def norm(t, p):
                dve.wait_ge(s.norm_rstd, t + 1)
                if counted(t - 1):
                    dve.wait_ge(s.proj_done, t - 1)
                nc.vector.tensor_scalar(xn[:, p, :], tile_of(X, t), aggr[:, 0:1], rstd[:, 0:1], ALU.subtract, ALU.mult) \
                    .then_inc(s.norm_done, 1)

            def rotate(t):
                dve.wait_ge(s.proj_done, t + 1)
                if counted(t):
                    dve.wait_ge(s.rope_sum, t)
                nc.vector.tensor_tensor(rm[:].rearrange("p a b t -> p (a b t)"), work[:],
                                        rot[:].rearrange("p a b t -> p (a b t)"), ALU.mult).then_inc(s.rope_mul, 1)

            def value_rows(t, p):
                dve.wait_ge(s.v_mm, t + 1)
                if counted(4 * t - 4):
                    dve.wait_ge(s.pv_mm, 4 * t - 4)
                if counted(t):
                    dve.wait_ge(s.v_lo_done, t)
                nc.vector.tensor_tensor(v_f[:], kv_bank[:, 0:P], b_v[:], ALU.add).then_inc(s.v_ready, 1)

            def value_lows(t, p):
                dve.wait_ge(s.v_hi_done, t + 1)
                nc.vector.tensor_tensor(V[:, p, :, :, KC + 1:2 * KC + 1], v_f[:].rearrange("p (b h c) -> p b h c", b=2, h=H0),
                                        V[:, p, :, :, 0:KC], ALU.subtract).then_inc(s.v_lo_done, 1)

            def weight_lows(t, j):
                dve.wait_ge(s.exp_done, 4 * t + j + 1)
                if counted(4 * t + j - 3):
                    dve.wait_ge(s.pv_mm, 4 * t + j - 3)
                nc.vector.tensor_tensor(PT_lo[:, j, :, :], PT[:, j, :, :], PT_hi[:, j, :, :], ALU.subtract) \
                    .then_inc(s.low_dve, 1)

            def maxima(t, j):
                dve.wait_ge(s.s_mm, 4 * t + j + 1)
                if j == 0:
                    if counted(t):
                        dve.wait_ge(s.m_mm, t)
                nc.vector.tensor_reduce(M[:, :, 32 * j + ROW_MAX:32 * j + ROW_MAX + 1],
                                        s_bank[:].rearrange("p (n t) -> p n t", n=4), AX_X, ALU.max) \
                    .then_inc(s.max_done, 1)

            def step(i, p):
                A1, A2, Bs, O, R = stages(i)
                q = 1 - p
                t = i - 4
                u = i - 3
                if R:
                    sel_t = tile_of(env.SEL, t).rearrange("p (k e) -> p k e", k=2)
                if A1:
                    rotate(i)
                if A2:
                    maxima(i - 1, 0)
                if O:
                    dve.wait_ge(s.pv_copied, i - 2)
                    nc.vector.reciprocal(inv[:], pv_s[:, :, KC]).then_inc(s.sums_inv, 1)
                    nc.vector.tensor_tensor(sums[:], pv_s[:, :, 0:KC], pv_s[:, :, KC + 1:2 * KC + 1], ALU.add).then_inc(s.sums_inv, 1)
                    dve.wait_ge(s.sums_inv, 2 * i - 4)
                    if counted(i - 3):
                        dve.wait_ge(s.ht_mm, i - 3)
                    nc.vector.tensor_tensor(heads[:].rearrange("p (h c) -> p h c", c=KC), sums[:],
                                            inv[:].unsqueeze(2).to_broadcast([P, 2 * H0, KC]), ALU.mult) \
                        .then_inc(s.heads_ready, 1)
                if Bs:
                    weight_lows(i - 2, 0)
                if R:
                    dve.wait_ge(s.logit_mm, t + 1)
                    nc.vector.tensor_tensor(lb[:], route_bank[:, 0:E], b_c[:], ALU.add).then_inc(s.logit_b, 1)
                if A2:
                    value_rows(i - 1, q)
                    maxima(i - 1, 1)
                if R:
                    dve.wait_ge(s.gate_exp, t + 1)
                    nc.vector.tensor_scalar(l1[:], le[:], 1.0, None, ALU.add).then_inc(s.gate_1p, 1)
                if A2:
                    value_lows(i - 1, q)
                if O:
                    dve.wait_ge(s.out_mm, u + 1)
                    nc.vector.scalar_tensor_tensor(tile_of(X, u), work[:, 0:P], b_o[:, 0:1], tile_of(X, u),
                                                   ALU.add, ALU.add).then_inc(s.x_ready, 1)
                if Bs:
                    weight_lows(i - 2, 2)
                if A2:
                    maxima(i - 1, 2)
                if R:
                    dve.wait_ge(s.gate_1p, t + 1)
                    nc.vector.reciprocal(li[:], l1[:]).then_inc(s.gate_inv, 1)
                if between(i, -1, TILES - 1):
                    dve.wait_ge(s.norm_done, i + 1)
                    if isinstance(i, int) and i == 1:
                        dve.wait_ge(s.x_in, 16)
                    alone(dve)
                    nc.vector.bn_stats(stat[:], tile_of(X, i + 1)).then_inc(s.norm_stat, 1)
                if R:
                    dve.wait_ge(s.gate_inv, t + 1)
                    nc.vector.tensor_tensor(bids[:], li[:], wealth[:], ALU.mult).then_inc(s.bids_ready, 1)
                if O:
                    dve.wait_ge(s.x_ready, u + 1)
                    alone(dve)
                    nc.vector.bn_stats(stat2[:], tile_of(X, u)).then_inc(s.n2_stat, 1)
                if between(i, -1, TILES - 1):
                    dve.wait_ge(s.norm_stat, i + 2)
                    alone(dve)
                    nc.vector.bn_aggr(aggr[:], stat[:]).then_inc(s.norm_aggr, 1)
                if R:
                    dve.wait_ge(s.bids_ready, t + 1)
                    alone(dve)
                    nc.vector.max(top[:], bids[:]).then_inc(s.top_val, 1)
                if O:
                    dve.wait_ge(s.n2_stat, u + 1)
                    alone(dve)
                    nc.vector.bn_aggr(aggr2[:], stat2[:]).then_inc(s.n2_aggr, 1)
                if A2:
                    maxima(i - 1, 3)
                if R:
                    dve.wait_ge(s.top_val, t + 1)
                    alone(dve)
                    nc.vector.max_index(topi[:], top[:], bids[:]).then_inc(s.top_idx, 1)
                    nc.vector.tensor_scalar(tile_of(env.TOP, t), top[:, 0:2], 1.0, None, ALU.mult)
                if R:
                    dve.wait_ge(s.top_idx, t + 1)
                    nc.vector.tensor_copy(topf[:], topi[:, 0:2]).then_inc(s.idx_f, 1)
                if between(i, -1, TILES - 1):
                    norm(i + 1, q)
                if R:
                    dve.wait_ge(s.idx_f, t + 1)
                    nc.vector.tensor_tensor(sel_t, env.iota2[:], topf[:].unsqueeze(2).to_broadcast([P, 2, E]), ALU.is_equal) \
                        .then_inc(s.sel_ready, 1)
                if O:
                    dve.wait_ge(s.n2_rstd, u + 1)
                    if counted(scatters(u, q)):
                        dve.wait_ge(s.scattered[q], scatters(u, q))
                    if counted(u - 1):
                        dve.wait_ge(s.xt_mm, u - 1)
                    nc.vector.tensor_scalar(xr[:, q, :], tile_of(X, u), aggr2[:, 0:1], rstd2[:, 0:1],
                                            ALU.subtract, ALU.mult).then_inc(s.n2_done, 1)
                if R:
                    dve.wait_ge(s.sel_ready, t + 1)
                    if counted(t):
                        dve.wait_ge(s.prev_ready, t)
                    nc.vector.tensor_tensor(selsum[:], sel_t[:, 0, :], sel_t[:, 1, :], ALU.add).then_inc(s.selsum_ready, 1)
                if A2:
                    dve.wait_ge(s.m_mm, i)
                    dve.wait_ge(s.qa_ready, i)
                    if counted(4 * i - 8):
                        dve.wait_ge(s.st_mm, 4 * i - 8)
                    nc.vector.tensor_tensor(Qb[:, q, :, :].rearrange("p n t -> p (n t)"), kv_bank[:],
                                            Qa[:, q, :, :].rearrange("p n t -> p (n t)"), ALU.add).then_inc(s.qb_ready, 1)
                if R:
                    dve.wait_ge(s.rank_mm, t + 1)
                    nc.vector.tensor_tensor(base[:], route_bank[:, 0:E], env.region[:], ALU.add).then_inc(s.rank_read, 1)
                    nc.vector.tensor_tensor(env.prev[:], env.prev[:], selsum[:], ALU.add).then_inc(s.prev_ready, 1)
                if R:
                    dve.wait_ge(s.rank_read, t + 1)
                    nc.vector.tensor_tensor(pm[:], sel_t, base[:].unsqueeze(1).to_broadcast([P, 2, E]), ALU.mult) \
                        .then_inc(s.pos_mul, 1)
                if R:
                    dve.wait_ge(s.pos_mul, t + 1)
                    nc.vector.tensor_reduce(tile_of(env.POS, t), pm[:], AX_X, ALU.add).then_inc(s.pos_ready, 1)
                    dve.wait_ge(s.pos_ready, t + 1)
                    if counted(scatters(t, p)):
                        dve.wait_ge(s.scattered[p], scatters(t, p))
                    nc.vector.tensor_scalar(idx[:, p, :], tile_of(env.POS, t), 1.0, None, ALU.mult).then_inc(s.idx_ready, 1)
                if A1:
                    dve.wait_ge(s.w_hi_done, i + 1)
                    nc.vector.scalar_tensor_tensor(w_lo[:, ds(SHARE * i, SHARE)], w_full[:, p, :], W_SCALE,
                                                   w_hi[:, ds(SHARE * i, SHARE)], ALU.mult, ALU.subtract).then_inc(s.w_lo_done, 1)

            nc.vector.memset(V[:], 1.0).then_inc(s.ones_set, 1)
            nc.vector.memset(M[:], 0.0).then_inc(s.ones_set, 1)
            nc.vector.memset(env.zeros[:], 0.0)
            nc.vector.memset(env.ones16[:], 1.0).then_inc(s.ones_set, 1)
            nc.vector.memset(env.prev[:], 0.0).then_inc(s.ones_set, 1)
            dve.wait_ge(s.x_in_first, 16)
            norm_stats(0)
            dve.wait_ge(s.w_in, env.n_w_in)
            for n in range(2):
                nc.vector.tensor_scalar(b_tmp[:, n, :], rot[:, n, 1, :], b_qk[:, 2 * n + 1:2 * n + 2], None, ALU.mult) \
                    .then_inc(s.tabs_t, 1)
            for n in range(2):
                dve.wait_ge(s.tabs_t, n + 1)
                nc.vector.scalar_tensor_tensor(rot_b[:, n, :], rot[:, n, 0, :], b_qk[:, 2 * n:2 * n + 1], b_tmp[:, n, :],
                                               ALU.mult, ALU.add).then_inc(s.tabs_done, 1)
            dve.wait_ge(s.ones_set, 4)
            norm(0, 0)
            steady_loop(dve, step, 8, TILES - 4, TILES + 4)

        @block.gpsimd
        def _(pool):
            nc.gpsimd.memset(env.eps[:], EPS).then_inc(s.consts_set, 1)
            nc.gpsimd.memset(env.minus_half[:], -0.5).then_inc(s.consts_set, 1)
            pool.wait_ge(s.consts_set, 2)

            def norm_scale(t):
                pool.wait_ge(s.norm_aggr, t + 1)
                nc.gpsimd.tensor_tensor(var_eps[:], aggr[:, 1:2], env.eps[:], ALU.add).then_inc(s.norm_eps, 1)
                pool.wait_ge(s.norm_eps, t + 1)
                nc.gpsimd.tensor_tensor(rstd[:], var_eps[:], env.minus_half[:], ALU.pow).then_inc(s.norm_rstd, 1)

            def step(i, p):
                A1, A2, Bs, O, R = stages(i)

                def weight_lows(t, j):
                    pool.wait_ge(s.exp_done, 4 * t + j + 1)
                    if counted(4 * t + j - 3):
                        pool.wait_ge(s.pv_mm, 4 * t + j - 3)
                    nc.gpsimd.tensor_tensor(PT_lo[:, j, :, :], PT[:, j, :, :], PT_hi[:, j, :, :], ALU.subtract) \
                        .then_inc(s.low_pool, 1)

                if between(i, 5, TILES + 5):
                    pool.wait_ge(s.idx_ready, i - 4)
                    alone(pool)
                    for k in range(2):
                        nc.gpsimd.indirect_dma_start(env.sorted_x, bass.IndirectOffsetOnAxis(idx[:, 1 - p, k:k + 1], 0),
                                                     xr[:, 1 - p, :], None).then_inc(s.scattered[1 - p], 16)
                if A1:
                    pool.wait_ge(s.rope_mul, i + 1)
                    nc.gpsimd.tensor_tensor(rs[:], rm[:, :, 0, :], rm[:, :, 1, :], ALU.add).then_inc(s.rope_sum, 1)
                    pool.wait_ge(s.rope_sum, i + 1)
                    if counted(i):
                        pool.wait_ge(s.rope_hi, i)
                        pool.wait_ge(s.rope_lo, i)
                    nc.gpsimd.tensor_tensor(rf[:], rs[:], rot_b[:], ALU.add).then_inc(s.rope_done, 1)
                if Bs:
                    weight_lows(i - 2, 1)
                if A1:
                    pool.wait_ge(s.rope_hi, i + 1)
                    if counted(i - 1):
                        pool.wait_ge(s.qa_mm, i - 1)
                    nc.gpsimd.tensor_tensor(r_lo[:, p, :, :], rf[:], r_hi[:, p, :, :], ALU.subtract).then_inc(s.rope_lo, 1)
                if Bs:
                    weight_lows(i - 2, 3)
                if between(i, -1, TILES - 1):
                    norm_scale(i + 1)
                if O:
                    pool.wait_ge(s.n2_aggr, i - 2)
                    nc.gpsimd.tensor_tensor(var_eps2[:], aggr2[:, 1:2], env.eps[:], ALU.add).then_inc(s.n2_eps, 1)
                    pool.wait_ge(s.n2_eps, i - 2)
                    nc.gpsimd.tensor_tensor(rstd2[:], var_eps2[:], env.minus_half[:], ALU.pow).then_inc(s.n2_rstd, 1)

            norm_scale(0)
            pool.wait_ge(s.tabs_done, 2)
            steady_loop(pool, step, 8, TILES - 4, TILES + 5)
            for p in range(2):
                pool.wait_ge(s.scattered[p], 16 * TILES)


def plan(nc, env, stack, name, slots, blocks, block_iota):
    s = Names()
    (s.iota_in, s.counted, s.step, s.pads_written, s.gap_exp) = \
        (semaphore(nc, env, f"{name}_{n}") for n in "iota_in counted step pads_written gap_exp".split())

    def sb(n, shape, dt=F32):
        return stack.enter_context(nc.sbuf_tensor(f"{name}_{n}", shape, dt))

    iota = sb("iota", [P, blocks, E])
    steps = sb("steps", [P, E, MOST])
    before = sb("before", [P, E, E])
    more = sb("more", [P, E, MOST])
    need = sb("need", [P, E])
    part = sb("part", [P, E, E])
    first = sb("first", [P, E])
    end = sb("end", [P, E])
    shift = sb("shift", [P, E])
    src_e = sb("src_e", [P, E])
    pad_f = sb("pad_f", [P, E])
    inside = sb("inside", [P, blocks, E])
    past = sb("past", [P, blocks, E])
    used = sb("used", [P, blocks])
    src = sb("src", [P, blocks])
    own = sb("own", [P, blocks])
    pads = sb("pads", [P, E], I32)
    gap = sb("gap", [P, TILES])
    total = sb("total", [P, TILES])
    shifts = sb("shifts", [P, TILES * slots, E])
    y_shift = sb("y_shift", [P, TILES * slots])
    counts = env.bank[0]

    with nc.Block() as block:
        @block.sync
        def _(sp):
            sp.dma_start(iota[:], block_iota).then_inc(s.iota_in, 16)
            sp.dma_start(steps[:], env.io["c_steps"]).then_inc(s.iota_in, 16)
            sp.dma_start(before[:], env.io["c_before"]).then_inc(s.iota_in, 16)
            sp.dma_start(env.sorted_x[SPARE:SPARE + BLOCK, :].rearrange("(r p) d -> p r d", p=P), env.zeros[:]).then_inc(s.pads_written, 16)
            sp.wait_ge(s.step, PADS_STEP)
            for e in range(E):
                row = sp.value_load(pads[0:1, e:e + 1], min_val=0, max_val=E * REGION - BLOCK)
                sp.dma_start(env.sorted_x[ds(row, BLOCK), :].rearrange("(r p) d -> p r d", p=P), env.zeros[:]).then_inc(s.pads_written, 16)
            sp.wait_ge(s.pads_written, 16 * (E + 1))

        if slots == 2:
            @block.scalar
            def _(act):
                act.wait_ge(s.step, GAP_STEP)
                nc.scalar.activation(gap[:], gap[:], ACT.Exp).then_inc(s.gap_exp, 1)

        @block.tensor
        def _(pe):
            nc.tensor.matmul(counts[:, 0:E], env.ones16[:], env.prev[:], start=True, stop=True).then_inc(s.counted, 1)

        @block.vector
        def _(dve):
            done = [0]

            def after(op):
                op.then_inc(s.step, 1)
                done[0] += 1
                dve.wait_ge(s.step, done[0])

            dve.wait_ge(s.counted, 1)
            dve.wait_ge(s.iota_in, 48)
            after(nc.vector.tensor_tensor(pad_f[:], counts[:, 0:E], env.region[:], ALU.add))
            after(nc.vector.tensor_scalar(pads[:], pad_f[:], 1.0, None, ALU.mult))
            assert done[0] == PADS_STEP
            if slots == 2:
                after(nc.vector.tensor_tensor(gap[:], env.TOP[:, :, 1], env.TOP[:, :, 0], ALU.subtract))
                assert done[0] == GAP_STEP
                dve.wait_ge(s.gap_exp, 1)
                after(nc.vector.tensor_scalar(total[:], gap[:], 1.0, None, ALU.add))
                after(nc.vector.reciprocal(env.W[:, :, 0], total[:]))
                after(nc.vector.tensor_tensor(env.W[:, :, 1], env.W[:, :, 0], gap[:], ALU.mult))
            after(nc.vector.tensor_tensor(more[:], counts[:, 0:E].unsqueeze(2).to_broadcast([P, E, MOST]), steps[:],
                                          ALU.is_gt))
            after(nc.vector.tensor_reduce(need[:], more[:], AX_X, ALU.add))
            after(nc.vector.tensor_tensor(part[:], before[:], need[:].unsqueeze(1).to_broadcast([P, E, E]), ALU.mult))
            after(nc.vector.tensor_reduce(first[:], part[:], AX_X, ALU.add))
            after(nc.vector.tensor_tensor(end[:], first[:], need[:], ALU.add))
            after(nc.vector.scalar_tensor_tensor(shift[:], first[:], -float(BLOCK), env.region[:], ALU.mult, ALU.add))
            after(nc.vector.tensor_scalar(src_e[:], shift[:], float(SPARE), None, ALU.subtract))
            after(nc.vector.tensor_tensor(inside[:], iota[:], first[:].unsqueeze(1).to_broadcast([P, blocks, E]), ALU.is_ge))
            after(nc.vector.tensor_tensor(past[:], iota[:], end[:].unsqueeze(1).to_broadcast([P, blocks, E]), ALU.is_ge))
            after(nc.vector.tensor_tensor(inside[:], inside[:], past[:], ALU.subtract))
            after(nc.vector.tensor_reduce(used[:], inside[:], AX_X, ALU.add))
            after(nc.vector.tensor_tensor(used[:], used[:], iota[:, :, 0], ALU.mult))
            after(nc.vector.tensor_tensor(past[:], inside[:], src_e[:].unsqueeze(1).to_broadcast([P, blocks, E]), ALU.mult))
            after(nc.vector.tensor_reduce(src[:], past[:], AX_X, ALU.add))
            after(nc.vector.scalar_tensor_tensor(src[:], used[:], float(BLOCK), src[:], ALU.mult, ALU.add))
            after(nc.vector.tensor_scalar(env.block_row[:, 0:blocks], src[:], float(SPARE), None, ALU.add))
            after(nc.vector.tensor_tensor(past[:], inside[:], env.iota2[:, 0:1, :].to_broadcast([P, blocks, E]), ALU.mult))
            after(nc.vector.tensor_reduce(own[:], past[:], AX_X, ALU.add))
            after(nc.vector.tensor_scalar(env.block_expert[:, 0:blocks], own[:], 1.0, None, ALU.mult))
            after(nc.vector.tensor_tensor(shifts[:], env.SEL[:, :, 0:slots * E].rearrange("p t (k e) -> p (t k) e", k=slots),
                                          shift[:].unsqueeze(1).to_broadcast([P, TILES * slots, E]), ALU.mult))
            after(nc.vector.tensor_reduce(y_shift[:], shifts[:], AX_X, ALU.add))
            after(nc.vector.tensor_tensor(env.Y_AT[:, :, 0:slots], env.POS[:, :, 0:slots], y_shift[:].rearrange("p (t k) -> p t k", k=slots),
                                          ALU.subtract))


def experts(nc, env, stack, name, blocks, gated, w_in, w_out, sorted_y):
    s = Names()
    (s.turned, s.x_hi_done, s.x_lo_done, s.hidden_mm, s.act_done, s.h_done, s.h_hi_done, s.h_lo_done, s.y_mm, s.y_ready,
     s.b_in) = (semaphore(nc, env, f"{name}_{n}") for n in """turned x_hi_done x_lo_done hidden_mm act_done h_done
     h_hi_done h_lo_done y_mm y_ready b_in""".split())
    s.x_in = [semaphore(nc, env, f"{name}_x_in{p}") for p in range(2)]
    s.y_out = [semaphore(nc, env, f"{name}_y_out{p}") for p in range(2)]

    def sb(n, shape, dt=F32):
        return stack.enter_context(nc.sbuf_tensor(f"{name}_{n}", shape, dt))

    x = sb("x", [P, 2, R, P])
    x_hi = sb("x_hi", [P, 2, BLOCK], F16)
    x_lo = sb("x_lo", [P, 2, BLOCK], F16)
    g = sb("g", [P, 2, 2 * BLOCK])
    h = sb("h", [P, 2, 2 * BLOCK])
    h_hi = sb("h_hi", [P, 2, 2, 2 * BLOCK], F16)
    h_lo = sb("h_lo", [P, 2, 2, 2 * BLOCK], F16)
    y = sb("y", [P, 2, R, P])
    if not gated:
        b_hidden = sb("b_hidden", [P, E * 2, FC // 2])
        b_out = sb("b_out", [P, E, P])
    x_bank, gate_bank, up_bank, y_bank = env.bank[0:2], env.bank[2:4], env.bank[4:6], env.bank[6:8]

    def transfers(t, p):
        return 8 * (t - p) + 16

    with nc.Block() as block:
        @block.sync
        def _(sp):
            y_rows = sorted_y.rearrange("(b r p) d -> p b r d", r=R, p=P)

            def step(i, p):
                if between(i, 0, blocks):
                    row = sp.value_load(env.block_row[0:1, ds(i, 1)], min_val=0, max_val=SPARE)
                    if counted(i - 1):
                        sp.wait_ge(s.turned, i - 1)
                    sp.dma_start(x[:, p, :, :], env.sorted_x[ds(row, BLOCK), :].rearrange("(r p) d -> p r d", p=P)) \
                        .then_inc(s.x_in[p], 16)
                if between(i, 4, blocks + 4):
                    sp.wait_ge(s.y_ready, i - 3)
                    sp.dma_start(y_rows[:, ds(i - 4, 1), :, :].rearrange("p b r d -> p (b r) d"), y[:, p, :, :]) \
                        .then_inc(s.y_out[p], 16)

            if not gated:
                sp.dma_start(b_hidden[:], env.io["f1_b_hidden"]).then_inc(s.b_in, 16)
                sp.dma_start(b_out[:], env.io["f1_b_out"]).then_inc(s.b_in, 16)
            steady_loop(sp, step, 4, blocks, blocks + 4)
            for p in range(2):
                sp.wait_ge(s.y_out[p], 8 * blocks)

        @block.tensor
        def _(pe):
            expert_of = [None]

            def hidden(half, e, xs):
                for w0, bank in zip(w_in, (gate_bank, up_bank)):
                    for n in range(2):
                        f = (2 * half + n) * P
                        for k in range(3):
                            w, rows = (env.w_hi, env.w_hi, env.w_lo)[k], (xs[0], xs[1], xs[0])[k]
                            mm = nc.tensor.matmul(bank[half][:, n * BLOCK:(n + 1) * BLOCK],
                                                  w[:, ds(e + w0, 1), f:f + P].rearrange("p a f -> p (a f)"), rows,
                                                  start=(k == 0), stop=(k == 2))
                    mm.then_inc(s.hidden_mm, 1)

            def step(i, p):
                q = 1 - p
                if between(i, 1, blocks + 1):
                    e_h = pe.value_load(env.block_expert[0:1, ds(i - 1, 1)], min_val=0, max_val=E - 1)
                if between(i, 0, blocks):
                    pe.wait_ge(s.x_in[p], transfers(i, p))
                    if counted(i - 1):
                        pe.wait_ge(s.x_lo_done, i - 1)
                    for r in range(R):
                        mm = nc.tensor.transpose(x_bank[p][:, r * P:(r + 1) * P], x[:, p, r, :], env.ident[:])
                    mm.then_inc(s.turned, 1)
                if between(i, 1, blocks + 1):
                    pe.wait_ge(s.x_hi_done, i)
                    pe.wait_ge(s.x_lo_done, i)
                    for half in range(2):
                        if counted(2 * i - 3 + half):
                            pe.wait_ge(s.h_done, 2 * i - 3 + half)
                        hidden(half, e_h, (x_hi[:, q, :], x_lo[:, q, :]))
                if between(i, 2, blocks + 2):
                    e_y = expert_of[0] if p else pe.value_load(env.block_expert[0:1, ds(i - 2, 1)], min_val=0, max_val=E - 1)
                    if counted(i - 3):
                        pe.wait_ge(s.y_ready, i - 3)
                    pe.wait_ge(s.h_hi_done, 2 * i - 2)
                    pe.wait_ge(s.h_lo_done, 2 * i - 2)
                    for n in range(FC):
                        for w, halves in ((env.w_hi, (h_hi, h_lo)), (env.w_lo, (h_hi,))):
                            for hk in halves:
                                for r in range(R):
                                    rows = (n % 2) * BLOCK + r * P
                                    mm = nc.tensor.matmul(y_bank[p][:, r * P:(r + 1) * P], hk[:, p, n // 2, rows:rows + P],
                                                          w[:, ds(e_y + w_out, 1), n * P:(n + 1) * P].rearrange("p a f -> p (a f)"),
                                                          start=(n == 0 and w is env.w_hi and hk is h_hi and r == 0),
                                                          stop=(n == FC - 1 and w is env.w_lo), skip_group_check=True)
                    mm.then_inc(s.y_mm, 1)
                if between(i, 1, blocks + 1):
                    expert_of[0] = e_h

            steady_loop(pe, step, 4, blocks, blocks + 2)

        @block.scalar
        def _(act):
            def step(i, p):
                q = 1 - p
                if between(i, 0, blocks):
                    act.wait_ge(s.turned, i + 1)
                    if counted((i - 1) * 2 * len(w_in)):
                        act.wait_ge(s.hidden_mm, (i - 1) * 2 * len(w_in))
                    nc.scalar.activation(x_hi[:, p, :], x_bank[p][:, 0:BLOCK], ACT.Copy, scale=X_SCALE).then_inc(s.x_hi_done, 1)
                if between(i, 1, blocks + 1):
                    for half in range(2):
                        t = 2 * i - 2 + half
                        if gated:
                            act.wait_ge(s.hidden_mm, 2 * t + 1)
                            if counted(t - 1):
                                act.wait_ge(s.h_done, t - 1)
                            nc.scalar.activation(g[:, half, :], gate_bank[half][:], ACT.Silu, scale=1 / (X_SCALE * W_SCALE)) \
                                .then_inc(s.act_done, 1)
                        else:
                            act.wait_ge(s.h_done, t + 1)
                            if counted(t - 1):
                                act.wait_ge(s.h_lo_done, t - 1)
                            nc.scalar.activation(h[:, half, :], g[:, half, :], ACT.Gelu).then_inc(s.act_done, 1)
                        act.wait_ge(s.h_done if gated else s.act_done, t + 1)
                        if counted(i - 2):
                            act.wait_ge(s.y_mm, i - 2)
                        nc.scalar.activation(h_hi[:, q, half, :], h[:, half, :], ACT.Copy, scale=1.0 if gated else W_SCALE) \
                            .then_inc(s.h_hi_done, 1)

            steady_loop(act, step, 4, blocks, blocks + 1)

        @block.vector
        def _(dve):
            expert_of = [None]

            def step(i, p):
                q = 1 - p
                if not gated and between(i, 1, blocks + 1):
                    alone(dve)
                    e_h = dve.value_load(env.block_expert[0:1, ds(i - 1, 1)], min_val=0, max_val=E - 1)
                if between(i, 0, blocks):
                    dve.wait_ge(s.x_hi_done, i + 1)
                    nc.vector.scalar_tensor_tensor(x_lo[:, p, :], x_bank[p][:, 0:BLOCK], X_SCALE, x_hi[:, p, :],
                                                   ALU.mult, ALU.subtract).then_inc(s.x_lo_done, 1)
                for half in range(2):
                    if between(i, 1, blocks + 1):
                        t = 2 * i - 2 + half
                        if gated:
                            dve.wait_ge(s.hidden_mm, 2 * t + 2)
                            dve.wait_ge(s.act_done, t + 1)
                            if counted(t - 1):
                                dve.wait_ge(s.h_hi_done, t - 1)
                                dve.wait_ge(s.h_lo_done, t - 1)
                            nc.vector.scalar_tensor_tensor(h[:, half, :], up_bank[half][:], 1 / X_SCALE, g[:, half, :],
                                                           ALU.mult, ALU.mult).then_inc(s.h_done, 1)
                        else:
                            dve.wait_ge(s.hidden_mm, t + 1)
                            if counted(t - 1):
                                dve.wait_ge(s.act_done, t - 1)
                            nc.vector.scalar_tensor_tensor(g[:, half, :].rearrange("p (n t) -> p n t", n=2),
                                                           gate_bank[half][:].rearrange("p (n t) -> p n t", n=2),
                                                           1 / (X_SCALE * W_SCALE),
                                                           b_hidden[:, ds(2 * e_h + half, 1), :].rearrange("p a n -> p (a n)")
                                                           .unsqueeze(2).to_broadcast([P, 2, BLOCK]), ALU.mult, ALU.add) \
                                .then_inc(s.h_done, 1)
                    if half == (0 if gated else 1) and between(i, 3, blocks + 3):
                        j = i - 3
                        dve.wait_ge(s.y_mm, i - 2)
                        if counted(transfers(j - 2, q)) and between(i, 5, blocks + 3):
                            dve.wait_ge(s.y_out[q], transfers(j - 2, q))
                        if gated:
                            nc.vector.tensor_scalar(y[:, q, :, :].rearrange("p r d -> p (r d)"), y_bank[q][:, 0:BLOCK],
                                                    1 / (W_SCALE * W_SCALE), None, ALU.mult).then_inc(s.y_ready, 1)
                        else:
                            alone(dve)
                            e_y = dve.value_load(env.block_expert[0:1, ds(j, 1)], min_val=0, max_val=E - 1)
                            nc.vector.scalar_tensor_tensor(y[:, q, :, :], y_bank[q][:, 0:BLOCK].rearrange("p (r d) -> p r d", r=R),
                                                           1 / (W_SCALE * W_SCALE), b_out[:, ds(e_y, 1), :].to_broadcast([P, R, P]),
                                                           ALU.mult, ALU.add).then_inc(s.y_ready, 1)
                if not gated and between(i, 1, blocks + 1):
                    for half in range(2):
                        dve.wait_ge(s.h_hi_done, 2 * i - 1 + half)
                        nc.vector.scalar_tensor_tensor(h_lo[:, q, half, :], h[:, half, :], W_SCALE, h_hi[:, q, half, :],
                                                       ALU.mult, ALU.subtract).then_inc(s.h_lo_done, 1)

            if not gated:
                dve.wait_ge(s.b_in, 32)
            steady_loop(dve, step, 8, blocks, blocks + 3)

        if gated:
            @block.gpsimd
            def _(pool):
                def step(i, p):
                    if between(i, 1, blocks + 1):
                        for half in range(2):
                            t = 2 * i - 2 + half
                            pool.wait_ge(s.h_hi_done, t + 1)
                            nc.gpsimd.tensor_tensor(h_lo[:, 1 - p, half, :], h[:, half, :], h_hi[:, 1 - p, half, :], ALU.subtract) \
                                .then_inc(s.h_lo_done, 1)

                steady_loop(pool, step, 4, blocks, blocks + 1)


def attention1(nc, env, stack):
    s = Names()
    (s.at_ready, s.w_ready, s.added_1, s.added_2, s.norm_stat, s.norm_aggr, s.norm_eps, s.norm_rstd, s.norm_done,
     s.turned, s.turned_copied, s.proj_done, s.q_hi, s.k_hi, s.q_lo, s.k_lo, s.v_ready, s.v_hi_done, s.v_lo_done,
     s.k_mm, s.q_mm, s.k_ready, s.qa_ready, s.s_mm, s.max_done, s.m_mm, s.qb_ready, s.st_mm, s.exp_done, s.low_dve,
     s.low_pool, s.pv_mm, s.sums_inv, s.heads_ready, s.x_bias, s.ht_mm, s.ht_ready, s.out_mm, s.x_ready,
     s.n2_stat, s.n2_aggr, s.n2_eps, s.n2_rstd, s.n2_done, s.xt_mm, s.xt_ready, s.logit_mm, s.logit_b, s.top_val,
     s.top_neg, s.top_idx, s.gate_exp, s.gate_sum, s.idx_f, s.sel_ready, s.sel_half, s.rank_mm, s.rank_read,
     s.prev_ready, s.pos_mul, s.pos_ready, s.idx_ready, s.w_in, s.scale_done, s.ones_set, s.pv_copied) = \
        (semaphore(nc, env, "a1_" + n) for n in """at_ready w_ready added_1 added_2 norm_stat norm_aggr norm_eps norm_rstd norm_done turned
        turned_copied proj_done q_hi k_hi q_lo k_lo v_ready v_hi_done v_lo_done k_mm q_mm k_ready qa_ready
        s_mm max_done m_mm qb_ready st_mm exp_done low_dve low_pool pv_mm sums_inv heads_ready
        x_bias ht_mm ht_ready out_mm x_ready n2_stat n2_aggr n2_eps n2_rstd n2_done xt_mm xt_ready logit_mm
        logit_b top_val top_neg top_idx gate_exp gate_sum idx_f sel_ready sel_half rank_mm rank_read
        prev_ready pos_mul pos_ready idx_ready w_in scale_done ones_set pv_copied""".split())
    s.ctx_in = [semaphore(nc, env, f"a1_ctx_in{p}") for p in range(2)]
    s.gathered = [semaphore(nc, env, f"a1_gathered{p}") for p in range(2)]
    s.scattered = [semaphore(nc, env, f"a1_scattered{p}") for p in range(2)]

    def sb(name, shape, dt=F32):
        return stack.enter_context(nc.sbuf_tensor("t1_" + name, shape, dt))

    X, sel, k_bias = env.X, env.sel, env.k_bias_sb
    w_q, w_k, w_v = (sb("w_" + n, [P, P]) for n in "qkv")
    w_o = sb("w_o", [CH, 2, P])
    b_qk = sb("b_qk", [P, 2])
    b_v, b_o = sb("b_v", [P, P]), sb("b_o", [P, P])
    w_g, b_g = sb("w_g", [P, E]), sb("b_g", [P, E])
    ctx = sb("ctx", [P, 2, P])
    y_at = sb("y_at", [P, 2, 2], I32)
    y_w = sb("y_w", [P, 2, 2])
    y = sb("y", [P, 2, 2, P])
    stat, aggr, rstd, var_eps = sb("stat", [P, 6]), sb("aggr", [P, 2]), sb("rstd", [P, 1]), sb("var_eps", [P, 1])
    stat2, aggr2, rstd2, var_eps2 = sb("stat2", [P, 6]), sb("aggr2", [P, 2]), sb("rstd2", [P, 1]), sb("var_eps2", [P, 1])
    xn = sb("xn", [P, 2, P])
    T = sb("T", [P, 2, P])
    r_hi = sb("r_hi", [P, 2, 2, P], F16)
    r_lo = sb("r_lo", [P, 2, 2, P], F16)
    Qa = sb("Qa", [P, 2, GROUPS1, P], F16)
    Qb = sb("Qb", [P, 2, GROUPS1, P], F16)
    Kt = sb("Kt", [P, 2, GROUPS1, P], F16)
    v_f = sb("v_f", [P, 2, P])
    V = sb("V", [P, 2, H1, 2, 2 * KC + 1], F16)
    M = sb("M", [P, GROUPS1, P], F16)
    PT = sb("PT", [P, 2, 8, CH])
    PT_hi = PT[:].bitcast(BF16).rearrange("p r n (t two) -> p r n t two", two=2)[:, :, :, :, 1]
    PT_lo = sb("PT_lo", [P, 2, 8, CH], F16)
    inv = sb("inv", [P, H1 // 2, 2])
    pv_s = sb("pv_s", [P, H1 // 2, 2, 2 * KC + 1])
    sums = sb("sums", [P, H1 // 2, 2, KC])
    heads = sb("heads", [P, 2, H1 // 2, KC])
    x_b = sb("x_b", [P, 2, P])
    hT = sb("hT", [CH, 2, 2, CH])
    xr = sb("xr", [P, 2, P])
    xT = sb("xT", [P, P])
    lb, le = sb("lb", [P, E]), sb("le", [P, E])
    top, topi, topf, topn = sb("top", [P, E]), sb("topi", [P, E], U32), sb("topf", [P, 1]), sb("topn", [P, 1])
    gate_sum = sb("gate_sum", [P, 1])
    sel16 = sb("sel16", [P, E], F16)
    base, pm = sb("base", [P, E]), sb("pm", [P, E])
    idx = sb("idx", [P, 2, 1], I32)

    work, q_bank, kv_bank = env.bank[0], env.bank[1], env.bank[2]
    s_bank, route_bank, st_bank, pv_bank = env.bank[3], env.bank[4], env.bank[5:7], env.bank[7]
    pv = pv_bank[:, 0:8 * 2 * (2 * KC + 1)].rearrange("p (m h b c) -> p m h b c", m=4, h=2, b=2)

    def stages(i):
        return [between(i, lag, TILES + lag) for lag in range(8)]

    def loads(t, p):
        return 8 * (t - p) + 16

    with nc.Block() as block:
        @block.sync
        def _(sp):
            c_dram = env.io["ctx"].rearrange("(i p) d -> p i d", p=P)
            weights = [(w_q, env.io["a1_w_q"]), (w_k, env.io["a1_w_k"]), (w_v, env.io["a1_w_v"]), (w_o, env.io["a1_w_o"]), (b_qk, env.io["a1_b_qk"]),
                       (b_v, env.io["a1_b_v"]), (b_o, env.io["a1_b_o"]), (w_g, env.io["f1_w_g"]), (b_g, env.io["f1_b_g"])]
            env.n_w_in = 16 * len(weights)
            for dst, src in weights:
                sp.dma_start(dst[:], src).then_inc(s.w_in, 16)
            for p in range(2):
                sp.dma_start(ctx[:, p, :], c_dram[:, p, :]).then_inc(s.ctx_in[p], 16)
            with sp.Fori(1, TILES // 2) as turn:
                for p in range(2):
                    i = 2 * turn
                    sp.wait_ge(s.turned, i + p - 1)
                    sp.dma_start(ctx[:, p, :], tile_of(c_dram, i + p)).then_inc(s.ctx_in[p], 16)

        @block.tensor
        def _(pe):
            def turn_rows(t, p):
                pe.wait_ge(s.norm_done, t + 1)
                pe.wait_ge(s.ctx_in[p], loads(t, p))
                if counted(t):
                    pe.wait_ge(s.q_lo, t)
                if counted(t):
                    pe.wait_ge(s.k_lo, t)
                if counted(t):
                    pe.wait_ge(s.v_ready, t)
                nc.tensor.transpose(work[:, 0:P], xn[:, p, :], env.ident[:])
                nc.tensor.transpose(work[:, P:2 * P], ctx[:, p, :], env.ident[:]).then_inc(s.turned, 1)

            def project(t, p):
                pe.wait_ge(s.turned_copied, t + 1)
                nc.tensor.matmul(work[:, 2 * P:3 * P], w_q[:], T[:, 0, :], start=True, stop=True)
                nc.tensor.matmul(work[:, 3 * P:4 * P], w_k[:], T[:, 1, :], start=True, stop=True)
                nc.tensor.matmul(work[:, 0:P], T[:, 1, :], w_v[:], start=True, stop=True).then_inc(s.proj_done, 1)

            def replicate(bank, p, kind, stop):
                for n in range(GROUPS1):
                    for part, r in enumerate((r_hi, r_lo)):
                        mm = nc.tensor.matmul(bank[:, n * P:(n + 1) * P], sel[:, 8 * kind + 2 * n + part, :], r[:, p, kind, :],
                                              start=(n == 0 and part == 0), stop=stop and part == 1, skip_group_check=True)
                return mm

            def keys(t, p):
                pe.wait_ge(s.k_hi, t + 1)
                pe.wait_ge(s.k_lo, t + 1)
                if counted(t - 1):
                    pe.wait_ge(s.qb_ready, t - 1)
                replicate(kv_bank, p, 1, True).then_inc(s.k_mm, 1)

            def queries(t, p):
                pe.wait_ge(s.q_hi, t + 1)
                pe.wait_ge(s.q_lo, t + 1)
                if counted(t):
                    pe.wait_ge(s.qa_ready, t)
                if counted(t - 2):
                    pe.wait_ge(s.x_ready, t - 2)
                replicate(q_bank, p, 0, True).then_inc(s.q_mm, 1)

            def head_products(bank, at, left, right, p, j):
                rows = slice(32 * j, 32 * j + 32)
                for n in range(GROUPS1):
                    for b in range(2):
                        c = slice(b * CH, b * CH + CH)
                        mm = nc.tensor.matmul(bank[c, at + n * CH:at + (n + 1) * CH], left[rows, p, n, c], right[rows, p, n, c],
                                              start=True, stop=True)
                return mm

            def scores(t, p, j):
                if j == 0:
                    pe.wait_ge(s.k_ready, t + 1)
                    pe.wait_ge(s.qa_ready, t + 1)
                if j % 2 == 0:
                    if counted(2 * t + j // 2):
                        pe.wait_ge(s.max_done, 2 * t + j // 2)
                else:
                    pe.wait_ge(s.s_mm, 4 * t + j)
                alone(pe)
                head_products(s_bank, 4 * CH * (j % 2), Qa, Kt, p, j).then_inc(s.s_mm, 1)

            def queries_less_max(t, p):
                pe.wait_ge(s.max_done, 2 * t + 2)
                pe.wait_ge(s.k_ready, min(t + 2, TILES) if isinstance(t, int) else t + 2)
                for n in range(GROUPS1):
                    mm = nc.tensor.matmul(kv_bank[:, n * P:(n + 1) * P], M[:, n, :], env.ident16[:], start=True, stop=True)
                mm.then_inc(s.m_mm, 1)

            def scores_t(t, p, j):
                if j == 0:
                    pe.wait_ge(s.qb_ready, t + 1)
                if j % 2 == 0:
                    if counted(2 * t + j // 2 - 1):
                        pe.wait_ge(s.exp_done, 2 * t + j // 2 - 1)
                else:
                    pe.wait_ge(s.st_mm, 4 * t + j)
                alone(pe)
                head_products(st_bank[j // 2], 4 * CH * (j % 2), Kt, Qb, p, j).then_inc(s.st_mm, 1)

            def values(t, p, r):
                if r == 0:
                    pe.wait_ge(s.low_dve, t + 1)
                    pe.wait_ge(s.v_lo_done, t + 1)
                else:
                    pe.wait_ge(s.low_pool, t + 1)
                if counted(2 * t + r):
                    pe.wait_ge(s.pv_copied, 2 * t + r)
                alone(pe)
                for m in range(4):
                    for part, w in enumerate((PT_hi, PT_lo)):
                        mm = nc.tensor.matmul(pv[:, m, :, :, :].rearrange("p h b c -> p (h b c)"), w[:, r, 2 * m:2 * m + 2, :],
                                              V[:, p, 8 * r + 2 * m:8 * r + 2 * m + 2, :, :].rearrange("p h b c -> p (h b c)"),
                                              start=(part == 0), stop=(part == 1))
                mm.then_inc(s.pv_mm, 1)

            def step(i, p):
                G, C, A1, A2, Bs, O, R, S = stages(i)
                q = 1 - p
                if A1:
                    turn_rows(i - 2, p)
                if A2:
                    scores(i - 3, q, 0)
                if Bs:
                    scores_t(i - 4, p, 0)
                if A2:
                    scores(i - 3, q, 1)
                if Bs:
                    scores_t(i - 4, p, 1)
                if R:
                    pe.wait_ge(s.n2_done, i - 5)
                    if counted(i - 6):
                        pe.wait_ge(s.rank_read, i - 6)
                    nc.tensor.transpose(route_bank[:, 0:P], xr[:, p, :], env.ident[:]).then_inc(s.xt_mm, 1)
                if A1:
                    project(i - 2, p)
                if Bs:
                    scores_t(i - 4, p, 2)
                if A2:
                    scores(i - 3, q, 2)
                if Bs:
                    scores_t(i - 4, p, 3)
                if A2:
                    scores(i - 3, q, 3)
                if R:
                    pe.wait_ge(s.xt_ready, i - 5)
                    nc.tensor.matmul(route_bank[:, 0:E], xT[:], w_g[:], start=True, stop=True).then_inc(s.logit_mm, 1)
                if Bs:
                    values(i - 4, p, 0)
                if O:
                    pe.wait_ge(s.heads_ready, i - 4)
                    pe.wait_ge(s.qa_ready, min(i - 2, TILES) if isinstance(i, int) else i - 2)
                    alone(pe)
                    for b in range(2):
                        mm = nc.tensor.transpose(q_bank[0:CH, b * P:(b + 1) * P], heads[:, b, :, :].rearrange("p m c -> p (m c)"),
                                                 env.ident[:])
                    mm.then_inc(s.ht_mm, 1)
                if A1:
                    keys(i - 2, p)
                if O:
                    pe.wait_ge(s.ht_ready, i - 4)
                    for half in range(2):
                        mm = nc.tensor.matmul(q_bank[:, 0:P], hT[:, half, :, :].rearrange("p b t -> p (b t)"), w_o[:, half, :],
                                              start=(half == 0), stop=(half == 1))
                    mm.then_inc(s.out_mm, 1)
                if Bs:
                    values(i - 4, p, 1)
                if A1:
                    queries(i - 2, p)
                if A2:
                    queries_less_max(i - 3, q)
                if R:
                    pe.wait_ge(s.sel_half, i - 5)
                    if counted(i - 6):
                        pe.wait_ge(s.prev_ready, i - 6)
                    nc.tensor.matmul(route_bank[:, 0:E], env.tri16[:], sel16[:], start=True, stop=False)
                    nc.tensor.matmul(route_bank[:, 0:E], env.ones16[:], env.prev[:], start=False, stop=True) \
                        .then_inc(s.rank_mm, 1)

            pe.wait_ge(s.w_in, env.n_w_in)
            pe.wait_ge(s.scale_done, 1)
            pe.wait_ge(s.ones_set, 5)
            steady_loop(pe, step, 8, TILES, TILES + 7)

        @block.scalar
        def _(act):
            def exps(t, r):
                act.wait_ge(s.st_mm, 4 * t + 2 * r + 2)
                if counted(2 * t + r - 1):
                    act.wait_ge(s.pv_mm, 2 * t + r - 1)
                nc.scalar.activation(PT[:, r, :, :].rearrange("p n t -> p (n t)"), st_bank[r][:], ACT.Exp) \
                    .then_inc(s.exp_done, 1)

            def sums_out(t, r):
                act.wait_ge(s.pv_mm, 2 * t + r + 1)
                if counted(2 * t):
                    act.wait_ge(s.sums_inv, 2 * t)
                for h, rows in enumerate((slice(0, CH), slice(CH, P))):
                    out = nc.scalar.copy(pv_s[rows, 4 * r:4 * r + 4, :, :].rearrange("p m b c -> p m (b c)"),
                                         pv[rows, :, h, :, :].rearrange("p m b c -> p m (b c)"))
                out.then_inc(s.pv_copied, 1)

            def step(i, p):
                G, C, A1, A2, Bs, O, R, S = stages(i)
                q = 1 - p
                if A1:
                    act.wait_ge(s.turned, i - 1)
                    if counted(i - 2):
                        act.wait_ge(s.proj_done, i - 2)
                    nc.scalar.copy(T[:].rearrange("p a t -> p (a t)"), work[:, 0:2 * P]).then_inc(s.turned_copied, 1)
                if Bs:
                    exps(i - 4, 0)
                if R:
                    act.wait_ge(s.xt_mm, i - 5)
                    if counted(i - 6):
                        act.wait_ge(s.logit_mm, i - 6)
                    nc.scalar.copy(xT[:], route_bank[:, 0:P]).then_inc(s.xt_ready, 1)
                if A2:
                    act.wait_ge(s.v_ready, i - 2)
                    if counted(2 * (i - 4)):
                        act.wait_ge(s.pv_mm, 2 * (i - 4))
                    for b, keys in enumerate((slice(0, CH), slice(CH, P))):
                        nc.scalar.copy(V[keys, q, :, b, 0:KC], v_f[keys, q, :].rearrange("p (h c) -> p h c", h=H1)) \
                            .then_inc(s.v_hi_done, 1)
                if A1:
                    act.wait_ge(s.proj_done, i - 1)
                    if counted(i - 3):
                        act.wait_ge(s.q_mm, i - 3)
                    for n, done in enumerate((s.q_hi, s.k_hi)):
                        nc.scalar.activation(r_hi[:, p, n, :], work[:, (2 + n) * P:(3 + n) * P], ACT.Identity,
                                             bias=b_qk[:, n:n + 1]).then_inc(done, 1)
                if Bs:
                    exps(i - 4, 1)
                if O:
                    act.wait_ge(s.ht_mm, i - 4)
                    if counted(i - 5):
                        act.wait_ge(s.out_mm, i - 5)
                    nc.scalar.copy(hT[:], q_bank[0:CH, 0:2 * P].rearrange("p (b h t) -> p h b t", b=2, h=2)).then_inc(s.ht_ready, 1)
                if Bs:
                    sums_out(i - 4, 0)
                if R:
                    act.wait_ge(s.top_neg, i - 5)
                    if counted(i - 6):
                        act.wait_ge(s.gate_sum, i - 6)
                    nc.scalar.activation(le[:], lb[:], ACT.Exp, bias=topn[:, 0:1]).then_inc(s.gate_exp, 1)
                if A1:
                    act.wait_ge(s.k_mm, i - 1)
                    if counted(4 * (i - 3)):
                        act.wait_ge(s.st_mm, 4 * (i - 3))
                    nc.scalar.activation(Kt[:, p, :, :].rearrange("p n t -> p (n t)"), kv_bank[:], ACT.Identity,
                                         bias=k_bias[:, 0:1]).then_inc(s.k_ready, 1)
                if Bs:
                    sums_out(i - 4, 1)
                if A1:
                    act.wait_ge(s.q_mm, i - 1)
                    if counted(4 * (i - 3)):
                        act.wait_ge(s.s_mm, 4 * (i - 3))
                    if counted(i - 3):
                        act.wait_ge(s.qb_ready, i - 3)
                    nc.scalar.copy(Qa[:, p, :, :].rearrange("p n t -> p (n t)"), q_bank[:]).then_inc(s.qa_ready, 1)

            act.wait_ge(s.w_in, env.n_w_in)
            act.wait_ge(s.scale_done, 2)
            act.wait_ge(s.ones_set, 5)
            steady_loop(act, step, 8, TILES, TILES + 7)

        @block.vector
        def _(dve):
            def maxima(t, r):
                dve.wait_ge(s.s_mm, 4 * t + 2 * r + 2)
                if r == 0:
                    if counted(t):
                        dve.wait_ge(s.m_mm, t)
                rows = M[:].rearrange("p n (j r) -> p j n r", r=32)[:, 2 * r:2 * r + 2, :, ROW_MAX:ROW_MAX + 1]
                nc.vector.tensor_reduce(rows, s_bank[:].rearrange("p (j n t) -> p j n t", j=2, n=GROUPS1), AX_X, ALU.max) \
                    .then_inc(s.max_done, 1)

            def step(i, p):
                G, C, A1, A2, Bs, O, R, S = stages(i)
                q = 1 - p
                t = i - 6
                u = i - 5
                if G:
                    if counted(loads(i - 2, p)) and between(i, 2, TILES):
                        dve.wait_ge(s.gathered[p], 2 * loads(i - 2, p))
                    nc.vector.tensor_scalar(y_at[:, p, :], tile_of(env.Y_AT, i), 1.0, None, ALU.mult).then_inc(s.at_ready, 1)
                if A2:
                    maxima(i - 3, 0)
                if C:
                    if counted(i - 1):
                        dve.wait_ge(s.added_2, i - 1)
                    nc.vector.tensor_scalar(y_w[:, q, :], tile_of(env.W, i - 1), 1.0, None, ALU.mult).then_inc(s.w_ready, 1)
                    dve.wait_ge(s.w_ready, i)
                    dve.wait_ge(s.gathered[q], 2 * loads(i - 1, q))
                    nc.vector.scalar_tensor_tensor(tile_of(X, i - 1), y[:, q, 0, :], y_w[:, q, 0:1], tile_of(X, i - 1),
                                                   ALU.mult, ALU.add).then_inc(s.added_1, 1)
                if Bs:
                    dve.wait_ge(s.exp_done, 2 * (i - 4) + 1)
                    if counted(2 * (i - 4) - 1):
                        dve.wait_ge(s.pv_mm, 2 * (i - 4) - 1)
                    nc.vector.tensor_tensor(PT_lo[:, 0, :, :], PT[:, 0, :, :], PT_hi[:, 0, :, :], ALU.subtract) \
                        .then_inc(s.low_dve, 1)
                if C:
                    dve.wait_ge(s.added_1, i)
                    nc.vector.scalar_tensor_tensor(tile_of(X, i - 1), y[:, q, 1, :], y_w[:, q, 1:2], tile_of(X, i - 1),
                                                   ALU.mult, ALU.add).then_inc(s.added_2, 1)
                if A2:
                    dve.wait_ge(s.v_hi_done, 2 * (i - 2))
                    for b, keys in enumerate((slice(0, CH), slice(CH, P))):
                        low = nc.vector.tensor_tensor(V[keys, q, :, b, KC + 1:2 * KC + 1],
                                                      v_f[keys, q, :].rearrange("p (h c) -> p h c", h=H1),
                                                      V[keys, q, :, b, 0:KC], ALU.subtract)
                    low.then_inc(s.v_lo_done, 1)
                if A1:
                    dve.wait_ge(s.k_hi, i - 1)
                    for n, lo in enumerate((s.q_lo, s.k_lo)):
                        nc.vector.scalar_tensor_tensor(r_lo[:, p, n, :], work[:, (2 + n) * P:(3 + n) * P], b_qk[:, n:n + 1],
                                                       r_hi[:, p, n, :], ALU.add, ALU.subtract).then_inc(lo, 1)
                    if counted(i - 3):
                        dve.wait_ge(s.v_lo_done, i - 3)
                    nc.vector.tensor_tensor(v_f[:, p, :], work[:, 0:P], b_v[:], ALU.add).then_inc(s.v_ready, 1)
                if C:
                    dve.wait_ge(s.added_2, i)
                    if counted(i - 1):
                        dve.wait_ge(s.norm_aggr, i - 1)
                    alone(dve)
                    nc.vector.bn_stats(stat[:], tile_of(X, i - 1)).then_inc(s.norm_stat, 1)
                if R:
                    dve.wait_ge(s.logit_mm, t + 1)
                    nc.vector.tensor_tensor(lb[:], route_bank[:, 0:E], b_g[:], ALU.add).then_inc(s.logit_b, 1)
                if C:
                    dve.wait_ge(s.norm_stat, i)
                    if counted(i - 1):
                        dve.wait_ge(s.norm_done, i - 1)
                    alone(dve)
                    nc.vector.bn_aggr(aggr[:], stat[:]).then_inc(s.norm_aggr, 1)
                if R:
                    dve.wait_ge(s.logit_b, t + 1)
                    alone(dve)
                    nc.vector.max(top[:], lb[:]).then_inc(s.top_val, 1)
                if A2:
                    maxima(i - 3, 1)
                if R:
                    dve.wait_ge(s.top_val, t + 1)
                    nc.vector.tensor_scalar(topn[:], top[:, 0:1], -1.0, None, ALU.mult).then_inc(s.top_neg, 1)
                    alone(dve)
                    nc.vector.max_index(topi[:], top[:], lb[:]).then_inc(s.top_idx, 1)
                if C:
                    dve.wait_ge(s.norm_rstd, i)
                    if counted(i - 3):
                        dve.wait_ge(s.turned, i - 3)
                    nc.vector.tensor_scalar(xn[:, q, :], tile_of(X, i - 1), aggr[:, 0:1], rstd[:, 0:1], ALU.subtract, ALU.mult) \
                        .then_inc(s.norm_done, 1)
                if R:
                    dve.wait_ge(s.top_idx, t + 1)
                    nc.vector.tensor_copy(topf[:], topi[:, 0:1]).then_inc(s.idx_f, 1)
                    dve.wait_ge(s.idx_f, t + 1)
                    nc.vector.tensor_scalar(tile_of(env.SEL, t)[:, 0:E], env.iota2[:, 0, :], topf[:, 0:1], None, ALU.is_equal) \
                        .then_inc(s.sel_ready, 1)
                    dve.wait_ge(s.sel_ready, t + 1)
                    if counted(t):
                        dve.wait_ge(s.prev_ready, t)
                    nc.vector.tensor_scalar(sel16[:], tile_of(env.SEL, t)[:, 0:E], 1.0, None, ALU.mult).then_inc(s.sel_half, 1)
                    dve.wait_ge(s.gate_exp, t + 1)
                    nc.vector.tensor_reduce(gate_sum[:], le[:], AX_X, ALU.add).then_inc(s.gate_sum, 1)
                if O:
                    dve.wait_ge(s.out_mm, u + 1)
                    dve.wait_ge(s.x_bias, u + 1)
                    nc.vector.tensor_tensor(tile_of(X, u), q_bank[:, 0:P], x_b[:, q, :], ALU.add).then_inc(s.x_ready, 1)
                if R:
                    dve.wait_ge(s.gate_sum, t + 1)
                    nc.vector.reciprocal(tile_of(env.W1, t), gate_sum[:])
                if O:
                    dve.wait_ge(s.x_ready, u + 1)
                    if counted(u):
                        dve.wait_ge(s.n2_aggr, u)
                    alone(dve)
                    nc.vector.bn_stats(stat2[:], tile_of(X, u)).then_inc(s.n2_stat, 1)
                    dve.wait_ge(s.n2_stat, u + 1)
                    if counted(u):
                        dve.wait_ge(s.n2_done, u)
                    alone(dve)
                    nc.vector.bn_aggr(aggr2[:], stat2[:]).then_inc(s.n2_aggr, 1)
                if Bs:
                    dve.wait_ge(s.pv_copied, 2 * (i - 3))
                    nc.vector.reciprocal(inv[:], pv_s[:, :, :, KC]).then_inc(s.sums_inv, 1)
                    nc.vector.tensor_tensor(sums[:], pv_s[:, :, :, 0:KC], pv_s[:, :, :, KC + 1:2 * KC + 1], ALU.add).then_inc(s.sums_inv, 1)
                if A2:
                    dve.wait_ge(s.m_mm, i - 2)
                    dve.wait_ge(s.qa_ready, i - 2)
                    if counted(4 * (i - 4)):
                        dve.wait_ge(s.st_mm, 4 * (i - 4))
                    nc.vector.tensor_tensor(Qb[:, q, :, :].rearrange("p n t -> p (n t)"), kv_bank[:],
                                            Qa[:, q, :, :].rearrange("p n t -> p (n t)"), ALU.add).then_inc(s.qb_ready, 1)
                if R:
                    dve.wait_ge(s.rank_mm, t + 1)
                    nc.vector.tensor_tensor(base[:], route_bank[:, 0:E], env.region[:], ALU.add).then_inc(s.rank_read, 1)
                    nc.vector.tensor_tensor(env.prev[:], env.prev[:], sel16[:], ALU.add).then_inc(s.prev_ready, 1)
                if R:
                    dve.wait_ge(s.rank_read, t + 1)
                    nc.vector.tensor_tensor(pm[:], sel16[:], base[:], ALU.mult).then_inc(s.pos_mul, 1)
                if O:
                    dve.wait_ge(s.n2_rstd, u + 1)
                    if counted(loads(u - 2, q)) and between(i, 7, TILES + 5):
                        dve.wait_ge(s.scattered[q], loads(u - 2, q))
                    if counted(u - 1):
                        dve.wait_ge(s.xt_mm, u - 1)
                    nc.vector.tensor_scalar(xr[:, q, :], tile_of(X, u), aggr2[:, 0:1], rstd2[:, 0:1],
                                            ALU.subtract, ALU.mult).then_inc(s.n2_done, 1)
                if Bs:
                    dve.wait_ge(s.sums_inv, 2 * (i - 3))
                    if counted(i - 4):
                        dve.wait_ge(s.ht_mm, i - 4)
                    nc.vector.tensor_tensor(heads[:].rearrange("p b m c -> p m b c"), sums[:],
                                            inv[:].unsqueeze(3).to_broadcast([P, H1 // 2, 2, KC]), ALU.mult).then_inc(s.heads_ready, 1)
                if R:
                    dve.wait_ge(s.pos_mul, t + 1)
                    nc.vector.tensor_reduce(tile_of(env.POS, t)[:, 0:1], pm[:], AX_X, ALU.add).then_inc(s.pos_ready, 1)
                    dve.wait_ge(s.pos_ready, t + 1)
                    if counted(loads(t - 2, p)) and between(i, 8, TILES + 6):
                        dve.wait_ge(s.scattered[p], loads(t - 2, p))
                    nc.vector.tensor_scalar(idx[:, p, :], tile_of(env.POS, t)[:, 0:1], 1.0, None, ALU.mult).then_inc(s.idx_ready, 1)

            nc.vector.memset(V[:], 0.0).then_inc(s.ones_set, 1)
            dve.wait_ge(s.ones_set, 1)
            for b, keys in enumerate((slice(0, CH), slice(CH, P))):
                nc.vector.memset(V[keys, :, :, b, KC:KC + 1], 1.0).then_inc(s.ones_set, 1)
            nc.vector.memset(M[:], 0.0).then_inc(s.ones_set, 1)
            nc.vector.memset(env.prev[:], 0.0).then_inc(s.ones_set, 1)
            dve.wait_ge(s.w_in, env.n_w_in)
            nc.vector.tensor_scalar(w_q[:], w_q[:], KC ** -0.5, None, ALU.mult).then_inc(s.scale_done, 1)
            nc.vector.tensor_scalar(b_qk[:, 0:1], b_qk[:, 0:1], KC ** -0.5, None, ALU.mult).then_inc(s.scale_done, 1)
            dve.wait_ge(s.scale_done, 2)
            dve.wait_ge(s.ones_set, 5)
            steady_loop(dve, step, 8, TILES, TILES + 7)

        @block.gpsimd
        def _(pool):
            def step(i, p):
                G, C, A1, A2, Bs, O, R, S = stages(i)
                q = 1 - p
                if S:
                    pool.wait_ge(s.idx_ready, i - 6)
                    alone(pool)
                    nc.gpsimd.indirect_dma_start(env.sorted_x, bass.IndirectOffsetOnAxis(idx[:, q, 0:1], 0),
                                                 xr[:, q, :], None).then_inc(s.scattered[q], 16)
                if G:
                    pool.wait_ge(s.at_ready, i + 1)
                    if counted(i - 1):
                        pool.wait_ge(s.added_2, i - 1)
                    alone(pool)
                    for k in range(2):
                        nc.gpsimd.indirect_dma_start(y[:, p, k, :], None, env.sorted_y0,
                                                     bass.IndirectOffsetOnAxis(y_at[:, p, k:k + 1], 0)).then_inc(s.gathered[p], 16)
                if Bs:
                    pool.wait_ge(s.exp_done, 2 * (i - 3))
                    nc.gpsimd.tensor_tensor(PT_lo[:, 1, :, :], PT[:, 1, :, :], PT_hi[:, 1, :, :], ALU.subtract) \
                        .then_inc(s.low_pool, 1)
                if C:
                    pool.wait_ge(s.norm_aggr, i)
                    nc.gpsimd.tensor_tensor(var_eps[:], aggr[:, 1:2], env.eps[:], ALU.add).then_inc(s.norm_eps, 1)
                    pool.wait_ge(s.norm_eps, i)
                    nc.gpsimd.tensor_tensor(rstd[:], var_eps[:], env.minus_half[:], ALU.pow).then_inc(s.norm_rstd, 1)
                if Bs:
                    if counted(i - 5):
                        pool.wait_ge(s.x_ready, i - 5)
                    nc.gpsimd.tensor_tensor(x_b[:, p, :], tile_of(X, i - 4), b_o[:], ALU.add).then_inc(s.x_bias, 1)
                if O:
                    pool.wait_ge(s.n2_aggr, i - 4)
                    nc.gpsimd.tensor_tensor(var_eps2[:], aggr2[:, 1:2], env.eps[:], ALU.add).then_inc(s.n2_eps, 1)
                    pool.wait_ge(s.n2_eps, i - 4)
                    nc.gpsimd.tensor_tensor(rstd2[:], var_eps2[:], env.minus_half[:], ALU.pow).then_inc(s.n2_rstd, 1)

            pool.wait_ge(s.w_in, env.n_w_in)
            pool.wait_ge(s.ones_set, 5)
            steady_loop(pool, step, 8, TILES, TILES + 7)
            for p in range(2):
                pool.wait_ge(s.scattered[p], 8 * TILES)


def finish(nc, env, stack):
    s = Names()
    (s.ready, s.added) = \
        (semaphore(nc, env, "f_" + n) for n in "ready added".split())
    s.gathered = [semaphore(nc, env, f"f_gathered{p}") for p in range(4)]
    s.stored = [semaphore(nc, env, f"f_stored{p}") for p in range(4)]
    y_at = stack.enter_context(nc.sbuf_tensor("f_y_at", [P, 4, 1], I32))
    y_w = stack.enter_context(nc.sbuf_tensor("f_y_w", [P, 4, 1], F32))
    y = stack.enter_context(nc.sbuf_tensor("f_y", [P, 4, P], F32))
    o = stack.enter_context(nc.sbuf_tensor("f_o", [P, 4, P], F32))
    out = env.io["out"].rearrange("(i p) d -> p i d", p=P)

    def steps(engine, step, lag):
        for i in range(8):
            step(i, i % 4)
        with engine.Fori(2, TILES // 4) as turn:
            for p in range(4):
                step(4 * turn + p, p)
        for i in range(TILES, TILES + lag):
            step(i, i % 4)

    with nc.Block() as block:
        @block.vector
        def _(dve):
            def step(i, p):
                if between(i, 0, TILES):
                    if counted(4 * (i - 4 - p) + 16):
                        dve.wait_ge(s.gathered[p], 4 * (i - 4 - p) + 16)
                    if not isinstance(i, int) or i >= 4:
                        dve.wait_ge(s.added, i - 3)
                    nc.vector.tensor_scalar(y_at[:, p, :], tile_of(env.Y_AT, i)[:, 0:1], 1.0, None, ALU.mult).then_inc(s.ready, 1)
                    nc.vector.tensor_scalar(y_w[:, p, :], tile_of(env.W1, i), 1.0, None, ALU.mult).then_inc(s.ready, 1)
                if between(i, 2, TILES + 2):
                    r = (p + 2) % 4
                    j = i - 2
                    dve.wait_ge(s.ready, 2 * (i - 1))
                    dve.wait_ge(s.gathered[r], 4 * (j - r) + 16)
                    if counted(4 * (j - 4 - r) + 16):
                        dve.wait_ge(s.stored[r], 4 * (j - 4 - r) + 16)
                    nc.vector.scalar_tensor_tensor(o[:, r, :], y[:, r, :], y_w[:, r, 0:1], tile_of(env.X, j), ALU.mult, ALU.add) \
                        .then_inc(s.added, 1)

            steps(dve, step, 2)

        @block.gpsimd
        def _(pool):
            def step(i, p):
                pool.wait_ge(s.ready, 2 * i + 2)
                if not isinstance(i, int) or i >= 4:
                    pool.wait_ge(s.added, i - 3)
                alone(pool)
                nc.gpsimd.indirect_dma_start(y[:, p, :], None, env.sorted_y1,
                                             bass.IndirectOffsetOnAxis(y_at[:, p, 0:1], 0)).then_inc(s.gathered[p], 16)

            steps(pool, step, 0)

        @block.sync
        def _(sp):
            def step(i, p):
                sp.wait_ge(s.added, i + 1)
                sp.dma_start(tile_of(out, i), o[:, p, :]).then_inc(s.stored[p], 16)

            steps(sp, step, 0)
            for p in range(4):
                sp.wait_ge(s.stored[p], 4 * TILES)


def build(nc, io, stop=None):
    env = Names()
    env.io = io
    env.X = nc.alloc_sbuf_tensor("X", [P, TILES, P], F32)
    env.bank = [nc.alloc_psum_tensor(f"bank{n}", [P, 512], F32) for n in range(8)]
    env.ident = nc.alloc_sbuf_tensor("ident", [P, P], F32)
    env.ident16 = nc.alloc_sbuf_tensor("ident16", [P, P], F16)
    env.tri16 = nc.alloc_sbuf_tensor("tri16", [P, P], F16)
    env.ones16 = nc.alloc_sbuf_tensor("ones16", [P, P], F16)
    env.region = nc.alloc_sbuf_tensor("region", [P, E], F32)
    env.iota2 = nc.alloc_sbuf_tensor("iota2", [P, 2, E], F32)
    env.prev = nc.alloc_sbuf_tensor("prev", [P, E], F16)
    env.eps = nc.alloc_sbuf_tensor("eps", [P, 1], F32)
    env.minus_half = nc.alloc_sbuf_tensor("minus_half", [P, 1], F32)
    env.TOP = nc.alloc_sbuf_tensor("TOP", [P, TILES, 2], F32)
    env.SEL = nc.alloc_sbuf_tensor("SEL", [P, TILES, 2 * E], F32)
    env.POS = nc.alloc_sbuf_tensor("POS", [P, TILES, 2], F32)
    env.sorted_x = nc.dram_tensor("sorted_x", (SPARE + BLOCK, P), F32, kind="Internal").ap()
    env.w_hi = nc.alloc_sbuf_tensor("w_hi", [P, W_COLUMNS, F], F16)
    env.w_lo = nc.alloc_sbuf_tensor("w_lo", [P, W_COLUMNS, F], F16)
    env.zeros = nc.alloc_sbuf_tensor("zeros", [P, R, P], F32)
    env.sorted_y0 = nc.dram_tensor("sorted_y0", (BLOCKS0 * BLOCK, P), F32, kind="Internal").ap()
    env.sorted_y1 = nc.dram_tensor("sorted_y1", (BLOCKS1 * BLOCK, P), F32, kind="Internal").ap()
    env.sel = nc.alloc_sbuf_tensor("sel", [P, 16, P], F16)
    env.k_bias_sb = nc.alloc_sbuf_tensor("k_bias", [P, 1], F32)
    env.block_row = nc.alloc_sbuf_tensor("block_row", [P, BLOCKS0], I32)
    env.block_expert = nc.alloc_sbuf_tensor("block_expert", [P, BLOCKS0], I32)
    env.Y_AT = nc.alloc_sbuf_tensor("Y_AT", [P, TILES, 2], F32)
    env.W = nc.alloc_sbuf_tensor("W", [P, TILES, 2], F32)
    env.W1 = nc.alloc_sbuf_tensor("W1", [P, TILES, 1], F32)
    phases = [lambda st: attention0(nc, env, st),
              lambda st: plan(nc, env, st, "p0", 2, BLOCKS0, env.io["c_blocks0"]),
              lambda st: experts(nc, env, st, "e0", BLOCKS0, True, (G0, U0), D0, env.sorted_y0),
              lambda st: attention1(nc, env, st),
              lambda st: plan(nc, env, st, "p1", 1, BLOCKS1, env.io["c_blocks1"]),
              lambda st: experts(nc, env, st, "e1", BLOCKS1, False, (G1,), D1, env.sorted_y1),
              lambda st: finish(nc, env, st)]
    for phase in phases[:stop]:
        env.phase_semaphores = []
        with ExitStack() as stack:
            phase(stack)
        nc.all_engine_barrier()
        nc.clear_and_free_semaphores(env.phase_semaphores)
        nc.all_engine_barrier()
    return env


def block_diagonal(w):
    out = np.zeros((P, P), np.float32)
    out[:CH, :CH] = w
    out[CH:, CH:] = w
    return out


def head_rows(kind, batch, group, heads_per_group=4):
    hi, lo = np.zeros((P, P), np.float16), np.zeros((P, P), np.float16)
    for j in range(4):
        for r in range(ROW_MAX):
            third = r // KC
            is_lo = third == (2 if kind == "q" else 1)
            (lo if is_lo else hi)[64 * batch + (4 * group + j) * KC + r % KC, 32 * j + r] = 1
    return hi, lo


def constants():
    c = {}
    half = KC // 2
    theta = (1.0 / np.float32(1250) ** (np.arange(0, half, 2, dtype=np.float32) / np.float32(half))).astype(np.float32)
    ang = np.arange(D, dtype=np.float32)[None, :] * np.concatenate([theta, theta])[:, None]
    cos, sin = np.ones((KC, D), np.float32), np.zeros((KC, D), np.float32)
    cos[:half] = np.cos(ang)
    sin[:half] = np.sin(ang) * np.array([-1, -1, 1, 1], np.float32)[:, None]
    cos, sin = np.tile(cos, (P // KC, 1)), np.tile(sin, (P // KC, 1))
    scale = np.float32(KC ** -0.5)
    c["a0_rot"] = np.stack([np.stack([cos * scale, sin * scale], 1), np.stack([cos, sin], 1)], 1)
    c["c_sel"] = np.stack([m for kind in "qk" for b in range(2) for g in range(GROUPS0) for m in head_rows(kind, b, g)], 1)
    kb = np.zeros((P, 1), np.float32)
    kb[ROW_MAX::32] = -1
    c["c_k_bias"] = kb
    c["c_ident"] = np.eye(P, dtype=np.float32)
    c["c_ident16"] = np.eye(P, dtype=np.float16)
    c["c_tri16"] = np.triu(np.ones((P, P), np.float16), 1)
    c["c_region"] = np.tile(np.arange(E, dtype=np.float32) * REGION, (P, 1))
    for name, blocks in (("c_blocks0", BLOCKS0), ("c_blocks1", BLOCKS1)):
        c[name] = np.tile(np.arange(blocks, dtype=np.float32)[:, None], (P, 1, E))
    c["c_steps"] = np.tile(np.arange(MOST, dtype=np.float32) * BLOCK, (P, E, 1))
    c["c_before"] = np.tile(np.tril(np.ones((E, E), np.float32), -1), (P, 1, 1))
    c["c_iota2"] = np.tile(np.arange(E, dtype=np.float32), (P, 2, 1))
    return c


def layout(a):
    v = {"x": a["x"].reshape(-1, D), "ctx": a["ctx_1024"].reshape(-1, D)}
    partner = np.array([8 * h + c for h in range(H0) for c in (2, 3, 0, 1, 4, 5, 6, 7)])
    wq, wk = a["L0_xattn_Wq"], a["L0_xattn_Wk"]
    bq, bk = a["L0_xattn_bq"], a["L0_xattn_bk"]
    v["a0_w_qk"] = np.stack([block_diagonal(w.T) for w in (wq, wq[partner], wk, wk[partner])], 1)
    v["a0_b_qk"] = np.stack([np.tile(b, 2) for b in (bq, bq[partner], bk, bk[partner])], 1)
    v["a0_w_v"] = block_diagonal(a["L0_xattn_Wv"].T)
    v["a0_w_o"] = block_diagonal(a["L0_xattn_Wo"].T)
    v["a0_b_v"] = np.tile(a["L0_xattn_bv"], (P, 2))
    v["a0_b_o"] = np.tile(a["L0_xattn_bo"], 2)[:, None]
    v["f0_w_c"] = a["L0_ffn_conf_w"].T
    v["f0_b_c"] = np.tile(a["L0_ffn_conf_b"], (P, 1))
    v["f0_wealth"] = np.tile(a["L0_ffn_wealth"], (P, 1))
    by_feature = lambda w: w.reshape(E, F, D).transpose(2, 0, 1)
    by_hidden = lambda w: w.reshape(E, D, FC, P).transpose(3, 0, 2, 1).reshape(P, E, F)
    v["w_experts"] = np.concatenate([by_feature(a["L0_ffn_gate_w"]), by_feature(a["L0_ffn_up_w"]), by_hidden(a["L0_ffn_down_w"]),
                                     a["L1_ffn_w1"].transpose(1, 0, 2), by_hidden(a["L1_ffn_w2"].transpose(0, 2, 1))], 1)
    v["a1_w_q"], v["a1_w_k"] = a["L1_xattn_Wq_w"].T, a["L1_xattn_Wk_w"].T
    paired = np.array([8 * h + c for pair in PAIRS for h in pair for c in range(KC)])
    halves = np.array([8 * pair[half] + c for half in range(2) for pair in PAIRS for c in range(KC)])
    v["a1_w_v"] = a["L1_xattn_Wv_w"].T[:, paired]
    v["a1_w_o"] = a["L1_xattn_Wo_w"].T[halves].reshape(2, CH, P).transpose(1, 0, 2)
    v["a1_b_qk"] = np.stack([a["L1_xattn_Wq_b"], a["L1_xattn_Wk_b"]], 1)
    v["a1_b_v"] = np.tile(a["L1_xattn_Wv_b"][paired], (P, 1))
    v["a1_b_o"] = np.tile(a["L1_xattn_Wo_b"], (P, 1))
    v["f1_w_g"] = a["L1_ffn_gate_w"]
    v["f1_b_g"] = np.tile(a["L1_ffn_gate_b"], (P, 1))
    v["f1_b_hidden"] = a["L1_ffn_b1"].reshape(E * 2, FC // 2, P).transpose(2, 0, 1)
    v["f1_b_out"] = np.tile(a["L1_ffn_b2"], (P, 1, 1))
    v.update(constants())
    return {k: np.ascontiguousarray(x) for k, x in v.items()}


def kernel(**inputs):
    import concourse.bacc as bacc
    from concourse.bass_utils import run_bass_kernel_spmd

    nc = bacc.Bacc("TRN2", target_bir_lowering=False, num_devices=1)
    arrays = layout({name: np.asarray(a) for name, a in inputs.items()})
    io = {name: nc.dram_tensor(name, a.shape, mybir.dt.from_np(a.dtype), kind="ExternalInput").ap() for name, a in arrays.items()}
    io["out"] = nc.dram_tensor("out", (B * CH, D), F32, kind="ExternalOutput").ap()
    build(nc, io)
    result = run_bass_kernel_spmd(nc, [arrays], core_ids=[0])
    return result.results[0]["out"].reshape(B, CH, D)
```
